# Optimizing a Trainium2 kernel written in Bass

```python
import numpy as np
import jax
import jax.numpy as jnp

def _softmax(x, axis=-1):
    return jax.nn.softmax(x, axis=axis)

def _gelu(x):
    return jax.nn.gelu(x, approximate=True)

def _silu(x):
    return jax.nn.silu(x)

def _sigmoid(x):
    return jax.nn.sigmoid(x)

def _layernorm(x, axis=-1, eps=1e-05):
    m = jnp.mean(x, axis=axis, keepdims=True)
    v = jnp.var(x, axis=axis, keepdims=True)
    return (x - m) / jnp.sqrt(v + eps)

def _scatter_add(tgt, idx, src, axis=0):
    return tgt.at[idx].add(src)

def _segment_sum(src, seg, n):
    return jax.ops.segment_sum(src, seg, n)
kernel_name = 'mk_decoder_postln_d1_seqx_r4_963f48'

def setup_inputs(seed: int=0):
    np.random.seed(seed)
    _w = jnp.asarray

    def _rec_inputs():
        import jax
        import jax.numpy as jnp
        _rk = jax.random.key(seed)
        x = -0.0002928 + 1 * jax.random.normal(jax.random.fold_in(_rk, 1), (4, 1024, 256), jnp.float32)
        _lenS = 1024 - jax.random.randint(jax.random.fold_in(_rk, 7), (4,), 0, max(1, 1024 // 4) + 1, jnp.int32)
        _lenS2 = 64 - jax.random.randint(jax.random.fold_in(_rk, 8), (4,), 0, max(1, 64 // 4) + 1, jnp.int32)
        _ctx_1024P = jax.random.normal(jax.random.fold_in(_rk, 11), (4, 16, 256), jnp.float32)
        _ctx_1024c = jax.random.dirichlet(jax.random.fold_in(_rk, 511), 0.3 * jnp.ones((16,), jnp.float32), (4, 64))
        _ctx_1024t = jnp.einsum('bsk,bkd->bsd', _ctx_1024c, _ctx_1024P)
        _ctx_1024t = _ctx_1024t * jax.lax.rsqrt(jnp.mean(jnp.square(_ctx_1024t)) + 1e-12) * 0.953939
        ctx_1024 = -1.39393e-06 + 0.999914 * (_ctx_1024t + 0.3 * jax.random.normal(jax.random.fold_in(_rk, 611), (4, 64, 256), jnp.float32))
        return (x, ctx_1024)
    x, ctx_1024 = _rec_inputs()

    def _L0_attn_setup():
        import jax, jax.numpy as jnp
        import numpy as np
        DIM = 256
        NUM_HEADS = 16
        HEAD_DIM = DIM // NUM_HEADS
        EPS = 1e-06

        def _apply_rope(q, k):
            B, N, H, D = q.shape
            half = D // 2
            freqs = 1.0 / 2500 ** (jnp.arange(0, half, dtype=jnp.float32) / half)
            t = jnp.arange(N, dtype=jnp.float32)
            freqs = jnp.outer(t, freqs)
            emb = jnp.concatenate([freqs, freqs], axis=-1)
            cos = jnp.cos(emb)[None, :, None, :]
            sin = jnp.sin(emb)[None, :, None, :]

            def rot(x):
                x1, x2 = (x[..., :half], x[..., half:])
                return jnp.concatenate([-x2, x1], axis=-1)
            return (q * cos + rot(q) * sin, k * cos + rot(k) * sin)

        def _rmsnorm(x, scale):
            var = jnp.mean(jnp.square(x.astype(jnp.float32)), axis=-1, keepdims=True)
            return (x * jax.lax.rsqrt(var + EPS) * scale).astype(x.dtype)
        key = jax.random.key(seed)
        ks = jax.random.split(key, 6)
        B, N = (4, 512)
        x = jax.random.normal(ks[0], (B, N, DIM), dtype=jnp.float32)
        lim_qkv = float(np.sqrt(6.0 / (DIM + 3 * DIM)))
        w_qkv = jax.random.uniform(ks[1], (DIM, 3 * DIM), jnp.float32, -lim_qkv, lim_qkv)
        q_scale = jnp.ones((HEAD_DIM,), jnp.float32)
        k_scale = jnp.ones((HEAD_DIM,), jnp.float32)
        lim_p = float(np.sqrt(6.0 / (DIM + DIM)))
        w_proj = jax.random.uniform(ks[2], (DIM, DIM), jnp.float32, -lim_p, lim_p)
        b_proj = jnp.zeros((DIM,), jnp.float32)
        return {'x': x, 'w_qkv': w_qkv, 'q_scale': q_scale, 'k_scale': k_scale, 'w_proj': w_proj, 'b_proj': b_proj}
    _L0_attn_all = _L0_attn_setup()
    _L0_attn_in = {k: v for k, v in _L0_attn_all.items() if k in ('w_qkv', 'q_scale', 'k_scale', 'w_proj', 'b_proj')}
    del _L0_attn_all

    def _L0_xattn_setup():
        import jax, jax.numpy as jnp
        import numpy as np
        DIM = 256
        NUM_HEADS = 16
        HEAD_DIM = DIM // NUM_HEADS
        key = jax.random.key(seed)
        ks = jax.random.split(key, 11)
        B, N, C = (2, 512, DIM)
        s = 1.0 / np.sqrt(C)
        inp = {'q': jax.random.normal(ks[0], (B, N, C), jnp.float32), 'k': jax.random.normal(ks[1], (B, N, C), jnp.float32), 'v': jax.random.normal(ks[2], (B, N, C), jnp.float32), 'Wq': jax.random.normal(ks[3], (C, C), jnp.float32) * s, 'bq': jnp.zeros((C,), jnp.float32), 'Wk': jax.random.normal(ks[4], (C, C), jnp.float32) * s, 'bk': jnp.zeros((C,), jnp.float32), 'Wv': jax.random.normal(ks[5], (C, C), jnp.float32) * s, 'bv': jnp.zeros((C,), jnp.float32), 'Wo': jax.random.normal(ks[6], (C, C), jnp.float32) * s, 'bo': jnp.zeros((C,), jnp.float32)}
        return inp
    _L0_xattn_all = _L0_xattn_setup()
    _L0_xattn_in = {k: v for k, v in _L0_xattn_all.items() if k in ('Wq', 'bq', 'Wk', 'bk', 'Wv', 'bv', 'Wo', 'bo')}
    del _L0_xattn_all

    def _L0_ffn_setup():
        import jax, jax.numpy as jnp
        import numpy as np
        DM, NEXPERTS, SETS, ESIZE = (256, 32, 4, 32)
        B, S = (2, 2048)
        key = jax.random.key(seed)
        ks = jax.random.split(key, 7)
        sc = 0.02
        return {'x': jax.random.normal(ks[0], (B, S, DM), jnp.float32), 'Wc': jax.random.normal(ks[1], (DM, NEXPERTS, SETS), jnp.float32) * sc, 'bc': jax.random.normal(ks[2], (NEXPERTS, SETS), jnp.float32) * sc, 'W1': jax.random.normal(ks[3], (NEXPERTS, SETS, DM, ESIZE), jnp.float32) * sc, 'b1': jax.random.normal(ks[4], (NEXPERTS, SETS, ESIZE), jnp.float32) * sc, 'W2': jax.random.normal(ks[5], (NEXPERTS, SETS, DM, ESIZE), jnp.float32) * sc, 'b2': jax.random.normal(ks[6], (NEXPERTS, SETS, DM), jnp.float32) * sc}
    _L0_ffn_all = _L0_ffn_setup()
    _L0_ffn_in = {k: v for k, v in _L0_ffn_all.items() if k in ('Wc', 'bc', 'W1', 'b1', 'W2', 'b2')}
    del _L0_ffn_all
    return {'x': x, 'ctx_1024': ctx_1024, 'L0_attn_w_qkv': _L0_attn_in['w_qkv'], 'L0_attn_q_scale': _L0_attn_in['q_scale'], 'L0_attn_k_scale': _L0_attn_in['k_scale'], 'L0_attn_w_proj': _L0_attn_in['w_proj'], 'L0_attn_b_proj': _L0_attn_in['b_proj'], 'L0_xattn_Wq': _L0_xattn_in['Wq'], 'L0_xattn_bq': _L0_xattn_in['bq'], 'L0_xattn_Wk': _L0_xattn_in['Wk'], 'L0_xattn_bk': _L0_xattn_in['bk'], 'L0_xattn_Wv': _L0_xattn_in['Wv'], 'L0_xattn_bv': _L0_xattn_in['bv'], 'L0_xattn_Wo': _L0_xattn_in['Wo'], 'L0_xattn_bo': _L0_xattn_in['bo'], 'L0_ffn_Wc': _L0_ffn_in['Wc'], 'L0_ffn_bc': _L0_ffn_in['bc'], 'L0_ffn_W1': _L0_ffn_in['W1'], 'L0_ffn_b1': _L0_ffn_in['b1'], 'L0_ffn_W2': _L0_ffn_in['W2'], 'L0_ffn_b2': _L0_ffn_in['b2']}

def reference(x, ctx_1024, L0_attn_w_qkv, L0_attn_q_scale, L0_attn_k_scale, L0_attn_w_proj, L0_attn_b_proj, L0_xattn_Wq, L0_xattn_bq, L0_xattn_Wk, L0_xattn_bk, L0_xattn_Wv, L0_xattn_bv, L0_xattn_Wo, L0_xattn_bo, L0_ffn_Wc, L0_ffn_bc, L0_ffn_W1, L0_ffn_b1, L0_ffn_W2, L0_ffn_b2):
    import jax
    import jax.numpy as jnp

    def _L0_attn_ref(x, w_qkv, q_scale, k_scale, w_proj, b_proj):
        import jax, jax.numpy as jnp
        import numpy as np
        DIM = 256
        NUM_HEADS = 16
        HEAD_DIM = DIM // NUM_HEADS
        EPS = 1e-06

        def _apply_rope(q, k):
            B, N, H, D = q.shape
            half = D // 2
            freqs = 1.0 / 2500 ** (jnp.arange(0, half, dtype=jnp.float32) / half)
            t = jnp.arange(N, dtype=jnp.float32)
            freqs = jnp.outer(t, freqs)
            emb = jnp.concatenate([freqs, freqs], axis=-1)
            cos = jnp.cos(emb)[None, :, None, :]
            sin = jnp.sin(emb)[None, :, None, :]

            def rot(x):
                x1, x2 = (x[..., :half], x[..., half:])
                return jnp.concatenate([-x2, x1], axis=-1)
            return (q * cos + rot(q) * sin, k * cos + rot(k) * sin)

        def _rmsnorm(x, scale):
            var = jnp.mean(jnp.square(x.astype(jnp.float32)), axis=-1, keepdims=True)
            return (x * jax.lax.rsqrt(var + EPS) * scale).astype(x.dtype)
        B, N, C = x.shape
        qkv = jnp.einsum('bnc,cd->bnd', x, w_qkv).reshape(B, N, 3, NUM_HEADS, HEAD_DIM)
        q, k, v = (qkv[:, :, 0], qkv[:, :, 1], qkv[:, :, 2])
        q = _rmsnorm(q, q_scale)
        k = _rmsnorm(k, k_scale)
        q, k = _apply_rope(q, k)
        q = q.astype(jnp.float32) * HEAD_DIM ** (-0.5)
        k = k.astype(jnp.float32)
        v = v.astype(jnp.float32)
        logits = jnp.einsum('bqhd,bkhd->bhqk', q, k)
        attn = jax.nn.softmax(logits, axis=-1)
        out = jnp.einsum('bhqk,bkhd->bqhd', attn, v).reshape(B, N, C)
        return jnp.einsum('bnc,cd->bnd', out, w_proj) + b_proj

    def _L0_xattn_ref(q, k, v, Wq, bq, Wk, bk, Wv, bv, Wo, bo):
        import jax, jax.numpy as jnp
        import numpy as np
        DIM = 256
        NUM_HEADS = 16
        HEAD_DIM = DIM // NUM_HEADS
        B, Nq, C = q.shape
        Nkv = k.shape[1]
        H, D = (NUM_HEADS, HEAD_DIM)
        qh = (q @ Wq.T + bq).reshape(B, Nq, H, D).transpose(0, 2, 1, 3)
        kh = (k @ Wk.T + bk).reshape(B, Nkv, H, D).transpose(0, 2, 1, 3)
        vh = (v @ Wv.T + bv).reshape(B, Nkv, H, D).transpose(0, 2, 1, 3)
        scale = D ** (-0.5)
        attn = jax.nn.softmax(jnp.einsum('bhqd,bhkd->bhqk', qh, kh) * scale, axis=-1)
        out = jnp.einsum('bhqk,bhkd->bhqd', attn, vh)
        out = out.transpose(0, 2, 1, 3).reshape(B, Nq, C)
        return out @ Wo.T + bo

    def _L0_ffn_ref(x, Wc, bc, W1, b1, W2, b2):
        import jax, jax.numpy as jnp
        import numpy as np
        DM, NEXPERTS, SETS, ESIZE = (256, 32, 4, 32)
        B, S = (2, 2048)
        b, s, d = x.shape
        g = Wc.shape[1]
        grouped = x.reshape(b, s // g, g, d)
        logits = jnp.einsum('bntd,des->bntes', grouped, Wc) + bc
        tie = jnp.linspace(0.0, 1e-06, g, dtype=x.dtype).reshape(-1, 1, 1)
        logits = logits + tie
        perm = (logits == jnp.max(logits, axis=-3, keepdims=True)).astype(x.dtype)
        permuted = jnp.einsum('bntd,bntes->bnesd', grouped, perm)
        inner = jax.nn.relu(jnp.einsum('bnesd,esdf->bnesf', permuted, W1) + b1)
        result_permuted = jnp.einsum('bnesf,esdf->bnesd', inner, W2) + b2
        result = jnp.einsum('bnesd,bntes->bntd', result_permuted, perm)
        return result.reshape(b, s, d)
    x = _layernorm(x + _L0_attn_ref(x, L0_attn_w_qkv, L0_attn_q_scale, L0_attn_k_scale, L0_attn_w_proj, L0_attn_b_proj), axis=-1)
    x = _layernorm(x + _L0_xattn_ref(x, ctx_1024, ctx_1024, L0_xattn_Wq, L0_xattn_bq, L0_xattn_Wk, L0_xattn_bk, L0_xattn_Wv, L0_xattn_bv, L0_xattn_Wo, L0_xattn_bo), axis=-1)
    x = _layernorm(x + _L0_ffn_ref(x, L0_ffn_Wc, L0_ffn_bc, L0_ffn_W1, L0_ffn_b1, L0_ffn_W2, L0_ffn_b2), axis=-1)
    return x

_drawn_inputs = setup_inputs


def setup_inputs(seed=0):
    import zlib

    import numpy as np

    out = dict(_drawn_inputs(seed))
    spreads = {'L0_attn_q_scale': (1.0, 0.6),
     'L0_attn_k_scale': (1.0, 0.6),
     'L0_attn_b_proj': (0.0, 0.1),
     'L0_xattn_bq': (0.0, 0.278),
     'L0_xattn_bk': (0.0, 0.8),
     'L0_xattn_bv': (0.0, 0.1),
     'L0_xattn_bo': (0.0, 0.1)}
    factors = {'L0_ffn_b1': 8.0}
    for name, (base, spread) in spreads.items():
        noise = np.random.default_rng([zlib.crc32(name.encode()), seed]).standard_normal(out[name].shape)
        drawn = base * np.exp(spread * noise) if base else spread * noise
        out[name] = jnp.asarray(drawn.astype(out[name].dtype))
    for name, factor in factors.items():
        out[name] = (out[name] * factor).astype(out[name].dtype)
    return out
```

```python
from contextlib import ExitStack

import concourse.bass as bass
from concourse import mybir

F32 = mybir.dt.float32
BF16 = mybir.dt.bfloat16
I32 = mybir.dt.int32
ACT = mybir.ActivationFunctionType
ALU = mybir.AluOpType
AX = mybir.AxisListType

P = 128
B, N, C = 4, 1024, 256
H, D = 16, 16
KT = N // P
HG = 4
GPB = H // HG
GROUPS = B * GPB
VW = 32
SPLIT = 3
Q_PART = [0, 0, 0, 1, 1, 2]
K_PART = [0, 1, 2, 0, 1, 0]
STACK = D * len(Q_PART)
SHIFT = 2
AHEAD = 6
PAIRS = B * KT // 2
LOOP_PAIRS = PAIRS - AHEAD
RMS_EPS = 1e-6
LN_EPS = 1e-5
SAFE_LOGIT = 60.0
MAGIC = float(0x5F3759DF)


def wait(eng, sem, value):
    if not (isinstance(value, int) and value <= 0):
        eng.wait_ge(sem, value)


def newton_rsqrt(nc, link, y, t, hv, v):
    bits = y.bitcast(I32)
    link(nc.vector.tensor_scalar(bits, v.bitcast(I32), 1, None, ALU.logical_shift_right))
    link(nc.vector.tensor_scalar(hv, v, -0.5, None, ALU.mult))
    link(nc.vector.tensor_scalar(bits, bits, -1.0, MAGIC, ALU.mult, ALU.add))
    for step in range(3):
        link(nc.vector.tensor_tensor(t, y, y, ALU.mult))
        link(nc.vector.tensor_tensor(t, t, hv, ALU.mult))
        link(nc.vector.scalar_tensor_tensor(out=y, in0=t, scalar=1.5, in1=y, op0=ALU.add, op1=ALU.mult))


def attention_phases(nc, io, qk_parts, v_scratch, attn_scratch, shift_scratch):
    with ExitStack() as ctx:
        def sb(name, shape, dt):
            return ctx.enter_context(nc.sbuf_tensor(name, shape, dt))

        def psum(name, shape):
            return ctx.enter_context(nc.psum_tensor(name, shape, F32))

        wqkv = sb("wqkv", [P, 2, 3 * C], F32)
        ident = sb("ident", [P, P], F32)
        zeros = sb("zeros", [P, 4 * P], F32)
        cos = sb("cos", [P, B * KT, D], F32)
        sin = sb("sin", [P, B * KT, D], F32)
        scales = sb("scales", [P, 2, D], F32)
        rope_c = sb("rope_c", [P, B * KT, 2, D], F32)
        rope_s = sb("rope_s", [P, B * KT, 2, D], F32)
        xT = sb("xT", [P, 2, 2 * P], F32)
        raw = sb("raw", [P, 2, 2 * C], F32)
        sq = sb("sq", [P, 2, 2 * C], F32)
        ra = sb("ra", [P, 2 * C], F32)
        rb = sb("rb", [P, 2 * C], F32)
        ms = sb("ms", [P, 2 * H], F32)
        rstd = sb("rstd", [P, 2 * H], F32)
        nt = sb("nt", [P, 2 * H], F32)
        nh = sb("nh", [P, 2 * H], F32)
        qn = sb("qn", [P, 2, 2 * C], F32)
        rest = sb("rest", [P, 2, 2 * C], F32)
        parts = sb("parts", [P, SPLIT, 4, 2, P], BF16)
        vbuf = sb("vbuf", [P, 2, H, VW], F32)
        qst = sb("qst", [P, 2, HG, N], BF16)
        kst = sb("kst", [P, 2, HG, N], BF16)
        vst = sb("vst", [P, 2, KT, HG, VW], F32)
        prob = sb("prob", [P, 2, HG, N], F32)
        oT = sb("oT", [P, N], F32)
        rden = sb("rden", [P, 2, 4 * HG], F32)
        attn = sb("attn", [P, KT, HG, D], F32)
        flag = sb("flag", [1, 1], I32)
        bound = sb("bound", [1, 4], F32)
        rmax = sb("rmax", [P, HG * KT], F32)
        shift = sb("shift", [HG * KT, SHIFT, P], BF16)

        S = [psum(f"S{n}", [P, N]) for n in range(2)]
        O = psum("O", [P, N])
        X = [psum(f"X{n}", [P, 512]) for n in range(2)]

        def rope_view(t):
            return t.rearrange("p (a h d) -> p a h d", a=2, d=D)

        def pe_qk(pe, u, bank):
            for c in range(2):
                mm = pe.matmul(bank[:, 0:2 * C], xT[:, c, u * P:(u + 1) * P], wqkv[:, c, 0:2 * C],
                               start=(c == 0), stop=(c == 1))
            return mm

        def pe_v(pe, u, bank):
            for c in range(2):
                mm = pe.matmul(bank[:, 0:C], xT[:, c, u * P:(u + 1) * P], wqkv[:, c, 2 * C:3 * C],
                               start=(c == 0), stop=(c == 1))
            return mm

        def pe_turn(pe, u, bank):
            for c in range(4):
                mm = pe.transpose(bank[:, c * P:(c + 1) * P], qn[:, u, c * P:(c + 1) * P], ident[:])
            return mm

        def dve_rope(dve, s, link, n, tile, u):
            def table(t, lo, hi):
                return t[:, bass.ds(tile, 1), :, lo:hi].rearrange("p o a d -> p (o a) d")[:, :, None, :] \
                    .to_broadcast([P, 2, H, hi - lo])
            dve.wait_ge(s["qn_ready"], n + 2)
            dve.wait_ge(s["raw_ready"], n + 3)
            nc.vector.tensor_tensor(rope_view(ra[:]), rope_view(raw[:, u, :]), table(rope_c, 0, D), ALU.mult)
            half = D // 2
            nc.vector.tensor_tensor(rope_view(rb[:])[:, :, :, 0:half], rope_view(raw[:, u, :])[:, :, :, half:D],
                                    table(rope_s, 0, half), ALU.mult)
            link(nc.vector.tensor_tensor(rope_view(rb[:])[:, :, :, half:D], rope_view(raw[:, u, :])[:, :, :, 0:half],
                                         table(rope_s, half, D), ALU.mult))
            link(nc.vector.tensor_tensor(ra[:], ra[:], rb[:], ALU.add))
            dve.wait_ge(s["sq_ready"], n + 1)
            link(nc.vector.tensor_reduce(ms[:], sq[:, u, :].rearrange("p (h d) -> p h d", d=D), AX.X, ALU.add))
            link(nc.vector.tensor_scalar(ms[:], ms[:], 1.0 / D, RMS_EPS, ALU.mult, ALU.add))
            newton_rsqrt(nc, link, rstd[:], nt[:], nh[:], ms[:])
            nc.vector.tensor_tensor(qn[:, u, :].rearrange("p (h d) -> p h d", d=D),
                                    ra[:].rearrange("p (h d) -> p h d", d=D),
                                    rstd[:, :, None].to_broadcast([P, 2 * H, D]), ALU.mult).then_inc(s["qn_ready"], 1)

        ROPE_LINKS = 4 + 3 + 9

        def dve_rest(dve, s, n, u, bank, hi_sem, hi_count):
            dve.wait_ge(hi_sem, hi_count)
            dve.wait_ge(s["parts_ready"], n + 1)
            nc.vector.tensor_tensor(rest[:, u, :].rearrange("p (c t) -> p c t", c=4),
                                    bank[:].rearrange("p (c t) -> p c t", c=4),
                                    parts[:, 0, :, u, :], ALU.subtract).then_inc(s["t_taken"], 1)

        def pool_square(pool, s, n, u):
            pool.wait_ge(s["raw_ready"], n + 3)
            pool.wait_ge(s["qn_ready"], n + 1)
            nc.gpsimd.tensor_tensor(sq[:, u, :], raw[:, u, :], raw[:, u, :], ALU.mult).then_inc(s["sq_ready"], 1)

        def pool_parts(pool, s, n, u):
            pool.wait_ge(s["t_taken"], n + 3)
            r = rest[:, u, :].rearrange("p (c t) -> p c t", c=4)
            nc.gpsimd.tensor_tensor(parts[:, 1, :, u, :], r, zeros[:].rearrange("p (c t) -> p c t", c=4),
                                    ALU.add).then_inc(s["mid_ready"], 1)
            pool.wait_ge(s["mid_ready"], n + 1)
            nc.gpsimd.tensor_tensor(parts[:, 2, :, u, :], r, parts[:, 1, :, u, :],
                                    ALU.subtract).then_inc(s["parts_ready"], 1)

        def sp_load_x(sp, s, pair):
            sp.dma_start(xT[:], io["xT"][:, :, bass.ds(pair * 2 * P, 2 * P)]).then_inc(s["x_loaded"], 16)

        def sp_store_v(sp, s, pair):
            sp.dma_start(v_scratch[bass.ds(pair, 1)].rearrange("o u p h w -> p (o u) (h w)"),
                         vbuf[:].rearrange("p u h w -> p u (h w)")).then_inc(s["v_written"], 16)

        def sp_store_parts(sp, s, b, quarter):
            for part in range(SPLIT):
                for a in range(2):
                    dst = qk_parts[part, a, bass.ds(b, 1), :, bass.ds(quarter * 2 * P, 2 * P)] \
                        .rearrange("o (c p) t -> p (o c) t", p=P)
                    src = parts[:, part, 2 * a:2 * a + 2].rearrange("p c u t -> p c (u t)")
                    sp.dma_start(dst, src).then_inc(s["parts_written"], 16)

        PARTS_WRITTEN = 16 * SPLIT * 2

        def projection_semaphores(stack, tag):
            names = ("x_loaded", "qk_ps", "v_ps", "t_ps", "raw_ready", "sq_ready", "v_ready", "hi_ready",
                     "qn_ready", "t_taken", "mid_ready", "parts_ready", "v_written", "parts_written")
            return {n: stack.enter_context(nc.semaphore(f"{tag}_{n}")) for n in names}

        def sp_credits(sp, s):
            sp.sem_inc(s["v_written"], 16)
            sp.sem_inc(s["parts_written"], PARTS_WRITTEN)

        with ExitStack() as stage:
            s = projection_semaphores(stage, "a")
            const_loaded = stage.enter_context(nc.semaphore("const_loaded"))
            table_step = stage.enter_context(nc.semaphore("table_step"))
            rope_step = stage.enter_context(nc.semaphore("a_rope_step"))
            zeros_set = stage.enter_context(nc.semaphore("zeros_set"))
            pad_set = stage.enter_context(nc.semaphore("pad_set"))
            block = stage.enter_context(nc.Block())

            @block.sync
            def _(sp):
                sp_credits(sp, s)
                for dst, src in ((wqkv[:], io["w_qkv"]), (ident[:], io["ident"]),
                                 (cos[:], io["cos"]), (sin[:], io["sin"])):
                    sp.dma_start(dst, src).then_inc(const_loaded, 16)
                sp.dma_start(scales[:, 0, :], io["q_scale"].to_broadcast([P, D])).then_inc(const_loaded, 16)
                sp.dma_start(scales[:, 1, :], io["k_scale"].to_broadcast([P, D])).then_inc(const_loaded, 16)
                with sp.Fori(0, AHEAD) as it:
                    sp.wait_ge(s["v_ps"], it * 2 + 1)
                    sp_load_x(sp, s, it)
                    sp.wait_ge(s["v_ready"], it * 2 + 4)
                    sp_store_v(sp, s, it)
                    sp.wait_ge(s["parts_ready"], it * 2 + 4)
                    sp_store_parts(sp, s, it // 4, it % 4)
                sp.wait_ge(s["v_written"], 16 * (AHEAD + 1))
                sp.wait_ge(s["parts_written"], PARTS_WRITTEN * (AHEAD + 1))

            @block.tensor
            def _(pe):
                pe.sem_inc(s["v_ps"], 1)
                pe.wait_ge(const_loaded, 16 * 6)
                with pe.Fori(0, AHEAD) as it:
                    for u in range(2):
                        if u == 0:
                            pe.wait_ge(s["x_loaded"], it * 16 + 16)
                        pe.wait_ge(s["raw_ready"], it * 2 + u + 1)
                        pe_qk(pe, u, S[u][:, 0:512]).then_inc(s["qk_ps"], 1)
                        pe.wait_ge(s["v_ready"], it * 2 + u + 1)
                        pe_v(pe, u, S[u][:, 512:1024]).then_inc(s["v_ps"], 1)
                    for u in range(2):
                        pe.wait_ge(s["qn_ready"], it * 2 + u + 3)
                        pe.wait_ge(s["t_taken"], it * 2 + u + 1)
                        pe_turn(pe, u, X[u]).then_inc(s["t_ps"], 1)

            @block.scalar
            def _(act):
                act.sem_inc(s["raw_ready"], 2)
                act.sem_inc(s["v_ready"], 2)
                act.wait_ge(pad_set, 1)
                with act.Fori(0, AHEAD) as it:
                    for u in range(2):
                        act.wait_ge(s["qk_ps"], it * 2 + u + 1)
                        act.wait_ge(s["qn_ready"], it * 2 + u + 1)
                        nc.scalar.copy(raw[:, u, :], S[u][:, 0:512]).then_inc(s["raw_ready"], 1)
                        if u == 0:
                            act.wait_ge(s["v_written"], it * 16 + 16)
                        act.wait_ge(s["v_ps"], it * 2 + u + 2)
                        nc.scalar.copy(vbuf[:, u, :, 0:D],
                                       S[u][:, 512:512 + C].rearrange("p (h d) -> p h d", d=D)).then_inc(s["v_ready"], 1)
                    for u in range(2):
                        act.wait_ge(s["t_ps"], it * 2 + u + 1)
                        if u == 0:
                            act.wait_ge(s["parts_written"], it * PARTS_WRITTEN + PARTS_WRITTEN)
                        nc.scalar.copy(parts[:, 0, :, u, :],
                                       X[u][:].rearrange("p (c t) -> p c t", c=4)).then_inc(s["hi_ready"], 1)

            @block.vector
            def _(dve):
                count = [0]

                def once(ins):
                    count[0] += 1
                    ins.then_inc(table_step, 1)
                    dve.wait_ge(table_step, count[0])

                nc.vector.memset(vbuf[:, :, :, D + 1:VW], 0.0)
                nc.vector.memset(vbuf[:, :, :, D:D + 1], 1.0).then_inc(pad_set, 1)
                nc.vector.memset(kst[STACK:P, :, :, :], 1.0)
                nc.vector.memset(qst[STACK:P, :, :, :], 0.0)
                dve.wait_ge(const_loaded, 16 * 6)
                half = D // 2
                for a in range(2):
                    def scale(lo, hi):
                        return scales[:, a:a + 1, lo:hi].to_broadcast([P, B * KT, hi - lo])
                    nc.vector.tensor_tensor(rope_c[:, :, a, :], cos[:], scale(0, D), ALU.mult)
                    nc.vector.tensor_tensor(rope_s[:, :, a, 0:half], sin[:, :, 0:half], scale(half, D), ALU.mult)
                    once(nc.vector.tensor_tensor(rope_s[:, :, a, half:D], sin[:, :, half:D], scale(0, half), ALU.mult))
                once(nc.vector.tensor_reduce(bound[:, 0:2], scales[0:1], AX.X, ALU.max, apply_absolute_value=True))
                once(nc.vector.tensor_tensor(bound[:, 2:3], bound[:, 0:1], bound[:, 1:2], ALU.mult))
                once(nc.vector.tensor_scalar(flag[:], bound[:, 2:3], SAFE_LOGIT * D ** 0.5 / D, None, ALU.is_le))
                dve.sem_inc(s["qn_ready"], 2)
                dve.sem_inc(s["t_taken"], 2)
                with dve.Fori(0, AHEAD) as it:
                    links = [0]

                    def link(ins):
                        links[0] += 1
                        ins.then_inc(rope_step, 1)
                        dve.wait_ge(rope_step, it * (2 * ROPE_LINKS) + links[0])

                    for u in range(2):
                        dve_rope(dve, s, link, it * 2 + u, it * 2 + u, u)
                    for u in range(2):
                        dve_rest(dve, s, it * 2 + u, u, X[u], s["hi_ready"], it * 2 + u + 1)
                    assert links[0] == 2 * ROPE_LINKS

            @block.gpsimd
            def _(pool):
                pool.sem_inc(s["parts_ready"], 2)
                nc.gpsimd.memset(zeros[:], 0.0).then_inc(zeros_set, 1)
                pool.wait_ge(zeros_set, 1)
                with pool.Fori(0, AHEAD) as it:
                    for u in range(2):
                        pool_square(pool, s, it * 2 + u, u)
                    for u in range(2):
                        pool_parts(pool, s, it * 2 + u, u)

        with ExitStack() as stage:
            s = projection_semaphores(stage, "m")

            def sem(name):
                return stage.enter_context(nc.semaphore(name))

            flag_read = sem("flag_read")
            rope_step = sem("m_rope_step")
            stacks_loaded = [sem(f"stacks_loaded{n}") for n in range(2)]
            qk_done, exp_done, av_done = sem("qk_done"), sem("exp_done"), sem("av_done")
            o_copied, at_ps, at_taken = sem("o_copied"), sem("at_ps"), sem("at_taken")
            rden_ready, attn_written = sem("rden_ready"), sem("attn_written")
            row_scores, row_taken, rows_turned = sem("row_scores"), sem("row_taken"), sem("rows_turned")
            shift_ready, shift_loaded = sem("shift_ready"), sem("shift_loaded")
            shift_high, shift_stored = sem("shift_high"), sem("shift_stored")
            block = stage.enter_context(nc.Block())
            LOADS = 16 * (2 * len(Q_PART) + 1)
            TILES = HG * KT

            WITH, WITHOUT = LOOP_PAIRS // 2, GROUPS // 2 - 1 - LOOP_PAIRS // 2

            def run_groups(eng, body):
                with eng.Fori(0, WITH) as jj:
                    for par in range(2):
                        body(jj * 2 + par, par, True, False)
                with eng.Fori(WITH, WITH + WITHOUT) as jj:
                    for par in range(2):
                        body(jj * 2 + par, par, False, False)
                for par in range(2):
                    body(GROUPS - 2 + par, par, False, par == 1)

            @block.sync
            def _(sp):
                def load_stacks(i, par):
                    b, g = i // GPB, i % GPB
                    for a, (dst, order) in enumerate(((qst, Q_PART), (kst, K_PART))):
                        for r, part in enumerate(order):
                            src = qk_parts[part, a, bass.ds(b, 1), bass.ds(g * HG * D, HG * D), :] \
                                .rearrange("o (h d) t -> d (o h) t", d=D)
                            sp.dma_start(dst[r * D:(r + 1) * D, par], src).then_inc(stacks_loaded[par], 16)
                    src = v_scratch[bass.ds(b * (KT // 2), KT // 2), :, :, bass.ds(g * HG, HG), :] \
                        .rearrange("q u p h w -> p (q u) (h w)")
                    sp.dma_start(vst[:, par].rearrange("p k h w -> p k (h w)"), src).then_inc(stacks_loaded[par], 16)

                sp_credits(sp, s)
                sp.sem_inc(attn_written, 16)
                general = sp.value_load(flag[:], min_val=0, max_val=1)

                def load_shift(i, par):
                    with sp.If(general < 1):
                        sp.wait_ge(shift_ready, i + 1)
                        sp.dma_start(shift_scratch.rearrange("r (n q) -> n r q", q=P), shift[:]).then_inc(shift_stored, 16)
                        sp.wait_ge(shift_stored, (i + 1) * 16)
                        sp.dma_start(qst[STACK:STACK + SHIFT, par].rearrange("r h t -> r (h t)"),
                                     shift_scratch).then_inc(shift_loaded, 16)

                load_stacks(0, 0)
                load_shift(0, 0)

                def body(i, par, project, last):
                    if project:
                        sp.wait_ge(s["v_ps"], i * 2 + 1)
                        sp_load_x(sp, s, i + AHEAD)
                    if not last:
                        sp.wait_ge(av_done, i * KT + 1)
                        if project:
                            sp.wait_ge(s["v_written"], i * 16 + 16)
                            sp.wait_ge(s["parts_written"], i * PARTS_WRITTEN + PARTS_WRITTEN)
                        elif not isinstance(i, int):
                            sp.wait_ge(s["v_written"], 16 * (LOOP_PAIRS + 1))
                            sp.wait_ge(s["parts_written"], PARTS_WRITTEN * (LOOP_PAIRS + 1))
                        load_stacks(i + 1, 1 - par)
                    if project:
                        sp.wait_ge(s["v_ready"], i * 2 + 4)
                        sp_store_v(sp, s, i + AHEAD)
                        sp.wait_ge(s["parts_ready"], i * 2 + 4)
                        sp_store_parts(sp, s, (i + AHEAD) // 4, (i + AHEAD) % 4)
                    if not last:
                        load_shift(i + 1, 1 - par)
                    sp.wait_ge(at_taken, i * 2 + 4)
                    sp.dma_start(attn_scratch[bass.ds(i, 1)].rearrange("o t p c -> p (o t) c"),
                                 attn[:].rearrange("p t h d -> p t (h d)")).then_inc(attn_written, 16)

                run_groups(sp, body)
                sp.wait_ge(attn_written, 16 * (GROUPS + 1))

            @block.tensor
            def _(pe):
                pe.sem_inc(s["v_ps"], 1)
                pe.sem_inc(av_done, 1)
                general = pe.value_load(flag[:], min_val=0, max_val=1)

                def scores(i, par, kt, h):
                    n = kt * HG + h
                    pe.wait_ge(exp_done, i * TILES + n + 1)
                    for half in range(2):
                        mm = pe.matmul(S[h % 2][:, half * 512:(half + 1) * 512],
                                       kst[0:STACK + SHIFT, par, h, kt * P:(kt + 1) * P],
                                       qst[0:STACK + SHIFT, par, h, half * 512:(half + 1) * 512],
                                       start=True, stop=True)
                    mm.then_inc(qk_done, 1)

                def values(i, par, kt, half):
                    if half == 0:
                        pe.wait_ge(exp_done, i * TILES + kt * HG + HG + 2)
                        if kt == 0:
                            pe.wait_ge(o_copied, i * 2 + 2)
                    for h in range(HG):
                        mm = pe.matmul(O[h * VW:(h + 1) * VW, half * 512:(half + 1) * 512],
                                       vst[:, par, kt, h, :], prob[:, kt % 2, h, half * 512:(half + 1) * 512],
                                       start=(kt == 0), stop=(kt == KT - 1))
                    if half == 1:
                        mm.then_inc(av_done, 1)

                def turn_output(i, half):
                    pe.wait_ge(o_copied, i * 2 + half + 3)
                    pe.wait_ge(at_taken, i * 2 + half + 1)
                    for t in range(4):
                        mm = pe.transpose(X[half][:, t * P:(t + 1) * P],
                                          oT[:, half * 512 + t * P:half * 512 + (t + 1) * P], ident[:])
                    mm.then_inc(at_ps, 1)

                def projection(i, slot):
                    u = 0 if slot in (1, 2, 6) else 1
                    if slot in (1, 3):
                        if slot == 1:
                            pe.wait_ge(s["x_loaded"], i * 16 + 16)
                            pe.wait_ge(at_taken, i * 2 + 1)
                        else:
                            pe.wait_ge(s["raw_ready"], i * 2 + 3)
                        pe_qk(pe, u, X[0]).then_inc(s["qk_ps"], 1)
                    elif slot in (2, 4):
                        if slot == 2:
                            pe.wait_ge(at_taken, i * 2 + 2)
                        else:
                            pe.wait_ge(s["v_ready"], i * 2 + 3)
                        pe_v(pe, u, X[1]).then_inc(s["v_ps"], 1)
                    elif slot in (6, 7):
                        pe.wait_ge(s["qn_ready"], i * 2 + u + 3)
                        pe.wait_ge(s["v_ready"] if u else s["raw_ready"], i * 2 + 4)
                        pe_turn(pe, u, X[u]).then_inc(s["t_ps"], 1)

                def row_maxima(i, par):
                    with pe.If(general < 1):
                        pe.wait_ge(stacks_loaded[par], (i // 2) * LOADS + LOADS)
                        pe.wait_ge(exp_done, i * TILES + 2)
                        for n in range(TILES):
                            h, t = n // KT, n % KT
                            pe.wait_ge(row_taken, i * TILES + n + 1)
                            for half in range(2):
                                mm = pe.matmul(S[n % 2][:, half * 512:(half + 1) * 512],
                                               qst[0:STACK, par, h, t * P:(t + 1) * P],
                                               kst[0:STACK, par, h, half * 512:(half + 1) * 512],
                                               start=True, stop=True)
                            mm.then_inc(row_scores, 1)
                        pe.wait_ge(row_taken, (i + 1) * TILES + 2)
                        pe.transpose(S[0][0:TILES, 0:P], rmax[:], ident[:]).then_inc(rows_turned, 1)
                        pe.wait_ge(shift_loaded, (i + 1) * 16)

                def first_slot(i, par, previous):
                    row_maxima(i, par)
                    pe.wait_ge(stacks_loaded[par], (i // 2) * LOADS + LOADS)
                    for h in range(HG):
                        scores(i, par, 0, h)
                        if previous is not None and h < 2:
                            values(previous, 1 - par, KT - 1, h)
                    if previous is not None:
                        for half in range(2):
                            turn_output(previous, half)

                first_slot(0, 0, None)

                def body(i, par, project, last):
                    for kt in range(1, KT):
                        for h in range(HG):
                            scores(i, par, kt, h)
                            if h in (0, 2):
                                values(i, par, kt - 1, h // 2)
                            if h == 1 and project:
                                projection(i, kt)
                    if last:
                        for half in range(2):
                            values(i, par, KT - 1, half)
                        for half in range(2):
                            turn_output(i, half)
                    else:
                        first_slot(i + 1, 1 - par, i)

                run_groups(pe, body)

            @block.scalar
            def _(act):
                act.sem_inc(exp_done, 2)

                def exps(i, par, kt):
                    for h in range(HG):
                        n = kt * HG + h
                        act.wait_ge(qk_done, i * TILES + n + 1)
                        if h == 0:
                            wait(act, av_done, i * KT + kt)
                        nc.scalar.activation(prob[:, kt % 2, h, :], S[h % 2][:], ACT.Exp,
                                             scale=float(D) ** -0.5).then_inc(exp_done, 1)

                exps(0, 0, 0)

                def body(i, par, project, last):
                    for kt in range(1, KT):
                        exps(i, par, kt)
                    if not last:
                        exps(i + 1, 1 - par, 0)

                run_groups(act, body)

            @block.vector
            def _(dve):
                dve.sem_inc(s["raw_ready"], 2)
                dve.sem_inc(s["v_ready"], 2)
                dve.sem_inc(s["qn_ready"], 2)
                dve.sem_inc(s["t_taken"], 2)
                dve.sem_inc(o_copied, 2)
                dve.sem_inc(at_taken, 2)
                dve.sem_inc(row_taken, 2)
                general = dve.value_load(flag[:], min_val=0, max_val=1)

                def raw_copy(i, u):
                    dve.wait_ge(s["qk_ps"], i * 2 + u + 1)
                    nc.vector.tensor_copy(raw[:, u, :], X[0][:]).then_inc(s["raw_ready"], 1)

                def v_copy(i, u):
                    if u == 0:
                        dve.wait_ge(s["v_written"], i * 16 + 16)
                    dve.wait_ge(s["v_ps"], i * 2 + u + 2)
                    nc.vector.tensor_copy(vbuf[:, u, :, 0:D],
                                          X[1][:, 0:C].rearrange("p (h d) -> p h d", d=D)).then_inc(s["v_ready"], 1)

                def first_part(i, u):
                    dve.wait_ge(s["t_ps"], i * 2 + u + 1)
                    if u == 0:
                        dve.wait_ge(s["parts_written"], i * PARTS_WRITTEN + PARTS_WRITTEN)
                    nc.vector.tensor_copy(parts[:, 0, :, u, :],
                                          X[u][:].rearrange("p (c t) -> p c t", c=4)).then_inc(s["hi_ready"], 1)

                def row_maxima(i):
                    with dve.If(general < 1):
                        for n in range(TILES):
                            dve.wait_ge(row_scores, i * TILES + n + 1)
                            nc.vector.tensor_reduce(rmax[:, n:n + 1], S[n % 2][:], AX.X, ALU.max)\
                                .then_inc(row_taken, 1)
                        dve.wait_ge(rows_turned, i + 1)
                        nc.vector.tensor_scalar(shift[:, 0, :], S[0][0:TILES, 0:P], -1.0, None, ALU.mult)\
                            .then_inc(shift_high, 1)
                        dve.wait_ge(shift_high, i + 1)
                        nc.vector.scalar_tensor_tensor(out=shift[:, 1, :], in0=S[0][0:TILES, 0:P], scalar=-1.0,
                                                       in1=shift[:, 0, :], op0=ALU.mult,
                                                       op1=ALU.subtract).then_inc(shift_ready, 1)

                row_maxima(0)

                def body(i, par, project, last):
                    if project:
                        links = [0]

                        def link(ins):
                            links[0] += 1
                            ins.then_inc(rope_step, 1)
                            dve.wait_ge(rope_step, i * (2 * ROPE_LINKS) + links[0])

                        raw_copy(i, 0)
                        v_copy(i, 0)
                        dve_rope(dve, s, link, i * 2, i * 2 + 2 * AHEAD, 0)
                        raw_copy(i, 1)
                        v_copy(i, 1)
                        dve_rope(dve, s, link, i * 2 + 1, i * 2 + 2 * AHEAD + 1, 1)
                        for u in range(2):
                            first_part(i, u)
                            dve_rest(dve, s, i * 2 + u, u, X[u], s["hi_ready"], i * 2 + u + 1)
                        assert links[0] == 2 * ROPE_LINKS
                    if not last:
                        row_maxima(i + 1)
                    for half in range(2):
                        if half == 0:
                            dve.wait_ge(av_done, (i + 1) * KT + 1)
                        nc.vector.tensor_copy(oT[:, half * 512:(half + 1) * 512],
                                              O[:, half * 512:(half + 1) * 512]).then_inc(o_copied, 1)
                    for half in range(2):
                        dve.wait_ge(at_ps, i * 2 + half + 1)
                        x = X[half][:].rearrange("p (c w) -> p c w", w=VW)
                        nc.vector.reciprocal(rden[:, half, :], x[:, :, D]).then_inc(rden_ready, 1)
                        dve.wait_ge(rden_ready, i * 2 + half + 1)
                        if half == 0:
                            dve.wait_ge(attn_written, i * 16 + 16)
                        nc.vector.tensor_tensor(attn[:, half * 4:(half + 1) * 4].rearrange("p t h d -> p (t h) d"),
                                                x[:, :, 0:D],
                                                rden[:, half, :, None].to_broadcast([P, 4 * HG, D]),
                                                ALU.mult).then_inc(at_taken, 1)

                run_groups(dve, body)

            @block.gpsimd
            def _(pool):
                pool.sem_inc(s["parts_ready"], 2)
                with pool.Fori(0, LOOP_PAIRS) as it:
                    for u in range(2):
                        pool_square(pool, s, it * 2 + u, u)
                    for u in range(2):
                        pool_parts(pool, s, it * 2 + u, u)


CHUNK = 4
CW = CHUNK * P
CHUNKS = B * N // CW
KC = 64
PAIRH = H // 2


def layer_norm(nc, link, y, dst, stats, mv, var, rsqrt, tail):
    for t in range(CHUNK):
        ins = nc.vector.bn_stats(stats[:, t, :], y[:, t, :])
    link(ins)
    mean, apart = mv[:, :, 0], mv[:, :, 1]
    nc.vector.tensor_tensor(mean, stats[:, :, 1], stats[:, :, 4], ALU.add)
    nc.vector.tensor_tensor(apart, stats[:, :, 1], stats[:, :, 4], ALU.subtract)
    link(nc.vector.tensor_tensor(var, stats[:, :, 2], stats[:, :, 5], ALU.add))
    nc.vector.tensor_scalar(mean, mean, 0.5, None, ALU.mult)
    nc.vector.tensor_tensor(apart, apart, apart, ALU.mult)
    link(nc.vector.tensor_scalar(var, var, 1.0 / C, LN_EPS, ALU.mult, ALU.add))
    link(nc.vector.scalar_tensor_tensor(out=var, in0=apart, scalar=0.25, in1=var, op0=ALU.mult, op1=ALU.add))
    newton_rsqrt(nc, link, *rsqrt, var)
    for t in range(CHUNK):
        ins = nc.vector.tensor_scalar(dst(t), y[:, t, :], mv[:, t, 0:1], rsqrt[0][:, t:t + 1],
                                      ALU.subtract, ALU.mult)
    tail(ins)


def cross_attention_phase(nc, io, attn_scratch, x_all, w1):
    with ExitStack() as ctx:
        def sb(name, shape, dt=F32):
            return ctx.enter_context(nc.sbuf_tensor(name, shape, dt))

        def psum(name, shape):
            return ctx.enter_context(nc.psum_tensor(name, shape, F32))

        def sem(name):
            return ctx.enter_context(nc.semaphore(name))

        ident = sb("ident2", [P, P])
        wproj, wq, wk = sb("wproj", [P, 2, C]), sb("wq", [P, 2, C]), sb("wk", [P, 2, C])
        wv, wo = sb("wv", [P, 2, C]), sb("wo", [P, 2, C])
        rows = {n: sb("row_" + n, [P, C]) for n in ("b_proj", "bv", "bo")}
        cols = sb("bias_cols", [P, 2, 2])
        head_mask = sb("head_mask", [P, P // D])
        half_mask = sb("half_mask", [P, 2 * D])
        ctxT = sb("ctxT", [P, 2, B, KC])
        ctxT2 = sb("ctxT2", [P, 2, B, 2, KC])
        kT = sb("kT", [P, 2, B, KC])
        kbd = sb("kbd", [P, B, 2, P // D, KC])
        vrow = sb("vrow", [P, B, C])
        vbd_all = sb("vbd_all", [P, B, PAIRH, 2 * D])
        vbd = sb("vbd", [P, PAIRH, 2 * D])

        at = sb("at", [P, CHUNK, C])
        aT = sb("aT", [P, 2, CW])
        y1 = sb("y1", [P, CHUNK, C])
        x1 = sb("x1", [P, CHUNK, C])
        x1T = sb("x1T", [P, 2, CW])
        qT = sb("qT", [P, 2, CW])
        mx = sb("mx", [P, 2, H])
        z = sb("z", [P, 2, H * KC])
        pr = sb("pr", [P, 2, H * KC])
        pT = sb("pT", [P, PAIRH, CW])
        rden = sb("rden2", [P, 2, CW])
        oT = sb("oT2", [P, 2, CW])
        y2 = sb("y2", [P, CHUNK, C])
        stats = sb("stats", [P, 2, CHUNK, 6])
        mv = sb("mv", [P, 2, CHUNK, 2])
        var, ln_t, ln_h, ln_r = (sb(n, [P, 2, CHUNK]) for n in ("var", "ln_t", "ln_h", "ln_r"))

        W = [psum(f"W{n}", [P, 2 * 512]) for n in range(2)]
        SS = [psum(f"SS{n}", [P, 2 * 512]) for n in range(2)]

        weights_loaded, x_in = sem("weights_loaded"), sem("x_in")
        at_loaded, vbd_loaded = sem("at_loaded"), sem("vbd_loaded")
        full = {j: sem("full_" + j) for j in ("prep", "x1T", "V", "D", "aT", "q", "proj", "O", "pT", "S")}
        taken = {j: sem("taken_" + j) for j in ("prep", "x1T", "V", "D", "aT", "q", "proj", "O", "pT")}
        z_ready, exp_done, x1_ready = sem("z_ready"), sem("exp_done2"), sem("x1_ready")
        bias_added, dve_step = sem("bias_added"), sem("dve_step2")
        max_ready, w1_loaded = sem("max_ready"), sem("w1_loaded")
        def run_chunks(eng, body):
            body(-1, True, False, False)
            body(0, True, True, False)
            body(1, True, True, True)
            with eng.Fori(2, CHUNKS - 1) as c:
                body(c, True, True, True)
            body(CHUNKS - 1, False, True, True)
            body(CHUNKS, False, False, True)

        PREP_DVE = 2 + B

        block = ctx.enter_context(nc.Block())

        @block.sync
        def _(sp):
            for dst, src in ((ident[:], io["ident"]), (wk[:], io["WkT"]), (wv[:], io["WvT"]), (ctxT[:], io["ctxT"]),
                             (ctxT2[:], io["ctxT2"]), (cols[:], io["bias_cols"]), (head_mask[:], io["head_mask"]),
                             (half_mask[:], io["half_mask"]), (wproj[:], io["w_proj"]), (wq[:], io["WqT"]), (wo[:], io["WoT"])):
                sp.dma_start(dst, src).then_inc(weights_loaded, 16)
            for dst, src in ((rows["b_proj"], io["b_proj"]), (rows["bv"], io["bv"]), (rows["bo"], io["bo"])):
                sp.dma_start(dst[:], src.to_broadcast([P, C])).then_inc(weights_loaded, 16)
            sp.dma_start(x_all[:], io["x"]).then_inc(x_in, 16)

            sp.dma_start(w1[:].rearrange("p (c n) -> p c n", c=2), io["W1"].rearrange("p c e f -> p c (e f)")).then_inc(w1_loaded, 16)

            def load_at(c):
                for t in range(CHUNK):
                    b, half = c // 2, c % 2
                    src = attn_scratch[bass.ds(b * GPB, GPB), bass.ds(half * CHUNK + t, 1)] \
                        .rearrange("g o p c -> p (g o) c")
                    sp.dma_start(at[:, t, :].rearrange("p (g c) -> p g c", g=GPB), src).then_inc(at_loaded, 16)

            def body(c, first, mid, last):
                if first:
                    if not (isinstance(c, int) and c < 0):
                        sp.wait_ge(full["aT"], c + 1)
                    load_at(c + 1)
                if last:
                    wait(sp, full["V"], c - 1)
                    sp.wait_ge(taken["prep"], PREP_DVE)
                    sp.dma_start(vbd[:], vbd_all[:, bass.ds((c - 1) // 2, 1)].rearrange("p o h d -> p (o h) d")) \
                        .then_inc(vbd_loaded, 16)

            run_chunks(sp, body)
            sp.wait_ge(w1_loaded, 16)

        @block.tensor
        def _(pe):
            pe.wait_ge(weights_loaded, 16 * 14)
            for m in range(2):
                for ci in range(2):
                    mm = pe.matmul(W[m][:, 0:B * KC], wk[:, ci, m * P:(m + 1) * P],
                                   ctxT[:, ci].rearrange("p b k -> p (b k)"), start=(ci == 0), stop=(ci == 1))
                mm.then_inc(full["prep"], 1)
            for b in range(B):
                pe.wait_ge(taken["prep"], b + 1)
                for ci in range(2):
                    mm = pe.matmul(W[b % 2][:, 0:C], ctxT2[:, ci, b].rearrange("p j k -> p (j k)"), wv[:, ci, :],
                                   start=(ci == 0), stop=(ci == 1))
                mm.then_inc(full["prep"], 1)
            pe.wait_ge(taken["prep"], PREP_DVE)

            def turn(dst, src):
                for ci in range(2):
                    for t in range(CHUNK):
                        mm = pe.transpose(dst[:, ci * CW + t * P:ci * CW + (t + 1) * P],
                                          src[:, t, ci * P:(ci + 1) * P], ident[:])
                return mm

            def scores(c, t):
                wait(pe, z_ready, c * CHUNK + t - 1)
                for g in range(2):
                    mm = pe.matmul(SS[t % 2][:, g * 512:(g + 1) * 512], qT[:, g, t * P:(t + 1) * P],
                                   kbd[:, bass.ds(c // 2, 1), g].rearrange("p o h k -> p (o h k)"),
                                   start=True, stop=True)
                mm.then_inc(full["S"], 1)

            def project(c, pair):
                if pair == 0:
                    pe.wait_ge(taken["aT"], c + 1)
                else:
                    wait(pe, taken["q"], c)
                for t in range(2 * pair, 2 * pair + 2):
                    for ci in range(2):
                        mm = pe.matmul(W[1 - pair][:, (t % 2) * C:(t % 2 + 1) * C], aT[:, ci, t * P:(t + 1) * P],
                                       wproj[:, ci, :], start=(ci == 0), stop=(ci == 1))
                mm.then_inc(full["proj"], 1)

            def turn_probs(c, t):
                pe.wait_ge(exp_done, c * CHUNK + t + 1)
                if t >= 2:
                    pe.wait_ge(taken["pT"], c * CHUNK + t - 1)
                else:
                    wait(pe, *((taken["proj"], c * 4 + 8) if t == 0 and not (isinstance(c, int) and c == CHUNKS - 1)
                               else (taken["q"], c + 1) if t == 0 else (taken["O"], c * CHUNK)))
                for h in range(PAIRH):
                    mm = pe.transpose(W[t % 2][:, h * P:(h + 1) * P], pr[:, t % 2, h * P:(h + 1) * P], ident[:])
                mm.then_inc(full["pT"], 1)

            def weighted(job, c, lhs):
                for g in range(2):
                    for j in range(4):
                        mm = pe.matmul(W[1 if job == "V" else 0][32 * j:32 * j + 32, g * CW:(g + 1) * CW],
                                       lhs(4 * g + j), pT[:, 4 * g + j, :], start=True, stop=True)
                mm.then_inc(full[job], 1)

            def body(c, first, mid, last):
                if mid:
                    pe.wait_ge(x1_ready, c + 1)
                    wait(pe, taken["pT"], c * CHUNK - 1)
                    if isinstance(c, int) and c == 0:
                        pe.wait_ge(taken["proj"], 4)
                    turn(W[0], x1).then_inc(full["x1T"], 1)
                if last:
                    pe.wait_ge(taken["pT"], c * CHUNK)
                    pe.wait_ge(vbd_loaded, c * 16)
                    weighted("V", c - 1, lambda h: vbd[:, h, :])
                    if mid:
                        pe.wait_ge(taken["x1T"], c + 1)
                    weighted("D", c - 1, lambda h: half_mask[:])
                if first:
                    pe.wait_ge(at_loaded, (c + 2) * 16 * CHUNK)
                    wait(pe, taken["V"], c)
                    turn(W[1], at).then_inc(full["aT"], 1)
                if mid:
                    pe.wait_ge(taken["x1T"], c + 1)
                    wait(pe, taken["D"], c)
                    for m in range(2):
                        for ci in range(2):
                            mm = pe.matmul(W[0][:, m * CW:(m + 1) * CW], wq[:, ci, m * P:(m + 1) * P], x1T[:, ci, :],
                                           start=(ci == 0), stop=(ci == 1))
                    mm.then_inc(full["q"], 1)
                if first:
                    project(c + 1, 0)
                if mid:
                    pe.wait_ge(taken["q"], c + 1)
                    scores(c, 0)
                if first:
                    project(c + 1, 1)
                if mid:
                    scores(c, 1)
                if last:
                    pe.wait_ge(taken["V"], c)
                    if first:
                        pe.wait_ge(taken["proj"], (c + 1) * 4 + 2)
                    for t in range(CHUNK):
                        for ci in range(2):
                            mm = pe.matmul(W[1][:, t * C:(t + 1) * C], oT[:, ci, t * P:(t + 1) * P], wo[:, ci, :],
                                           start=(ci == 0), stop=(ci == 1))
                    mm.then_inc(full["O"], 1)
                if mid:
                    turn_probs(c, 0)
                    scores(c, 2)
                    turn_probs(c, 1)
                    scores(c, 3)
                    turn_probs(c, 2)
                    turn_probs(c, 3)

            run_chunks(pe, body)

        @block.scalar
        def _(act):
            act.wait_ge(weights_loaded, 16 * 14)

            def body(c, first, mid, last):
                if mid:
                    act.wait_ge(full["x1T"], c + 1)
                    nc.scalar.copy(x1T[:].rearrange("p c t -> p (c t)"), W[0][:]).then_inc(taken["x1T"], 1)
                if first:
                    act.wait_ge(full["aT"], c + 2)
                    if not (isinstance(c, int) and c < 0):
                        act.wait_ge(full["proj"], c * 2 + 2)
                    nc.scalar.copy(aT[:].rearrange("p c t -> p (c t)"), W[1][:]).then_inc(taken["aT"], 1)
                if mid:
                    act.wait_ge(full["q"], c + 1)
                    for m in range(2):
                        ins = nc.scalar.activation(qT[:, m, :], W[0][:, m * CW:(m + 1) * CW], ACT.Identity,
                                                   bias=cols[:, 0, m:m + 1])
                    ins.then_inc(taken["q"], 1)
                    for t in range(CHUNK):
                        act.wait_ge(z_ready, c * CHUNK + t + 1)
                        wait(act, full["pT"], c * CHUNK + t - 1)
                        nc.scalar.activation(pr[:, t % 2, :], z[:, t % 2, :], ACT.Exp,
                                             scale=float(D) ** -0.5).then_inc(exp_done, 1)
                        if t >= 1:
                            evacuate(c, t - 1)
                    evacuate(c, CHUNK - 1)

            def evacuate(c, t):
                act.wait_ge(full["pT"], c * CHUNK + t + 1)
                if t == 0:
                    wait(act, full["D"], c)
                nc.scalar.copy(pT[:, :, t * P:(t + 1) * P], W[t % 2][:].rearrange("p (h q) -> p h q", q=P)) \
                    .then_inc(taken["pT"], 1)

            run_chunks(act, body)

        @block.vector
        def _(dve):
            dve.wait_ge(weights_loaded, 16 * 14)
            steps = [0]

            def once(ins):
                steps[0] += 1
                ins.then_inc(max_ready, 1)
                dve.wait_ge(max_ready, steps[0])

            for m in range(2):
                dve.wait_ge(full["prep"], m + 1)
                nc.vector.tensor_scalar(kT[:, m].rearrange("p b k -> p (b k)"), W[m][:, 0:B * KC],
                                        cols[:, 1, m:m + 1], None, ALU.add).then_inc(taken["prep"], 1)
            for b in range(B):
                dve.wait_ge(full["prep"], 3 + b)
                nc.vector.tensor_tensor(vrow[:, b], W[b % 2][:, 0:C], rows["bv"][:], ALU.add) \
                    .then_inc(dve_step, 1)
                dve.wait_ge(dve_step, b + 1)
                ins = nc.vector.tensor_tensor(vbd_all[:, b], vrow[:, b].rearrange("p (h d) -> p h d", d=2 * D),
                                              half_mask[:, None, :].to_broadcast([P, PAIRH, 2 * D]), ALU.mult)
                ins.then_inc(taken["prep"], 1)
            for b in range(B):
                for m in range(2):
                    ins = nc.vector.tensor_tensor(kbd[:, b, m],
                                                  kT[:, m, b, None, :].to_broadcast([P, P // D, KC]),
                                                  head_mask[:, :, None].to_broadcast([P, P // D, KC]), ALU.mult)
            once(ins)
            dve.wait_ge(x_in, 16)
            once(nc.vector.tensor_tensor(x_all[:], x_all[:],
                                         rows["b_proj"][:, None, :].to_broadcast([P, B * KT, C]), ALU.add))
            BASE, MAXBASE = B, steps[0]

            def norm(which, y, dst, start, tail):
                n = [0]

                def link(ins):
                    n[0] += 1
                    ins.then_inc(dve_step, 1)
                    dve.wait_ge(dve_step, start + n[0])

                layer_norm(nc, link, y, dst, stats[:, which], mv[:, which], var[:, which],
                           (ln_r[:, which], ln_t[:, which], ln_h[:, which]), tail)
                return n[0]

            NORM = 4 + 3 + 9
            STEP1 = NORM + 1
            STEP2 = NORM

            def body(c, first, mid, last):
                if isinstance(c, int) and c <= 0:
                    base = BASE + (c + 1) * STEP1
                elif isinstance(c, int) and c == CHUNKS:
                    base = BASE + CHUNKS * STEP1 + (c - 1) * STEP2
                else:
                    base = (c + 1) * STEP1 + (c - 1) * STEP2 + BASE
                if last:
                    wait(dve, full["O"], c - 1)
                    dve.wait_ge(full["D"], c)
                    nc.vector.reciprocal(rden[:].rearrange("p c t -> p (c t)"), W[0][:]).then_inc(taken["D"], 1)
                    dve.wait_ge(taken["D"], c)
                    nc.vector.tensor_tensor(oT[:].rearrange("p c t -> p (c t)"), W[1][:],
                                            rden[:].rearrange("p c t -> p (c t)"), ALU.mult).then_inc(taken["V"], 1)
                if first:
                    for pair in range(2):
                        dve.wait_ge(full["proj"], (c + 1) * 2 + pair + 1)
                        for t in range(2 * pair, 2 * pair + 2):
                            nc.vector.tensor_tensor(y1[:, t, :], W[1 - pair][:, (t % 2) * C:(t % 2 + 1) * C],
                                                    x_all[:, bass.ds((c + 1) * CHUNK + t, 1), :]
                                                    .rearrange("p o c -> p (o c)"), ALU.add).then_inc(taken["proj"], 1)
                if mid:
                    attend(c, 0)
                    attend(c, 1)
                if first:
                    dve.wait_ge(taken["proj"], (c + 1) * 4 + 4)
                    if mid:
                        dve.wait_ge(full["x1T"], c + 1)
                    norm(0, y1, lambda t: x1[:, t, :], base, lambda ins: ins.then_inc(x1_ready, 1))
                    dve.wait_ge(x1_ready, c + 2)
                    nc.vector.tensor_tensor(x_all[:, bass.ds((c + 1) * CHUNK, CHUNK), :], x1[:],
                                            rows["bo"][:, None, :].to_broadcast([P, CHUNK, C]), ALU.add) \
                        .then_inc(dve_step, 1)
                    dve.wait_ge(dve_step, base + STEP1)
                if last:
                    dve.wait_ge(full["O"], c)
                    for t in range(CHUNK):
                        nc.vector.tensor_tensor(y2[:, t, :], W[1][:, t * C:(t + 1) * C],
                                                x_all[:, bass.ds((c - 1) * CHUNK + t, 1), :]
                                                .rearrange("p o c -> p (o c)"), ALU.add).then_inc(taken["O"], 1)
                if mid:
                    attend(c, 2)
                    attend(c, 3)
                if last:
                    dve.wait_ge(taken["O"], c * CHUNK)
                    norm(1, y2, lambda t: x_all[:, bass.ds((c - 1) * CHUNK + t, 1), :].rearrange("p o c -> p (o c)"),
                         base + (STEP1 if first else 0), lambda ins: ins.then_inc(bias_added, 1))
                    dve.wait_ge(bias_added, c)

            def attend(c, t):
                dve.wait_ge(full["S"], c * CHUNK + t + 1)
                s = SS[t % 2][:].rearrange("p (h k) -> p h k", k=KC)
                nc.vector.tensor_reduce(mx[:, t % 2, :], s, AX.X, ALU.max).then_inc(max_ready, 1)
                dve.wait_ge(max_ready, c * CHUNK + t + 1 + MAXBASE)
                wait(dve, exp_done, c * CHUNK + t - 1)
                nc.vector.tensor_tensor(z[:, t % 2, :].rearrange("p (h k) -> p h k", k=KC), s,
                                        mx[:, t % 2, :, None].to_broadcast([P, H, KC]), ALU.subtract) \
                    .then_inc(z_ready, 1)
                dve.wait_ge(z_ready, c * CHUNK + t + 1)

            run_chunks(dve, body)


GT = 32
ES = 128
F = 32
QUADS = ES // 4
GB = N // GT
GALL = B * GB
HALF_C = C // 2


def route_phase(nc, io, x_all, w1, perm_all, inner):
    with ExitStack() as ctx:
        def sb(name, shape, dt=F32):
            return ctx.enter_context(nc.sbuf_tensor(name, shape, dt))

        def sem(name):
            return ctx.enter_context(nc.semaphore(name))

        ident, identb = sb("ident3", [P, P]), sb("ident3b", [P, P], BF16)
        w1 = w1[:].rearrange("p (c e f) -> p c e f", c=2, f=F)
        wc = sb("wc", [P, 2, ES])
        b1 = sb("b1", [P, QUADS])
        bc = sb("bc", [P, 1])
        tie = sb("tie", [P, GT])
        xs = sb("xs", [P, KT, C])
        xT = sb("xT3", [P, 2, N])
        lg = sb("lg", [P, N])
        gmax = sb("gmax", [P, GB])
        permT = sb("permT", [P, N], BF16)
        perm = sb("perm", [P, KT, ES], BF16)
        xp = sb("xp", [P, SPLIT, KT, C], BF16)
        taken_x = sb("taken_x", [P, 2, ES, GB])

        banks = [ctx.enter_context(nc.psum_tensor(f"R{n}", [P, 512], F32)) for n in range(8)]
        loaded = sem("loaded3")
        xs_ready, turned, xT_ready, logits_done = sem("xs_ready"), sem("turned"), sem("xT_ready"), sem("logits_done")
        lg_step, perm_ready, perm_turned, perm_out = sem("lg_step"), sem("perm_ready"), sem("perm_turned"), sem("perm_out")
        hi_ready, rest_ready, mid_ready, lo_ready = sem("hi3"), sem("rest3"), sem("mid3"), sem("lo3")
        gathered, got_act, got_dve = sem("gathered"), sem("got_act"), sem("got_dve")
        hidden_done, hidden_out = sem("hidden_done"), sem("hidden_out")
        zeros_set, perm_kept = sem("zeros_set3"), sem("perm_kept")
        block = ctx.enter_context(nc.Block())

        @block.sync
        def _(sp):
            for dst, src in ((ident[:], io["ident"]), (wc[:], io["Wc"]), (b1[:], io["b1"]), (bc[:], io["bc"]),
                             (tie[:], io["tie"].to_broadcast([P, GT]))):
                sp.dma_start(dst, src).then_inc(loaded, 16)

        @block.gpsimd
        def _(pool):
            nc.gpsimd.memset(inner[:], 0.0).then_inc(zeros_set, 1)
            pool.sem_inc(lo_ready, 1)
            with pool.Fori(0, B) as b:
                pool.wait_ge(rest_ready, b + 1)
                nc.gpsimd.tensor_tensor(xp[:, 2], xs[:], xp[:, 1], ALU.subtract).then_inc(lo_ready, 1)

        @block.tensor
        def _(pe):
            pe.wait_ge(loaded, 16 * 5)
            with pe.Fori(0, B) as b:
                pe.wait_ge(xs_ready, b + 1)
                for ci in range(2):
                    for half in range(2):
                        for t in range(4):
                            mm = pe.transpose(banks[ci * 2 + half][:, t * P:(t + 1) * P],
                                              xs[:, half * 4 + t, ci * P:(ci + 1) * P], ident[:])
                mm.then_inc(turned, 1)
                pe.wait_ge(xT_ready, b + 1)
                for half in range(2):
                    for ci in range(2):
                        mm = pe.matmul(banks[4 + half][:], wc[:, ci, :], xT[:, ci, half * 512:(half + 1) * 512],
                                       start=(ci == 0), stop=(ci == 1))
                mm.then_inc(logits_done, 1)
                pe.wait_ge(perm_ready, b + 1)
                for t in range(KT):
                    mm = pe.transpose(banks[6][:].bitcast(BF16)[:, t * ES:(t + 1) * ES],
                                      permT[:, t * P:(t + 1) * P], identb[:])
                mm.then_inc(perm_turned, 1)
                pe.wait_ge(perm_out, b + 1)
                pe.wait_ge(lo_ready, b + 2)
                for k in range(KT // 2):
                    if k >= 2:
                        pe.wait_ge(got_act, b * (KT // 2) + k - 1)
                        pe.wait_ge(got_dve, b * (KT // 2) + k - 1)
                    for t in range(2):
                        for ci in range(2):
                            for part in range(SPLIT):
                                for g in range(4):
                                    mm = pe.matmul(banks[(k % 2) * 4 + g][:, (t * 2 + ci) * ES:(t * 2 + ci + 1) * ES],
                                                   xp[g * GT:(g + 1) * GT, part, 2 * k + t, ci * P:(ci + 1) * P],
                                                   perm[g * GT:(g + 1) * GT, 2 * k + t, :],
                                                   start=(part == 0), stop=(part == SPLIT - 1))
                    mm.then_inc(gathered, 1)
                pe.wait_ge(got_act, (b + 1) * (KT // 2))
                pe.wait_ge(got_dve, (b + 1) * (KT // 2))
                for q in range(QUADS):
                    for ci in range(2):
                        for j in range(4):
                            mm = pe.matmul(banks[q // 16][j * F:(j + 1) * F, (q % 16) * GB:(q % 16 + 1) * GB],
                                           w1[:, ci, 4 * q + j, :], taken_x[:, ci, 4 * q + j, :],
                                           start=(ci == 0), stop=(ci == 1))
                mm.then_inc(hidden_done, 1)

        def gather_out(copy, k, g):
            src = banks[(k % 2) * 4 + g][:].rearrange("p (t c e) -> p t c e", t=2, c=2)
            for ci in range(2):
                ins = copy(taken_x[:, ci].rearrange("p e (t g) -> p t e g", g=4)[:, 2 * k:2 * k + 2, :, g],
                           src[:, :, ci, :])
            return ins

        @block.scalar
        def _(act):
            with act.Fori(0, B) as b:
                act.wait_ge(turned, b + 1)
                for ci in range(2):
                    for half in range(2):
                        ins = nc.scalar.copy(xT[:, ci, half * 512:(half + 1) * 512], banks[ci * 2 + half][:])
                ins.then_inc(xT_ready, 1)
                nc.scalar.copy(xp[:, 0], xs[:]).then_inc(hi_ready, 1)
                act.wait_ge(mid_ready, b + 1)
                nc.scalar.copy(xp[:, 1], xs[:]).then_inc(rest_ready, 1)
                act.wait_ge(perm_turned, b + 1)
                nc.scalar.copy(perm[:].rearrange("p t e -> p (t e)"), banks[6][:].bitcast(BF16)).then_inc(perm_out, 1)
                for k in range(KT // 2):
                    act.wait_ge(gathered, b * (KT // 2) + k + 1)
                    for g in range(2):
                        ins = gather_out(nc.scalar.copy, k, g)
                    ins.then_inc(got_act, 1)

        @block.vector
        def _(dve):
            dve.wait_ge(loaded, 16 * 5)
            nc.vector.tensor_copy(identb[:], ident[:])
            dve.wait_ge(zeros_set, 1)
            with dve.Fori(0, B) as b:
                dve.wait_ge(lo_ready, b + 1)
                nc.vector.tensor_copy(xs[:], x_all[:, bass.ds(b * KT, KT), :]).then_inc(xs_ready, 1)
                dve.wait_ge(hi_ready, b + 1)
                nc.vector.tensor_tensor(xs[:], xs[:], xp[:, 0], ALU.subtract).then_inc(mid_ready, 1)
                dve.wait_ge(logits_done, b + 1)
                for half in range(2):
                    ins = nc.vector.scalar_tensor_tensor(
                        out=lg[:, half * 512:(half + 1) * 512].rearrange("p (g t) -> p g t", t=GT),
                        in0=banks[4 + half][:].rearrange("p (g t) -> p g t", t=GT), scalar=bc[:, 0:1],
                        in1=tie[:, None, :].to_broadcast([P, GB // 2, GT]), op0=ALU.add, op1=ALU.add)
                ins.then_inc(lg_step, 1)
                dve.wait_ge(lg_step, b * 3 + 1)
                by_group = lg[:].rearrange("p (g t) -> p g t", t=GT)
                nc.vector.tensor_reduce(gmax[:], by_group, AX.X, ALU.max).then_inc(lg_step, 1)
                dve.wait_ge(lg_step, b * 3 + 2)
                nc.vector.tensor_tensor(permT[:].rearrange("p (g t) -> p g t", t=GT), by_group,
                                        gmax[:, :, None].to_broadcast([P, GB, GT]), ALU.is_equal) \
                    .then_inc(perm_ready, 1)
                dve.wait_ge(perm_ready, b + 1)
                nc.vector.tensor_copy(perm_all[:, bass.ds(b * N, N)], permT[:]).then_inc(perm_kept, 1)
                for k in range(KT // 2):
                    dve.wait_ge(gathered, b * (KT // 2) + k + 1)
                    for g in range(2, 4):
                        ins = gather_out(nc.vector.tensor_copy, k, g)
                    ins.then_inc(got_dve, 1)
                dve.wait_ge(hidden_done, b + 1)
                for half in range(2):
                    ins = nc.vector.tensor_tensor(
                        lg[:, half * 512:(half + 1) * 512].rearrange("p (q g) -> p q g", g=GB),
                        banks[half][:].rearrange("p (q g) -> p q g", g=GB),
                        b1[:, half * 16:(half + 1) * 16, None].to_broadcast([P, 16, GB]), ALU.add)
                ins.then_inc(lg_step, 1)
                dve.wait_ge(lg_step, b * 3 + 3)
                for j in range(4):
                    ins = nc.vector.tensor_scalar(
                        inner[j * F:(j + 1) * F, :, j, bass.ds(b * GB, GB)],
                        lg[j * F:(j + 1) * F, :].rearrange("p (q g) -> p q g", g=GB), 0.0, None, ALU.max)
                ins.then_inc(hidden_out, 1)
                dve.wait_ge(hidden_out, b + 1)


def combine_phase(nc, io, x_all, w1, perm_all, inner, out):
    with ExitStack() as ctx:
        def sb(name, shape, dt=F32):
            return ctx.enter_context(nc.sbuf_tensor(name, shape, dt))

        def sem(name):
            return ctx.enter_context(nc.semaphore(name))

        ident = sb("ident4", [P, P])
        w2 = w1[:, 0:QUADS * HALF_C].rearrange("p (q d) -> p q d", d=HALF_C)
        permf = w1[:, QUADS * HALF_C:QUADS * HALF_C + B * N]
        b2 = sb("b2", [ES, HALF_C])
        res = sb("res", [P, GALL, ES])
        resT = sb("resT", [P, 2, 4, HALF_C])
        stats = sb("stats4", [P, CHUNK, 6])
        mv = sb("mv4", [P, CHUNK, 2])
        var, ln_t, ln_h, ln_r = (sb(n, [P, CHUNK]) for n in ("var4", "ln_t4", "ln_h4", "ln_r4"))
        outer_banks = [ctx.enter_context(nc.psum_tensor(f"E{n}", [P, 512], F32)) for n in range(4)]
        turn_banks = [ctx.enter_context(nc.psum_tensor(f"T{n}", [P, 512], F32)) for n in range(2)]
        sum_banks = [ctx.enter_context(nc.psum_tensor(f"Y{n}", [P, 512], F32)) for n in range(2)]
        loaded, w2_loaded = sem("loaded4"), sem("w2_loaded")
        outer_done, out_act, out_dve = sem("outer_done"), sem("out_act"), sem("out_dve")
        rows_turned, rows_act, rows_dve = sem("rows_turned4"), sem("rows_act"), sem("rows_dve")
        summed, added = sem("summed"), sem("added")
        permf_ready, ln_step, normed, stored = sem("permf_ready"), sem("ln_step"), sem("normed"), sem("stored")
        block = ctx.enter_context(nc.Block())
        TILES = B * KT

        @block.sync
        def _(sp):
            sp.dma_start(ident[:], io["ident"]).then_inc(loaded, 16)
            with sp.Fori(0, 2) as c:
                sp.wait_ge(summed, c * (TILES // 4) + 1)
                sp.dma_start(w2, io["W2T"][:, bass.ds(c, 1)].rearrange("p o q d -> p (o q) d")) \
                    .then_inc(w2_loaded, 16)
                sp.dma_start(b2[:], io["b2"][:, bass.ds(c, 1)].rearrange("e o d -> e (o d)")).then_inc(w2_loaded, 16)
            for k in range(CHUNKS):
                sp.wait_ge(normed, k + 1)
                sp.dma_start(out[:, k * CHUNK:(k + 1) * CHUNK], x_all[:, k * CHUNK:(k + 1) * CHUNK]) \
                    .then_inc(stored, 16)
            sp.wait_ge(stored, 16 * CHUNKS)

        @block.tensor
        def _(pe):
            pe.sem_inc(summed, 1)
            pe.wait_ge(loaded, 16)
            pe.wait_ge(permf_ready, 1)
            with pe.Fori(0, 2) as c:
                pe.wait_ge(w2_loaded, c * 32 + 32)
                for q in range(QUADS):
                    if q >= 4:
                        pe.wait_ge((out_act, out_dve)[q % 2], c * (QUADS // 2) + q // 2 - 1)
                    pe.matmul(outer_banks[q % 4][:], w2[:, q, :], inner[:, q].rearrange("p j g -> p (j g)"),
                              start=True, stop=True).then_inc(outer_done, 1)
                pe.wait_ge(out_act, (c + 1) * (QUADS // 2))
                pe.wait_ge(out_dve, (c + 1) * (QUADS // 2))

                def combine(k):
                    pe.wait_ge((rows_act, rows_dve)[k % 2], c * (TILES // 2) + k // 2 + 1)
                    y = sum_banks[(k // 4) % 2]
                    if k % 4 == 0 and k >= 8:
                        pe.wait_ge(added, c * (TILES // 4) + k // 4 - 1)
                    for first in (True, False):
                        for g in range(4):
                            mm = pe.matmul(y[g * GT:(g + 1) * GT, (k % 4) * HALF_C:(k % 4 + 1) * HALF_C],
                                           permf[:, k * P + g * GT:k * P + (g + 1) * GT],
                                           b2[:] if first else resT[:, k % 2, g, :],
                                           start=first, stop=not first)
                    if k % 4 == 3:
                        mm.then_inc(summed, 1)

                for k in range(TILES):
                    if k >= 2:
                        pe.wait_ge((rows_act, rows_dve)[k % 2], c * (TILES // 2) + k // 2)
                    for g in range(4):
                        mm = pe.transpose(turn_banks[k % 2][:, g * HALF_C:(g + 1) * HALF_C],
                                          res[:, 4 * k + g, :], ident[:])
                    mm.then_inc(rows_turned, 1)
                    if k >= 1:
                        combine(k - 1)
                combine(TILES - 1)
                pe.wait_ge(added, (c + 1) * (TILES // 4))

        def experts_out(copy, q):
            return copy(res[:, :, 4 * q:4 * q + 4].rearrange("p g j -> p j g"),
                        outer_banks[q % 4][:].rearrange("p (j g) -> p j g", j=4))

        def evacuate(eng, copy, c, which, out_sem, rows_sem, extra):
            for q in range(which, QUADS, 2):
                eng.wait_ge(outer_done, c * QUADS + q + 1)
                experts_out(copy, q).then_inc(out_sem, 1)
            for k in range(which, TILES, 2):
                eng.wait_ge(rows_turned, c * TILES + k + 1)
                copy(resT[:, k % 2].rearrange("p g d -> p (g d)"), turn_banks[k % 2][:]).then_inc(rows_sem, 1)
                extra(c, k)

        @block.scalar
        def _(act):
            with act.Fori(0, 2) as c:
                evacuate(act, nc.scalar.copy, c, 0, out_act, rows_act, lambda c, k: None)

        @block.vector
        def _(dve):
            nc.vector.tensor_copy(permf, perm_all[:]).then_inc(permf_ready, 1)

            def add(c, k4):
                dve.wait_ge(summed, c * (TILES // 4) + k4 + 2)
                x = x_all[:, k4 * 4:k4 * 4 + 4, bass.ds(c * HALF_C, HALF_C)]
                nc.vector.tensor_tensor(x, sum_banks[k4 % 2][:].rearrange("p (t d) -> p t d", d=HALF_C), x,
                                        ALU.add).then_inc(added, 1)

            with dve.Fori(0, 2) as c:
                evacuate(dve, nc.vector.tensor_copy, c, 1, out_dve, rows_dve,
                         lambda c, k: add(c, k // 4 - 1) if k % 4 == 1 and k > 4 else None)
                add(c, TILES // 4 - 1)

            n = [0]

            def link(ins):
                n[0] += 1
                ins.then_inc(ln_step, 1)
                dve.wait_ge(ln_step, n[0])

            dve.wait_ge(added, 2 * (TILES // 4))
            for k in range(CHUNKS):
                layer_norm(nc, link, x_all[:, k * CHUNK:(k + 1) * CHUNK], lambda t: x_all[:, k * CHUNK + t, :],
                           stats[:], mv[:], var[:], (ln_r[:], ln_t[:], ln_h[:]), lambda ins: ins.then_inc(normed, 1))
                dve.wait_ge(normed, k + 1)


def program(nc, io, out):
    qk_parts = nc.dram_tensor("qk_parts", [SPLIT, 2, B, C, N], BF16, kind="Internal").ap()
    v_scratch = nc.dram_tensor("v_scratch", [PAIRS, 2, P, H, VW], F32, kind="Internal").ap()
    attn_scratch = nc.dram_tensor("attn_scratch", [GROUPS, KT, P, HG * D], F32, kind="Internal").ap()
    shift_scratch = nc.dram_tensor("shift_scratch", [SHIFT, HG * N], BF16, kind="Internal").ap()
    attention_phases(nc, io, qk_parts, v_scratch, attn_scratch, shift_scratch)
    with nc.sbuf_tensor("x_all", [P, B * KT, C], F32) as x_all:
        with nc.sbuf_tensor("w1", [P, 2 * ES * F], F32) as w1:
            cross_attention_phase(nc, io, attn_scratch, x_all, w1)
            with nc.sbuf_tensor("perm_all", [P, B * N], BF16) as perm_all, \
                    nc.sbuf_tensor("inner", [P, QUADS, 4, GALL], F32) as inner:
                route_phase(nc, io, x_all, w1, perm_all, inner)
                combine_phase(nc, io, x_all, w1, perm_all, inner, out)


def kernel(**inputs):
    import numpy as np
    import concourse.bacc as bacc
    from concourse.bass_utils import run_bass_kernel_spmd as run

    a = {k: np.asarray(v) for k, v in inputs.items()}
    half = D // 2
    freqs = (1.0 / 2500 ** (np.arange(half, dtype=np.float32) / half)).astype(np.float32)
    angle = np.outer(np.arange(N, dtype=np.float32), freqs).astype(np.float32)
    angle = np.concatenate([angle, angle], -1)

    def by_tile(t):
        return np.ascontiguousarray(np.tile(t.reshape(KT, P, D).transpose(1, 0, 2), (1, B, 1)))

    sign = np.where(np.arange(D) < half, -1.0, 1.0).astype(np.float32)
    x = a["x"].reshape(B * N, C)
    ctxT = a["ctx_1024"].reshape(B * KC, C).T

    def by_half(w):
        return w.reshape(2, P, -1).transpose(1, 0, 2)

    arrays = {
        "xT": x.T.reshape(2, P, B * N).transpose(1, 0, 2),
        "w_qkv": a["L0_attn_w_qkv"].reshape(2, P, 3 * C).transpose(1, 0, 2),
        "q_scale": a["L0_attn_q_scale"].reshape(1, D),
        "k_scale": a["L0_attn_k_scale"].reshape(1, D),
        "ident": np.eye(P, dtype=np.float32),
        "cos": by_tile(np.cos(angle).astype(np.float32)),
        "sin": by_tile(np.sin(angle).astype(np.float32) * sign),
        "x": x.reshape(B * KT, P, C).transpose(1, 0, 2),
        "w_proj": by_half(a["L0_attn_w_proj"]),
        "WqT": by_half(a["L0_xattn_Wq"].T), "WkT": by_half(a["L0_xattn_Wk"].T),
        "WvT": by_half(a["L0_xattn_Wv"].T), "WoT": by_half(a["L0_xattn_Wo"].T),
        "b_proj": a["L0_attn_b_proj"].reshape(1, C), "bv": a["L0_xattn_bv"].reshape(1, C),
        "bo": a["L0_xattn_bo"].reshape(1, C),
        "bias_cols": np.stack([a["L0_xattn_bq"].reshape(2, P).T, a["L0_xattn_bk"].reshape(2, P).T], 1),
        "head_mask": (np.arange(P)[:, None] // D == np.arange(P // D)[None]).astype(np.float32),
        "half_mask": (np.arange(P)[:, None] // KC == np.arange(2 * D)[None] // D).astype(np.float32),
        "Wc": by_half(a["L0_ffn_Wc"].reshape(C, ES)),
        "bc": a["L0_ffn_bc"].reshape(ES, 1),
        "tie": np.linspace(0.0, 1e-6, GT, dtype=np.float32).reshape(1, GT),
        "W1": a["L0_ffn_W1"].reshape(ES, 2, P, F).transpose(2, 1, 0, 3),
        "b1": a["L0_ffn_b1"].reshape(QUADS, P).T,
        "W2T": a["L0_ffn_W2"].reshape(QUADS, 4, 2, HALF_C, F).transpose(1, 4, 2, 0, 3).reshape(P, 2, QUADS, HALF_C),
        "b2": a["L0_ffn_b2"].reshape(ES, 2, HALF_C),
        "ctxT": by_half(ctxT).reshape(P, 2, B, KC),
        "ctxT2": np.repeat(by_half(ctxT).reshape(P, 2, B, 1, KC), 2, axis=3),
    }
    nc = bacc.Bacc("TRN2", target_bir_lowering=False, num_devices=1)
    feed, handles = {}, {}
    for name, array in arrays.items():
        feed["in_" + name] = np.ascontiguousarray(array)
        handles[name] = nc.dram_tensor("in_" + name, array.shape, F32, kind="ExternalInput").ap()
    out = nc.dram_tensor("out_0", [P, B * KT, C], F32, kind="ExternalOutput").ap()
    program(nc, handles, out)
    r = run(nc, [feed], core_ids=[0])
    return np.ascontiguousarray(r.results[0]["out_0"].transpose(1, 0, 2)).reshape(B, N, C)
```

```python
from contextlib import ExitStack

import concourse.bass as bass
from concourse import mybir

F32 = mybir.dt.float32
BF16 = mybir.dt.bfloat16
I32 = mybir.dt.int32
ACT = mybir.ActivationFunctionType
ALU = mybir.AluOpType
AX = mybir.AxisListType

P = 128
B, N, C = 4, 1024, 256
H, D = 16, 16
KT = N // P
HG = 4
GPB = H // HG
GROUPS = B * GPB
VW = 32
SPLIT = 3
Q_PART = [0, 0, 0, 1, 1, 2]
K_PART = [0, 1, 2, 0, 1, 0]
STACK = D * len(Q_PART)
SHIFT = 2
AHEAD = 6
PAIRS = B * KT // 2
LOOP_PAIRS = PAIRS - AHEAD
RMS_EPS = 1e-6
LN_EPS = 1e-5
SAFE_LOGIT = 60.0
MAGIC = float(0x5F3759DF)


PROBS = 4
QW = N // HG


def wait(eng, sem, value):
    if not (isinstance(value, int) and value <= 0):
        eng.wait_ge(sem, value)


def newton_rsqrt(nc, link, y, t, hv, v):
    bits = y.bitcast(I32)
    nc.vector.tensor_scalar(bits, v.bitcast(I32), 1, None, ALU.logical_shift_right)
    link(nc.vector.tensor_scalar(hv, v, -0.5, None, ALU.mult))
    link(nc.vector.tensor_scalar(bits, bits, -1.0, MAGIC, ALU.mult, ALU.add))
    for step in range(3):
        link(nc.vector.tensor_tensor(t, y, y, ALU.mult))
        link(nc.vector.tensor_tensor(t, t, hv, ALU.mult))
        link(nc.vector.scalar_tensor_tensor(out=y, in0=t, scalar=1.5, in1=y, op0=ALU.add, op1=ALU.mult))


def attention_phases(nc, io, qk_parts, v_scratch, attn_scratch, shift_scratch):
    with ExitStack() as ctx:
        def sb(name, shape, dt):
            return ctx.enter_context(nc.sbuf_tensor(name, shape, dt))

        def psum(name, shape):
            return ctx.enter_context(nc.psum_tensor(name, shape, F32))

        wqkv = sb("wqkv", [P, 2, 3 * C], F32)
        ident = sb("ident", [P, P], F32)
        zeros = sb("zeros", [P, 8 * P], F32)
        cos = sb("cos", [P, B * KT, D], F32)
        sin = sb("sin", [P, B * KT, D], F32)
        scales = sb("scales", [P, 2, D], F32)
        rope_c = sb("rope_c", [P, B * KT, 2, D], F32)
        rope_s = sb("rope_s", [P, B * KT, 2, D], F32)
        xT = sb("xT", [P, 2, 2 * P], F32)
        raw = sb("raw", [P, 2, 2 * C], F32)
        sq = sb("sq", [P, 2, 2 * C], F32)
        ra = sb("ra", [P, 2, 2 * C], F32)
        rb = sb("rb", [P, 2, 2 * C], F32)
        ms, rstd, nt, nh = (sb(n, [P, 2 * 2 * H], F32) for n in ("ms", "rstd", "nt", "nh"))
        qn = sb("qn", [P, 2, 2 * C], F32)
        rest = sb("rest", [P, 4, 2, P], F32)
        parts = sb("parts", [P, SPLIT, 4, 2, P], BF16)
        vbuf = sb("vbuf", [P, 2, H, VW], F32)
        qst = sb("qst", [P, 2, HG, N], BF16)
        kst = sb("kst", [P, 2, HG, N], BF16)
        vst = sb("vst", [P, 2, KT, HG, VW], F32)
        prob = sb("prob", [P, PROBS, HG, N], F32)
        oT = sb("oT", [P, N], F32)
        rden = sb("rden", [P, 2, 4 * HG], F32)
        attn = sb("attn", [P, KT, HG, D], F32)
        flag = sb("flag", [1, 1], I32)
        bound = sb("bound", [1, 4], F32)
        rmax = sb("rmax", [P, HG * KT], F32)
        shift = sb("shift", [HG * KT, SHIFT, P], BF16)

        S = [psum(f"S{n}", [P, N]) for n in range(2)]
        O = psum("O", [P, N])
        X = [psum(f"X{n}", [P, 512]) for n in range(2)]

        def pe_qk(pe, x, bank):
            for c in range(2):
                mm = pe.matmul(bank[:, 0:2 * C], x(c), wqkv[:, c, 0:2 * C], start=(c == 0), stop=(c == 1))
            return mm

        def pe_v(pe, x, bank):
            for c in range(2):
                mm = pe.matmul(bank[:, 0:C], x(c), wqkv[:, c, 2 * C:3 * C], start=(c == 0), stop=(c == 1))
            return mm

        def x_tile(u):
            return lambda c: xT[:, c, u * P:(u + 1) * P]

        def pe_turn(pe, u, bank):
            for c in range(4):
                mm = pe.transpose(bank[:, c * P:(c + 1) * P], qn[:, u, c * P:(c + 1) * P], ident[:])
            return mm

        def rope_view(t):
            return t.rearrange("p u (a h d) -> p (u a) h d", a=2, d=D)

        ROPE_LINKS = 1 + 2 + 11

        def dve_products(dve, s, link, n, pair):
            def table(t, lo, hi):
                return t[:, bass.ds(pair * 2, 2), :, lo:hi].rearrange("p u a d -> p (u a) d")[:, :, None, :] \
                    .to_broadcast([P, 4, H, hi - lo])
            dve.wait_ge(s["qn_ready"], n + 1)
            dve.wait_ge(s["raw_ready"], n * 2 + 4)
            half = D // 2
            nc.vector.tensor_tensor(rope_view(ra[:]), rope_view(raw[:]), table(rope_c, 0, D), ALU.mult)
            nc.vector.tensor_tensor(rope_view(rb[:])[:, :, :, 0:half], rope_view(raw[:])[:, :, :, half:D],
                                    table(rope_s, 0, half), ALU.mult)
            link(nc.vector.tensor_tensor(rope_view(rb[:])[:, :, :, half:D], rope_view(raw[:])[:, :, :, 0:half],
                                         table(rope_s, half, D), ALU.mult))
            nc.vector.tensor_tensor(ra[:], ra[:], rb[:], ALU.add).then_inc(s["rotated"], 1)

        def dve_norm(dve, s, link, n):
            dve.wait_ge(s["sq_ready"], n + 1)
            link(nc.vector.tensor_reduce(ms[:], sq[:].rearrange("p u (h d) -> p (u h) d", d=D), AX.X, ALU.add))
            link(nc.vector.tensor_scalar(ms[:], ms[:], 1.0 / D, RMS_EPS, ALU.mult, ALU.add))
            newton_rsqrt(nc, link, rstd[:], nt[:], nh[:], ms[:])
            dve.wait_ge(s["rotated"], n + 2)
            nc.vector.tensor_tensor(qn[:].rearrange("p u (h d) -> p (u h) d", d=D),
                                    ra[:].rearrange("p u (h d) -> p (u h) d", d=D),
                                    rstd[:, :, None].to_broadcast([P, 4 * H, D]), ALU.mult).then_inc(s["qn_ready"], 1)

        def dve_rest(dve, s, n, u, bank, hi_sem, hi_count):
            dve.wait_ge(hi_sem, hi_count)
            if u == 0:
                dve.wait_ge(s["parts_ready"], n + 1)
            nc.vector.tensor_tensor(rest[:, :, u, :], bank[:].rearrange("p (c t) -> p c t", c=4),
                                    parts[:, 0, :, u, :], ALU.subtract).then_inc(s["t_taken"], 1)

        def pool_square(pool, s, n):
            pool.wait_ge(s["raw_ready"], n * 2 + 4)
            pool.wait_ge(s["qn_ready"], n + 1)
            nc.gpsimd.tensor_tensor(sq[:], raw[:], raw[:], ALU.mult).then_inc(s["sq_ready"], 1)

        def pool_parts(pool, s, n):
            def flat(t):
                return t.rearrange("p c u t -> p (c u t)")
            pool.wait_ge(s["t_taken"], n * 2 + 4)
            nc.gpsimd.tensor_tensor(flat(parts[:, 1]), flat(rest[:]), zeros[:], ALU.add).then_inc(s["mid_ready"], 1)
            pool.wait_ge(s["mid_ready"], n + 1)
            nc.gpsimd.tensor_tensor(flat(parts[:, 2]), flat(rest[:]), flat(parts[:, 1]),
                                    ALU.subtract).then_inc(s["parts_ready"], 1)

        def load_x(eng, s, pair):
            eng.dma_start(xT[:], io["xT"][:, :, bass.ds(pair * 2 * P, 2 * P)]).then_inc(s["x_loaded"], 16)

        def sp_store_v(sp, s, pair):
            sp.dma_start(v_scratch[bass.ds(pair, 1)].rearrange("o u p h w -> p (o u) (h w)"),
                         vbuf[:].rearrange("p u h w -> p u (h w)")).then_inc(s["v_written"], 16)

        def sp_store_parts(sp, s, b, quarter):
            for part in range(SPLIT):
                for a in range(2):
                    dst = qk_parts[part, a, bass.ds(b, 1), :, bass.ds(quarter * 2 * P, 2 * P)] \
                        .rearrange("o (c p) t -> p (o c) t", p=P)
                    src = parts[:, part, 2 * a:2 * a + 2].rearrange("p c u t -> p c (u t)")
                    sp.dma_start(dst, src).then_inc(s["parts_written"], 16)

        PARTS_WRITTEN = 16 * SPLIT * 2

        def projection_semaphores(stack, tag):
            names = ("x_loaded", "qk_ps", "v_ps", "t_ps", "raw_ready", "sq_ready", "v_ready", "hi_ready",
                     "rotated", "qn_ready", "t_taken", "mid_ready", "parts_ready", "v_written", "parts_written")
            return {n: stack.enter_context(nc.semaphore(f"{tag}_{n}")) for n in names}

        def sp_credits(sp, s):
            sp.sem_inc(s["v_written"], 16)
            sp.sem_inc(s["parts_written"], PARTS_WRITTEN)

        with ExitStack() as stage:
            s = projection_semaphores(stage, "a")
            const_loaded = stage.enter_context(nc.semaphore("const_loaded"))
            tables_loaded = stage.enter_context(nc.semaphore("tables_loaded"))
            table_step = stage.enter_context(nc.semaphore("table_step"))
            rope_step = stage.enter_context(nc.semaphore("a_rope_step"))
            zeros_set = stage.enter_context(nc.semaphore("zeros_set"))
            pad_set = stage.enter_context(nc.semaphore("pad_set"))
            block = stage.enter_context(nc.Block())

            def run_pairs(eng, body):
                with eng.Fori(0, AHEAD - 2) as it:
                    body(it, 2)
                body(AHEAD - 2, 1)
                body(AHEAD - 1, 0)

            @block.sync
            def _(sp):
                sp_credits(sp, s)
                load_x(sp, s, 0)
                sp.dma_start(wqkv[:], io["w_qkv"]).then_inc(const_loaded, 16)
                sp.dma_start(scales[:, 0, :], io["q_scale"].to_broadcast([P, D])).then_inc(tables_loaded, 16)
                sp.dma_start(scales[:, 1, :], io["k_scale"].to_broadcast([P, D])).then_inc(tables_loaded, 16)
                sp.dma_start(cos[:], io["cos"]).then_inc(tables_loaded, 16)
                sp.dma_start(sin[:], io["sin"]).then_inc(tables_loaded, 16)
                sp.dma_start(ident[:], io["ident"]).then_inc(const_loaded, 16)
                sp.wait_ge(s["v_ps"], 2)
                load_x(sp, s, 1)
                sp.wait_ge(s["v_ready"], 4)
                sp_store_v(sp, s, 0)

                def body(it, more):
                    if more:
                        sp.wait_ge(s["v_ready"], it * 2 + 6)
                        sp_store_v(sp, s, it + 1)
                    if more == 2:
                        load_x(sp, s, it + 2)
                    sp.wait_ge(s["parts_ready"], it + 2)
                    sp_store_parts(sp, s, it // 4, it % 4)

                run_pairs(sp, body)
                sp.wait_ge(s["v_written"], 16 * (AHEAD + 1))
                sp.wait_ge(s["parts_written"], PARTS_WRITTEN * (AHEAD + 1))

            @block.tensor
            def _(pe):
                def project(pair):
                    pe.wait_ge(s["x_loaded"], pair * 16 + 16)
                    for u in range(2):
                        pe.wait_ge(s["raw_ready"], pair * 2 + u + 1)
                        pe_qk(pe, x_tile(u), S[u][:, 0:512]).then_inc(s["qk_ps"], 1)
                        pe.wait_ge(s["v_ready"], pair * 2 + u + 1)
                        pe_v(pe, x_tile(u), S[u][:, 512:1024]).then_inc(s["v_ps"], 1)

                pe.wait_ge(const_loaded, 16 * 2)
                project(0)

                def body(it, more):
                    if more:
                        project(it + 1)
                    for u in range(2):
                        pe.wait_ge(s["qn_ready"], it + 2)
                        pe.wait_ge(s["t_taken"], it * 2 + u + 1)
                        pe_turn(pe, u, X[u]).then_inc(s["t_ps"], 1)

                run_pairs(pe, body)

            @block.scalar
            def _(act):
                act.sem_inc(s["raw_ready"], 2)
                act.sem_inc(s["v_ready"], 2)
                act.wait_ge(pad_set, 1)

                def evacuate(pair):
                    for u in range(2):
                        act.wait_ge(s["qk_ps"], pair * 2 + u + 1)
                        if u == 0:
                            act.wait_ge(s["rotated"], pair + 1)
                            wait(act, s["sq_ready"], pair)
                        nc.scalar.copy(raw[:, u, :], S[u][:, 0:512]).then_inc(s["raw_ready"], 1)
                        if u == 0:
                            act.wait_ge(s["v_written"], pair * 16 + 16)
                        act.wait_ge(s["v_ps"], pair * 2 + u + 1)
                        nc.scalar.copy(vbuf[:, u, :, 0:D],
                                       S[u][:, 512:512 + C].rearrange("p (h d) -> p h d", d=D)).then_inc(s["v_ready"], 1)

                evacuate(0)

                def body(it, more):
                    if more:
                        evacuate(it + 1)
                    for u in range(2):
                        act.wait_ge(s["t_ps"], it * 2 + u + 1)
                        if u == 0:
                            act.wait_ge(s["parts_written"], it * PARTS_WRITTEN + PARTS_WRITTEN)
                        nc.scalar.copy(parts[:, 0, :, u, :],
                                       X[u][:].rearrange("p (c t) -> p c t", c=4)).then_inc(s["hi_ready"], 1)

                run_pairs(act, body)

            @block.vector
            def _(dve):
                count = [0]

                def once(ins):
                    count[0] += 1
                    ins.then_inc(table_step, 1)
                    dve.wait_ge(table_step, count[0])

                nc.vector.memset(vbuf[:, :, :, D + 1:VW], 0.0)
                nc.vector.memset(vbuf[:, :, :, D:D + 1], 1.0).then_inc(pad_set, 1)
                dve.wait_ge(tables_loaded, 16 * 4)
                half = D // 2
                for a in range(2):
                    def scale(lo, hi):
                        return scales[:, a:a + 1, lo:hi].to_broadcast([P, B * KT, hi - lo])
                    nc.vector.tensor_tensor(rope_c[:, :, a, :], cos[:], scale(0, D), ALU.mult)
                    nc.vector.tensor_tensor(rope_s[:, :, a, 0:half], sin[:, :, 0:half], scale(half, D), ALU.mult)
                    once(nc.vector.tensor_tensor(rope_s[:, :, a, half:D], sin[:, :, half:D], scale(0, half), ALU.mult))
                once(nc.vector.tensor_reduce(bound[:, 0:2], scales[0:1], AX.X, ALU.max, apply_absolute_value=True))
                once(nc.vector.tensor_tensor(bound[:, 2:3], bound[:, 0:1], bound[:, 1:2], ALU.mult))
                once(nc.vector.tensor_scalar(flag[:], bound[:, 2:3], SAFE_LOGIT * D ** 0.5 / D, None, ALU.is_le))
                dve.sem_inc(s["qn_ready"], 1)
                dve.sem_inc(s["rotated"], 1)
                dve.sem_inc(s["t_taken"], 2)

                def linker(start):
                    links = [0]

                    def link(ins):
                        links[0] += 1
                        ins.then_inc(rope_step, 1)
                        dve.wait_ge(rope_step, start + links[0])
                    return link

                dve_products(dve, s, linker(0), 0, 0)

                def body(it, more):
                    dve_norm(dve, s, linker(it * ROPE_LINKS + 1), it)
                    if more:
                        dve_products(dve, s, linker((it + 1) * ROPE_LINKS), it + 1, it + 1)
                    for u in range(2):
                        dve_rest(dve, s, it, u, X[u], s["hi_ready"], it * 2 + u + 1)

                run_pairs(dve, body)

            @block.gpsimd
            def _(pool):
                pool.sem_inc(s["parts_ready"], 1)
                nc.gpsimd.memset(zeros[:], 0.0).then_inc(zeros_set, 1)
                pool.wait_ge(zeros_set, 1)
                nc.gpsimd.memset(kst[STACK:P, :, :, :], 1.0).then_inc(zeros_set, 1)
                pool.wait_ge(zeros_set, 2)
                nc.gpsimd.memset(qst[STACK:P, :, :, :], 0.0).then_inc(zeros_set, 1)
                pool.wait_ge(zeros_set, 3)
                pool_square(pool, s, 0)

                def body(it, more):
                    if more:
                        pool_square(pool, s, it + 1)
                    pool_parts(pool, s, it)

                run_pairs(pool, body)

        with ExitStack() as stage:
            s = projection_semaphores(stage, "m")

            def sem(name):
                return stage.enter_context(nc.semaphore(name))

            flag_read = sem("flag_read")
            rope_step = sem("m_rope_step")
            stacks_loaded = [sem(f"stacks_loaded{n}") for n in range(2)]
            qk_done, exp_done, av_done = sem("qk_done"), sem("exp_done"), sem("av_done")
            o_copied, at_ps, at_taken = sem("o_copied"), sem("at_ps"), sem("at_taken")
            rden_ready, attn_written = sem("rden_ready"), sem("attn_written")
            row_scores, row_taken, rows_turned = sem("row_scores"), sem("row_taken"), sem("rows_turned")
            shift_ready, shift_loaded = sem("shift_ready"), sem("shift_loaded")
            shift_high, shift_stored = sem("shift_high"), sem("shift_stored")
            block = stage.enter_context(nc.Block())
            LOADS = 16 * (2 * len(Q_PART) + 1)
            TILES = HG * KT

            WITH, WITHOUT = LOOP_PAIRS // 2, GROUPS // 2 - 1 - LOOP_PAIRS // 2

            def run_groups(eng, body):
                with eng.Fori(0, WITH) as jj:
                    for par in range(2):
                        body(jj * 2 + par, par, True, False)
                with eng.Fori(WITH, WITH + WITHOUT) as jj:
                    for par in range(2):
                        body(jj * 2 + par, par, False, False)
                for par in range(2):
                    body(GROUPS - 2 + par, par, False, par == 1)

            @block.sync
            def _(sp):
                def load_stacks(i, par):
                    b, g = i // GPB, i % GPB
                    for a, (dst, order) in enumerate(((qst, Q_PART), (kst, K_PART))):
                        for r, part in enumerate(order):
                            src = qk_parts[part, a, bass.ds(b, 1), bass.ds(g * HG * D, HG * D), :] \
                                .rearrange("o (h d) t -> d (o h) t", d=D)
                            sp.dma_start(dst[r * D:(r + 1) * D, par], src).then_inc(stacks_loaded[par], 16)
                    src = v_scratch[bass.ds(b * (KT // 2), KT // 2), :, :, bass.ds(g * HG, HG), :] \
                        .rearrange("q u p h w -> p (q u) (h w)")
                    sp.dma_start(vst[:, par].rearrange("p k h w -> p k (h w)"), src).then_inc(stacks_loaded[par], 16)

                sp_credits(sp, s)
                sp.sem_inc(attn_written, 16)
                general = sp.value_load(flag[:], min_val=0, max_val=1)

                def load_shift(i, par):
                    with sp.If(general < 1):
                        sp.wait_ge(shift_ready, i + 1)
                        sp.dma_start(shift_scratch.rearrange("r (n q) -> n r q", q=P), shift[:]).then_inc(shift_stored, 16)
                        sp.wait_ge(shift_stored, (i + 1) * 16)
                        sp.dma_start(qst[STACK:STACK + SHIFT, par].rearrange("r h t -> r (h t)"),
                                     shift_scratch).then_inc(shift_loaded, 16)

                load_stacks(0, 0)
                load_shift(0, 0)

                def body(i, par, project, last):
                    if not last:
                        groups_before = i * (2 * KT) + 2 * KT
                        sp.wait_ge(av_done, groups_before)
                        if project:
                            sp.wait_ge(s["v_written"], groups_before)
                            sp.wait_ge(s["parts_written"], i * PARTS_WRITTEN + PARTS_WRITTEN)
                        elif not isinstance(i, int):
                            sp.wait_ge(s["v_written"], 16 * (LOOP_PAIRS + 1))
                            sp.wait_ge(s["parts_written"], PARTS_WRITTEN * (LOOP_PAIRS + 1))
                        load_stacks(i + 1, 1 - par)
                    if project:
                        sp.wait_ge(s["v_ready"], i * 2 + 4)
                        sp_store_v(sp, s, i + AHEAD)
                        sp.wait_ge(s["parts_ready"], i + 2)
                        sp_store_parts(sp, s, (i + AHEAD) // 4, (i + AHEAD) % 4)
                    if not last:
                        load_shift(i + 1, 1 - par)
                    sp.wait_ge(at_taken, i * 2 + 4)
                    sp.dma_start(attn_scratch[bass.ds(i, 1)].rearrange("o t p c -> p (o t) c"),
                                 attn[:].rearrange("p t h d -> p t (h d)")).then_inc(attn_written, 16)

                run_groups(sp, body)
                sp.wait_ge(attn_written, 16 * (GROUPS + 1))

            @block.tensor
            def _(pe):
                pe.sem_inc(s["v_ps"], 1)
                pe.sem_inc(av_done, 2 * KT)
                general = pe.value_load(flag[:], min_val=0, max_val=1)

                def scores(i, par, kt, h):
                    n = kt * HG + h
                    pe.wait_ge(exp_done, i * TILES + n + 1)
                    for half in range(2):
                        mm = pe.matmul(S[h % 2][:, half * 512:(half + 1) * 512],
                                       kst[0:STACK + SHIFT, par, h, kt * P:(kt + 1) * P],
                                       qst[0:STACK + SHIFT, par, h, half * 512:(half + 1) * 512],
                                       start=True, stop=True)
                    mm.then_inc(qk_done, 1)

                def values(i, par, kt, quarter, width=1):
                    pe.wait_ge(exp_done, i * TILES + kt * HG + HG + 2)
                    if kt == 0 and quarter % 2 == 0:
                        pe.wait_ge(o_copied, i * 2 + quarter // 2 + 1)
                    q = slice(quarter * QW, (quarter + width) * QW)
                    ends_bank = (quarter + width) % 2 == 0
                    for h in range(HG):
                        mm = pe.matmul(O[h * VW:(h + 1) * VW, q], vst[:, par, kt, h, :], prob[:, kt % PROBS, h, q],
                                       start=(kt == 0 and quarter % 2 == 0), stop=(kt == KT - 1 and ends_bank))
                    if ends_bank:
                        mm.then_inc(av_done, 1)

                def turn_output(i, half):
                    pe.wait_ge(o_copied, i * 2 + half + 3)
                    pe.wait_ge(at_taken, i * 2 + half + 1)
                    for t in range(4):
                        mm = pe.transpose(X[half][:, t * P:(t + 1) * P],
                                          oT[:, half * 512 + t * P:half * 512 + (t + 1) * P], ident[:])
                    mm.then_inc(at_ps, 1)

                def projection(i, kt, h):
                    if (kt, h) == (2, 2):
                        pe.wait_ge(s["x_loaded"], i * 16 + 16)
                        pe.wait_ge(at_taken, i * 2 + 1)
                        pe_qk(pe, x_tile(0), X[0]).then_inc(s["qk_ps"], 1)
                    elif (kt, h) == (3, 0):
                        pe.wait_ge(at_taken, i * 2 + 2)
                        pe_v(pe, x_tile(0), X[1]).then_inc(s["v_ps"], 1)
                    elif (kt, h) == (3, 2):
                        pe.wait_ge(s["raw_ready"], i * 2 + 3)
                        pe_qk(pe, x_tile(1), X[0]).then_inc(s["qk_ps"], 1)
                    elif (kt, h) == (4, 1):
                        pe.wait_ge(s["v_ready"], i * 2 + 3)
                        pe_v(pe, x_tile(1), X[1]).then_inc(s["v_ps"], 1)
                    elif (kt, h) in ((7, 0), (7, 2)):
                        u = h // 2
                        pe.wait_ge(s["qn_ready"], i + 2)
                        pe.wait_ge(s["v_ready"] if u else s["raw_ready"], i * 2 + 4)
                        pe_turn(pe, u, X[u]).then_inc(s["t_ps"], 1)

                def row_maxima(i, par):
                    with pe.If(general < 1):
                        pe.wait_ge(stacks_loaded[par], (i // 2) * LOADS + LOADS)
                        pe.wait_ge(exp_done, i * TILES + 2)
                        for n in range(TILES):
                            h, t = n // KT, n % KT
                            pe.wait_ge(row_taken, i * TILES + n + 1)
                            for half in range(2):
                                mm = pe.matmul(S[n % 2][:, half * 512:(half + 1) * 512],
                                               qst[0:STACK, par, h, t * P:(t + 1) * P],
                                               kst[0:STACK, par, h, half * 512:(half + 1) * 512],
                                               start=True, stop=True)
                            mm.then_inc(row_scores, 1)
                        pe.wait_ge(row_taken, (i + 1) * TILES + 2)
                        pe.transpose(S[0][0:TILES, 0:P], rmax[:], ident[:]).then_inc(rows_turned, 1)
                        pe.wait_ge(shift_loaded, (i + 1) * 16)

                def first_tiles(i, par, previous, projected=False):
                    row_maxima(i, par)
                    pe.wait_ge(stacks_loaded[par], (i // 2) * LOADS + LOADS)
                    if previous is None:
                        for h in range(HG):
                            scores(i, par, 0, h)
                        for h in range(HG):
                            scores(i, par, 1, h)
                            if h > 0:
                                values(i, par, 0, h - 1)
                        return
                    last = (previous, 1 - par, KT - 1)
                    for h in range(HG):
                        scores(i, par, 0, h)
                        if h > 0:
                            values(*last, h - 1)
                        elif not projected:
                            values(previous, 1 - par, KT - 2, HG - 1)
                    scores(i, par, 1, 0)
                    values(*last, HG - 1)
                    turn_output(previous, 0)
                    scores(i, par, 1, 1)
                    values(i, par, 0, 0)
                    scores(i, par, 1, 2)
                    values(i, par, 0, 1)
                    turn_output(previous, 1)
                    scores(i, par, 1, 3)
                    values(i, par, 0, 2)

                first_tiles(0, 0, None)

                def body(i, par, project, last):
                    for kt in range(2, KT):
                        for h in range(HG):
                            scores(i, par, kt, h)
                            if h == 0 and (kt == 2 or not project):
                                values(i, par, kt - 2, HG - 1)
                            elif project and h % 2 == 1:
                                values(i, par, kt - 1, h - 1, 2)
                            elif not project and h > 0:
                                values(i, par, kt - 1, h - 1)
                            if project:
                                projection(i, kt, h)
                    if last:
                        values(i, par, KT - 2, HG - 1)
                        for quarter in range(HG):
                            values(i, par, KT - 1, quarter)
                        for half in range(2):
                            turn_output(i, half)
                    else:
                        first_tiles(i + 1, 1 - par, i, project)

                run_groups(pe, body)

            @block.scalar
            def _(act):
                act.sem_inc(exp_done, 2)

                def exps(i, par, kt):
                    for h in range(HG):
                        n = kt * HG + h
                        act.wait_ge(qk_done, i * TILES + n + 1)
                        if h == 0:
                            act.wait_ge(av_done, (i * KT + kt - PROBS) * 2 + 2 * KT + 2)
                        nc.scalar.activation(prob[:, kt % PROBS, h, :], S[h % 2][:], ACT.Exp,
                                             scale=float(D) ** -0.5).then_inc(exp_done, 1)

                for kt in range(2):
                    exps(0, 0, kt)

                def body(i, par, project, last):
                    for kt in range(2, KT):
                        exps(i, par, kt)
                    if not last:
                        for kt in range(2):
                            exps(i + 1, 1 - par, kt)

                run_groups(act, body)

            @block.vector
            def _(dve):
                dve.sem_inc(s["raw_ready"], 2)
                dve.sem_inc(s["v_ready"], 2)
                dve.sem_inc(s["qn_ready"], 1)
                dve.sem_inc(s["rotated"], 1)
                dve.sem_inc(s["t_taken"], 2)
                dve.sem_inc(o_copied, 2)
                dve.sem_inc(at_taken, 2)
                dve.sem_inc(row_taken, 2)
                general = dve.value_load(flag[:], min_val=0, max_val=1)

                def raw_copy(i, u):
                    dve.wait_ge(s["qk_ps"], i * 2 + u + 1)
                    nc.vector.tensor_copy(raw[:, u, :], X[0][:]).then_inc(s["raw_ready"], 1)

                def v_copy(i, u):
                    if u == 0:
                        dve.wait_ge(s["v_written"], i * 16 + 16)
                    dve.wait_ge(s["v_ps"], i * 2 + u + 2)
                    nc.vector.tensor_copy(vbuf[:, u, :, 0:D],
                                          X[1][:, 0:C].rearrange("p (h d) -> p h d", d=D)).then_inc(s["v_ready"], 1)

                def first_part(i, u):
                    dve.wait_ge(s["t_ps"], i * 2 + u + 1)
                    if u == 0:
                        dve.wait_ge(s["parts_written"], i * PARTS_WRITTEN + PARTS_WRITTEN)
                    nc.vector.tensor_copy(parts[:, 0, :, u, :],
                                          X[u][:].rearrange("p (c t) -> p c t", c=4)).then_inc(s["hi_ready"], 1)

                def row_maxima(i):
                    with dve.If(general < 1):
                        for n in range(TILES):
                            dve.wait_ge(row_scores, i * TILES + n + 1)
                            nc.vector.tensor_reduce(rmax[:, n:n + 1], S[n % 2][:], AX.X, ALU.max)\
                                .then_inc(row_taken, 1)
                        dve.wait_ge(rows_turned, i + 1)
                        nc.vector.tensor_scalar(shift[:, 0, :], S[0][0:TILES, 0:P], -1.0, None, ALU.mult)\
                            .then_inc(shift_high, 1)
                        dve.wait_ge(shift_high, i + 1)
                        nc.vector.scalar_tensor_tensor(out=shift[:, 1, :], in0=S[0][0:TILES, 0:P], scalar=-1.0,
                                                       in1=shift[:, 0, :], op0=ALU.mult,
                                                       op1=ALU.subtract).then_inc(shift_ready, 1)

                row_maxima(0)

                def body(i, par, project, last):
                    if project:
                        links = [0]

                        def link(ins):
                            links[0] += 1
                            ins.then_inc(rope_step, 1)
                            dve.wait_ge(rope_step, i * ROPE_LINKS + links[0])

                        for u in range(2):
                            raw_copy(i, u)
                            v_copy(i, u)
                        dve_products(dve, s, link, i, i + AHEAD)
                        dve_norm(dve, s, link, i)
                        for u in range(2):
                            first_part(i, u)
                            dve_rest(dve, s, i, u, X[u], s["hi_ready"], i * 2 + u + 1)
                        assert links[0] == ROPE_LINKS
                    if not last:
                        row_maxima(i + 1)
                    for half in range(2):
                        dve.wait_ge(av_done, (i * KT + KT - 1) * 2 + 2 * KT + half + 1)
                        nc.vector.tensor_copy(oT[:, half * 512:(half + 1) * 512],
                                              O[:, half * 512:(half + 1) * 512]).then_inc(o_copied, 1)
                    for half in range(2):
                        dve.wait_ge(at_ps, i * 2 + half + 1)
                        x = X[half][:].rearrange("p (c w) -> p c w", w=VW)
                        nc.vector.reciprocal(rden[:, half, :], x[:, :, D]).then_inc(rden_ready, 1)
                        dve.wait_ge(rden_ready, i * 2 + half + 1)
                        if half == 0:
                            dve.wait_ge(attn_written, i * 16 + 16)
                        nc.vector.tensor_tensor(attn[:, half * 4:(half + 1) * 4].rearrange("p t h d -> p (t h) d"),
                                                x[:, :, 0:D],
                                                rden[:, half, :, None].to_broadcast([P, 4 * HG, D]),
                                                ALU.mult).then_inc(at_taken, 1)

                run_groups(dve, body)

            @block.gpsimd
            def _(pool):
                pool.sem_inc(s["parts_ready"], 1)
                with pool.Fori(0, LOOP_PAIRS) as it:
                    pool.wait_ge(s["v_ps"], it * 2 + 1)
                    load_x(pool, s, it + AHEAD)
                    pool_square(pool, s, it)
                    pool_parts(pool, s, it)


CHUNK = 4
CW = CHUNK * P
CHUNKS = B * N // CW
KC = 64
PAIRH = H // 2


NORM_LINKS = 4 + 11


def norm_factors(nc, link, tiles, y, stats, mv, var, rsqrt, minus):
    for t in range(tiles):
        ins = nc.vector.bn_stats(stats[:, t, :], y(t))
    link(ins)
    mean, apart = mv[:, :, 0], mv[:, :, 1]
    nc.vector.tensor_tensor(mean, stats[:, :, 1], stats[:, :, 4], ALU.add)
    nc.vector.tensor_tensor(apart, stats[:, :, 1], stats[:, :, 4], ALU.subtract)
    link(nc.vector.tensor_tensor(var, stats[:, :, 2], stats[:, :, 5], ALU.add))
    nc.vector.tensor_tensor(apart, apart, apart, ALU.mult)
    link(nc.vector.tensor_scalar(var, var, 1.0 / C, LN_EPS, ALU.mult, ALU.add))
    link(nc.vector.scalar_tensor_tensor(out=var, in0=apart, scalar=0.25, in1=var, op0=ALU.mult, op1=ALU.add))
    newton_rsqrt(nc, link, *rsqrt, var)
    return nc.vector.scalar_tensor_tensor(out=minus, in0=mean, scalar=-0.5, in1=rsqrt[0], op0=ALU.mult, op1=ALU.mult)


def cross_attention_phase(nc, io, attn_scratch, x_all, w1):
    with ExitStack() as ctx:
        def sb(name, shape, dt=F32):
            return ctx.enter_context(nc.sbuf_tensor(name, shape, dt))

        def psum(name, shape):
            return ctx.enter_context(nc.psum_tensor(name, shape, F32))

        def sem(name):
            return ctx.enter_context(nc.semaphore(name))

        ident = sb("ident2", [P, P])
        wproj, wq, wk = sb("wproj", [P, 2, C]), sb("wq", [P, 2, C]), sb("wk", [P, 2, C])
        wv, wo = sb("wv", [P, 2, C]), sb("wo", [P, 2, C])
        rows = {n: sb("row_" + n, [P, C]) for n in ("b_proj", "bv", "bo")}
        cols = sb("bias_cols", [P, 2, 2])
        head_mask = sb("head_mask", [P, P // D])
        half_mask = sb("half_mask", [P, 2 * D])
        ctxT = sb("ctxT", [P, 2, B, KC])
        ctxT2 = sb("ctxT2", [P, 2, B, 2, KC])
        kT = sb("kT", [P, 2, B, KC])
        kbd = sb("kbd", [P, B, 2, P // D, KC])
        vrow = sb("vrow", [P, B, C])
        vbd_all = sb("vbd_all", [P, B, PAIRH, 2 * D])
        vbd = sb("vbd", [P, PAIRH, 2 * D])

        at = sb("at", [P, CHUNK, C])
        aT = sb("aT", [P, 2, CW])
        y1 = sb("y1", [P, CHUNK, C])
        x1 = sb("x1", [P, CHUNK, C])
        x1T = sb("x1T", [P, 2, CW])
        qT = sb("qT", [P, 2, CW])
        mx = sb("mx", [P, 2, H])
        z = sb("z", [P, 2, H * KC])
        pr = sb("pr", [P, 2, H * KC])
        pT = sb("pT", [P, PAIRH, CW])
        total = sb("total", [P, 2, H])
        rden = sb("rden2", [P, 2, H])
        pn = sb("pn", [P, 2, H * KC])
        oT = sb("oT2", [P, 2, CW])
        y2 = sb("y2", [P, CHUNK, C])
        stats = sb("stats", [P, 2, CHUNK, 6])
        mv = sb("mv", [P, 2, CHUNK, 2])
        var, ln_t, ln_h, ln_r, ln_m = (sb(n, [P, 2, CHUNK]) for n in ("var", "ln_t", "ln_h", "ln_r", "ln_m"))

        W = [psum(f"W{n}", [P, 2 * 512]) for n in range(2)]
        SS = [psum(f"SS{n}", [P, 2 * 512]) for n in range(2)]

        context_loaded, weights_loaded = sem("context_loaded"), sem("weights_loaded")
        x_first_in, x_rest_in, at_loaded = sem("x_first_in"), sem("x_rest_in"), sem("at_loaded")
        full = {j: sem("full_" + j) for j in ("prep", "x1T", "V", "aT", "q", "proj", "O", "pT", "S")}
        taken = {j: sem("taken_" + j) for j in ("prep", "x1T", "V", "aT", "q", "proj", "O", "pT")}
        z_ready, exp_done, x1_ready = sem("z_ready"), sem("exp_done2"), sem("x1_ready")
        proj_bias_added, out_bias_added, dve_step = sem("proj_bias_added"), sem("out_bias_added"), sem("dve_step2")
        factors, x2_ready, k_ready = sem("factors"), sem("x2_ready"), sem("k_ready")
        total_ready, rden_ready, normalised = sem("total_ready"), sem("rden_ready2"), sem("normalised")
        vbd_loaded = sem("vbd_loaded")
        max_ready, w1_loaded = sem("max_ready"), sem("w1_loaded")

        def run_chunks(eng, body):
            body(-2, True, False, False, False)
            body(-1, True, True, False, False)
            body(0, True, True, True, False)
            with eng.Fori(1, CHUNKS - 2) as c:
                body(c, True, True, True, True)
            body(CHUNKS - 2, False, True, True, True)
            body(CHUNKS - 1, False, False, True, True)
            body(CHUNKS, False, False, False, True)

        PREP_DVE = 2 + B

        block = ctx.enter_context(nc.Block())

        @block.sync
        def _(sp):
            def load_at(c):
                for t in range(CHUNK):
                    b, half = c // 2, c % 2
                    src = attn_scratch[bass.ds(b * GPB, GPB), bass.ds(half * CHUNK + t, 1)] \
                        .rearrange("g o p c -> p (g o) c")
                    sp.dma_start(at[:, t, :].rearrange("p (g c) -> p g c", g=GPB), src).then_inc(at_loaded, 16)

            for dst, src in ((ctxT[:], io["ctxT"]), (wk[:], io["WkT"]), (ctxT2[:], io["ctxT2"]), (wv[:], io["WvT"]),
                             (cols[:], io["bias_cols"]), (rows["bv"][:], io["bv"].to_broadcast([P, C])),
                             (head_mask[:], io["head_mask"]), (half_mask[:], io["half_mask"]),
                             (ident[:], io["ident"])):
                sp.dma_start(dst, src).then_inc(context_loaded, 16)
            load_at(0)
            for dst, src in ((wproj[:], io["w_proj"]), (rows["b_proj"][:], io["b_proj"].to_broadcast([P, C])),
                             (wq[:], io["WqT"]), (rows["bo"][:], io["bo"].to_broadcast([P, C])),
                             (wo[:], io["WoT"])):
                sp.dma_start(dst, src).then_inc(weights_loaded, 16)
            sp.dma_start(x_all[:, 0:CHUNK], io["x"][:, 0:CHUNK]).then_inc(x_first_in, 16)
            sp.dma_start(x_all[:, CHUNK:], io["x"][:, CHUNK:]).then_inc(x_rest_in, 16)
            sp.dma_start(w1[:].rearrange("p (c n) -> p c n", c=2), io["W1"].rearrange("p c e f -> p c (e f)")) \
                .then_inc(w1_loaded, 16)

            def load_vbd(k):
                wait(sp, full["V"], k)
                sp.dma_start(vbd[:], vbd_all[:, bass.ds(k // 2, 1)].rearrange("p o h d -> p (o h) d")) \
                    .then_inc(vbd_loaded, 16)

            sp.wait_ge(taken["prep"], PREP_DVE)
            load_vbd(0)
            for k in range(1, 4):
                sp.wait_ge(full["aT"], k)
                load_at(k)
            with sp.Fori(1, CHUNKS - 3) as k:
                load_vbd(k)
                sp.wait_ge(full["aT"], k + 3)
                load_at(k + 3)
            for k in range(CHUNKS - 3, CHUNKS):
                load_vbd(k)
            sp.wait_ge(w1_loaded, 16)

        @block.tensor
        def _(pe):
            pe.wait_ge(context_loaded, 16 * 9)
            for m in range(2):
                for ci in range(2):
                    mm = pe.matmul(W[m][:, 0:B * KC], wk[:, ci, m * P:(m + 1) * P],
                                   ctxT[:, ci].rearrange("p b k -> p (b k)"), start=(ci == 0), stop=(ci == 1))
                mm.then_inc(full["prep"], 1)
            for b in range(B):
                pe.wait_ge(taken["prep"], b + 1)
                for ci in range(2):
                    mm = pe.matmul(W[b % 2][:, 0:C], ctxT2[:, ci, b].rearrange("p j k -> p (j k)"), wv[:, ci, :],
                                   start=(ci == 0), stop=(ci == 1))
                mm.then_inc(full["prep"], 1)
            pe.wait_ge(taken["prep"], PREP_DVE)

            def turn(dst, src):
                for ci in range(2):
                    for t in range(CHUNK):
                        mm = pe.transpose(dst[:, ci * CW + t * P:ci * CW + (t + 1) * P],
                                          src[:, t, ci * P:(ci + 1) * P], ident[:])
                return mm

            def scores(c, t):
                wait(pe, z_ready, c * CHUNK + t - 1)
                for g in range(2):
                    mm = pe.matmul(SS[t % 2][:, g * 512:(g + 1) * 512], qT[:, g, t * P:(t + 1) * P],
                                   kbd[:, bass.ds(c // 2, 1), g].rearrange("p o h k -> p (o h k)"),
                                   start=True, stop=True)
                mm.then_inc(full["S"], 1)

            def turn_probs(c, t):
                pe.wait_ge(normalised, c * CHUNK + t + 1)
                for h in range(PAIRH):
                    mm = pe.transpose(W[t % 2][:, h * P:(h + 1) * P], pn[:, t % 2, h * P:(h + 1) * P], ident[:])
                mm.then_inc(full["pT"], 1)

            def by_tokens(bank, lhs, weights):
                for t in range(CHUNK):
                    for ci in range(2):
                        mm = pe.matmul(bank[:, t * C:(t + 1) * C], lhs[:, ci, t * P:(t + 1) * P], weights[:, ci, :],
                                       start=(ci == 0), stop=(ci == 1))
                return mm

            def body(c, a, b, m, l):
                if m:
                    if isinstance(c, int) and c == 0:
                        pe.wait_ge(k_ready, 1)
                    pe.wait_ge(taken["q"], c + 1)
                    scores(c, 0)
                    scores(c, 1)
                if l:
                    pe.wait_ge(taken["pT"], c * CHUNK)
                    pe.wait_ge(vbd_loaded, c * 16)
                    for g in range(2):
                        for j in range(4):
                            mm = pe.matmul(W[1][32 * j:32 * j + 32, g * CW:(g + 1) * CW],
                                           vbd[:, 4 * g + j, :], pT[:, 4 * g + j, :], start=True, stop=True)
                    mm.then_inc(full["V"], 1)
                if b:
                    pe.wait_ge(x1_ready, c + 2)
                    if not m:
                        pe.wait_ge(taken["proj"], 1)
                    turn(W[0], x1).then_inc(full["x1T"], 1)
                if a:
                    pe.wait_ge(at_loaded, (c + 3) * 16 * CHUNK)
                    wait(pe, taken["aT"], c + 2)
                    if l:
                        pe.wait_ge(taken["V"], c)
                    turn(W[1], at).then_inc(full["aT"], 1)
                if m:
                    scores(c, 2)
                    scores(c, 3)
                    if b:
                        pe.wait_ge(taken["x1T"], c + 2)
                    turn_probs(c, 0)
                if l:
                    pe.wait_ge(taken["V"], c)
                    if a:
                        pe.wait_ge(taken["aT"], c + 3)
                    by_tokens(W[1], oT, wo).then_inc(full["O"], 1)
                if a:
                    if isinstance(c, int) and c == -2:
                        pe.wait_ge(weights_loaded, 16 * 5)
                    pe.wait_ge(taken["aT"], c + 3)
                    if m:
                        pe.wait_ge(taken["pT"], c * CHUNK + 1)
                    elif b:
                        pe.wait_ge(taken["x1T"], c + 2)
                    by_tokens(W[0], aT, wproj).then_inc(full["proj"], 1)
                if m:
                    if l:
                        pe.wait_ge(taken["O"], c)
                    turn_probs(c, 1)
                    if a:
                        pe.wait_ge(taken["proj"], c + 3)
                    else:
                        pe.wait_ge(taken["pT"], c * CHUNK + 1)
                    turn_probs(c, 2)
                if b:
                    pe.wait_ge(taken["x1T"], c + 2)
                    if m:
                        pe.wait_ge(taken["pT"], c * CHUNK + 3)
                    else:
                        pe.wait_ge(taken["proj"], c + 3)
                    for half in range(2):
                        for ci in range(2):
                            mm = pe.matmul(W[0][:, half * CW:(half + 1) * CW], wq[:, ci, half * P:(half + 1) * P],
                                           x1T[:, ci, :], start=(ci == 0), stop=(ci == 1))
                    mm.then_inc(full["q"], 1)
                if m:
                    pe.wait_ge(taken["pT"], c * CHUNK + 2)
                    turn_probs(c, 3)

            run_chunks(pe, body)

        @block.scalar
        def _(act):
            act.wait_ge(context_loaded, 16 * 9)

            def expo(c, t):
                act.wait_ge(z_ready, c * CHUNK + t + 1)
                wait(act, normalised, c * CHUNK + t - 1)
                nc.scalar.activation(pr[:, t % 2, :], z[:, t % 2, :], ACT.Exp, scale=float(D) ** -0.5) \
                    .then_inc(exp_done, 1)

            def probs_out(c, t):
                act.wait_ge(full["pT"], c * CHUNK + t + 1)
                if t == 0:
                    wait(act, full["V"], c)
                nc.scalar.copy(pT[:, :, t * P:(t + 1) * P], W[t % 2][:].rearrange("p (h q) -> p h q", q=P)) \
                    .then_inc(taken["pT"], 1)

            def scaled(which, t, dst, src):
                return nc.scalar.activation(dst, src[:, t, :], ACT.Identity, scale=ln_r[:, which, t:t + 1],
                                            bias=ln_m[:, which, t:t + 1])

            def body(c, a, b, m, l):
                if m:
                    expo(c, 0)
                if l:
                    act.wait_ge(full["V"], c)
                    wait(act, full["O"], c - 1)
                    nc.scalar.copy(oT[:].rearrange("p c t -> p (c t)"), W[1][:]).then_inc(taken["V"], 1)
                if b:
                    act.wait_ge(full["x1T"], c + 2)
                    wait(act, full["q"], c + 1)
                    nc.scalar.copy(x1T[:].rearrange("p c t -> p (c t)"), W[0][:]).then_inc(taken["x1T"], 1)
                if m:
                    expo(c, 1)
                if a:
                    act.wait_ge(full["aT"], c + 3)
                    wait(act, full["proj"], c + 2)
                    nc.scalar.copy(aT[:].rearrange("p c t -> p (c t)"), W[1][:]).then_inc(taken["aT"], 1)
                if m:
                    expo(c, 2)
                    probs_out(c, 0)
                    expo(c, 3)
                    probs_out(c, 1)
                    probs_out(c, 2)
                if b:
                    act.wait_ge(full["q"], c + 2)
                    if m:
                        act.wait_ge(full["S"], (c + 1) * CHUNK)
                    for half in range(2):
                        ins = nc.scalar.activation(qT[:, half, :], W[0][:, half * CW:(half + 1) * CW], ACT.Identity,
                                                   bias=cols[:, 0, half:half + 1])
                    ins.then_inc(taken["q"], 1)
                if m:
                    probs_out(c, 3)
                act.wait_ge(factors, c + 3)
                if a:
                    wait(act, out_bias_added, c + 2)
                    for t in range(CHUNK):
                        ins = scaled(0, t, x1[:, t, :], y1)
                    ins.then_inc(x1_ready, 1)
                if l:
                    for t in range(CHUNK):
                        ins = scaled(1, t, x_all[:, bass.ds((c - 1) * CHUNK + t, 1), :].rearrange("p o c -> p (o c)"), y2)
                    ins.then_inc(x2_ready, 1)

            run_chunks(act, body)

        @block.vector
        def _(dve):
            dve.wait_ge(context_loaded, 16 * 9)
            for m in range(2):
                dve.wait_ge(full["prep"], m + 1)
                nc.vector.tensor_scalar(kT[:, m].rearrange("p b k -> p (b k)"), W[m][:, 0:B * KC],
                                        cols[:, 1, m:m + 1], None, ALU.add).then_inc(taken["prep"], 1)
            for b in range(B):
                dve.wait_ge(full["prep"], 3 + b)
                nc.vector.tensor_tensor(vrow[:, b], W[b % 2][:, 0:C], rows["bv"][:], ALU.add) \
                    .then_inc(dve_step, 1)
                dve.wait_ge(dve_step, b + 1)
                nc.vector.tensor_tensor(vbd_all[:, b], vrow[:, b].rearrange("p (h d) -> p h d", d=2 * D),
                                        half_mask[:, None, :].to_broadcast([P, PAIRH, 2 * D]), ALU.mult) \
                    .then_inc(taken["prep"], 1)
            for b in range(B):
                for m in range(2):
                    ins = nc.vector.tensor_tensor(kbd[:, b, m],
                                                  kT[:, m, b, None, :].to_broadcast([P, P // D, KC]),
                                                  head_mask[:, :, None].to_broadcast([P, P // D, KC]), ALU.mult)
            ins.then_inc(k_ready, 1)

            def norm(first, last, start):
                n = [0]

                def link(ins):
                    n[0] += 1
                    ins.then_inc(dve_step, 1)
                    dve.wait_ge(dve_step, start + n[0])

                def both(t):
                    return t[:, first:last + 1].rearrange("p w t -> p (w t)")

                norm_factors(nc, link, (last - first + 1) * CHUNK,
                             lambda t: (y1, y2)[first + t // CHUNK][:, t % CHUNK, :],
                             stats[:, first:last + 1].rearrange("p w t s -> p (w t) s"),
                             mv[:, first:last + 1].rearrange("p w t s -> p (w t) s"), both(var),
                             (both(ln_r), both(ln_t), both(ln_h)), both(ln_m)).then_inc(factors, 1)
                assert n[0] == NORM_LINKS

            def sums(c, t):
                dve.wait_ge(exp_done, c * CHUNK + t + 1)
                nc.vector.tensor_reduce(total[:, t % 2, :], pr[:, t % 2, :].rearrange("p (h k) -> p h k", k=KC),
                                        AX.X, ALU.add).then_inc(total_ready, 1)
                dve.wait_ge(total_ready, c * CHUNK + t + 1)
                wait(dve, normalised, c * CHUNK + t - 1)
                nc.vector.reciprocal(rden[:, t % 2, :], total[:, t % 2, :]).then_inc(rden_ready, 1)

            def add_x(y, bank, k):
                return nc.vector.tensor_tensor(y[:], bank[:].rearrange("p (t c) -> p t c", c=C),
                                               x_all[:, bass.ds(k * CHUNK, CHUNK), :], ALU.add)

            def body(c, a, b, m, l):
                if m:
                    attend(c, 0)
                    attend(c, 1)
                    sums(c, 0)
                    attend(c, 2)
                    attend(c, 3)
                    sums(c, 1)
                    sums(c, 2)
                if l:
                    dve.wait_ge(full["O"], c)
                    dve.wait_ge(out_bias_added, c)
                    wait(dve, x2_ready, c - 1)
                    add_x(y2, W[1], c - 1).then_inc(taken["O"], 1)
                if a:
                    dve.wait_ge(full["proj"], c + 3)
                    dve.wait_ge(proj_bias_added, c + 3)
                    wait(dve, x1_ready, c + 2)
                    add_x(y1, W[0], c + 2).then_inc(taken["proj"], 1)
                if m:
                    sums(c, 3)
                if l:
                    dve.wait_ge(taken["O"], c)
                if a:
                    dve.wait_ge(taken["proj"], c + 3)
                norm(0 if a else 1, 1 if l else 0, B + (c + 2) * NORM_LINKS)

            def attend(c, t):
                dve.wait_ge(full["S"], c * CHUNK + t + 1)
                s = SS[t % 2][:].rearrange("p (h k) -> p h k", k=KC)
                nc.vector.tensor_reduce(mx[:, t % 2, :], s, AX.X, ALU.max).then_inc(max_ready, 1)
                dve.wait_ge(max_ready, c * CHUNK + t + 1)
                wait(dve, exp_done, c * CHUNK + t - 1)
                nc.vector.tensor_tensor(z[:, t % 2, :].rearrange("p (h k) -> p h k", k=KC), s,
                                        mx[:, t % 2, :, None].to_broadcast([P, H, KC]), ALU.subtract) \
                    .then_inc(z_ready, 1)

            run_chunks(dve, body)

        @block.gpsimd
        def _(pool):
            pool.wait_ge(weights_loaded, 16 * 5)
            pool.wait_ge(x_first_in, 16)
            for k in range(CHUNKS):
                if k == 1:
                    pool.wait_ge(x_rest_in, 16)
                x = x_all[:, k * CHUNK:(k + 1) * CHUNK, :]
                nc.gpsimd.tensor_tensor(x, x, rows["b_proj"][:, None, :].to_broadcast([P, CHUNK, C]), ALU.add) \
                    .then_inc(proj_bias_added, 1)

            def body(c, a, b, m, l):
                if b:
                    pool.wait_ge(x1_ready, c + 2)
                    nc.gpsimd.tensor_tensor(x_all[:, bass.ds((c + 1) * CHUNK, CHUNK), :], x1[:],
                                            rows["bo"][:, None, :].to_broadcast([P, CHUNK, C]), ALU.add) \
                        .then_inc(out_bias_added, 1)
                if m:
                    for t in range(CHUNK):
                        pool.wait_ge(rden_ready, c * CHUNK + t + 1)
                        wait(pool, full["pT"], c * CHUNK + t - 1)
                        nc.gpsimd.tensor_tensor(pn[:, t % 2, :].rearrange("p (h k) -> p h k", k=KC),
                                                pr[:, t % 2, :].rearrange("p (h k) -> p h k", k=KC),
                                                rden[:, t % 2, :, None].to_broadcast([P, H, KC]), ALU.mult) \
                            .then_inc(normalised, 1)

            run_chunks(pool, body)


GT = 32
ES = 128
F = 32
QUADS = ES // 4
GB = N // GT
GALL = B * GB
HALF_C = C // 2


def route_phase(nc, io, x_all, w1, perm_all, inner):
    with ExitStack() as ctx:
        def sb(name, shape, dt=F32):
            return ctx.enter_context(nc.sbuf_tensor(name, shape, dt))

        def sem(name):
            return ctx.enter_context(nc.semaphore(name))

        ident, identb = sb("ident3", [P, P]), sb("ident3b", [P, P], BF16)
        w1 = w1[:].rearrange("p (c e f) -> p c e f", c=2, f=F)
        wc = sb("wc", [P, 2, ES])
        b1 = sb("b1", [P, QUADS])
        bc = sb("bc", [P, 1])
        tie = sb("tie", [P, GT])
        xs = sb("xs", [P, KT, C])
        xT = sb("xT3", [P, 2, N])
        lg = sb("lg", [P, N])
        hidden = sb("hidden", [P, N // 2])
        gmax = sb("gmax", [P, GB])
        perm = sb("perm", [P, KT, ES], BF16)
        xp = sb("xp", [P, SPLIT, KT, C], BF16)
        taken_x = sb("taken_x", [P, 2, ES, GB])

        banks = [ctx.enter_context(nc.psum_tensor(f"R{n}", [P, 512], F32)) for n in range(8)]
        loaded = sem("loaded3")
        xs_ready, turned, xT_ready, logits_done = sem("xs_ready"), sem("turned"), sem("xT_ready"), sem("logits_done")
        lg_step, perm_ready, perm_turned, perm_out = sem("lg_step"), sem("perm_ready"), sem("perm_turned"), sem("perm_out")
        hi_ready, rest_ready, mid_ready, lo_ready = sem("hi3"), sem("rest3"), sem("mid3"), sem("lo3")
        gathered, got_act, got_dve = sem("gathered"), sem("got_act"), sem("got_dve")
        hidden_done, hidden_taken, hidden_out = sem("hidden_done"), sem("hidden_taken"), sem("hidden_out")
        zeros_set = sem("zeros_set3")

        def run_batches(eng, body):
            with eng.Fori(0, B - 1) as b:
                body(b, True)
            body(B - 1, False)

        block = ctx.enter_context(nc.Block())

        @block.sync
        def _(sp):
            for dst, src in ((ident[:], io["ident"]), (wc[:], io["Wc"]), (b1[:], io["b1"]), (bc[:], io["bc"]),
                             (tie[:], io["tie"].to_broadcast([P, GT]))):
                sp.dma_start(dst, src).then_inc(loaded, 16)

        @block.gpsimd
        def _(pool):
            nc.gpsimd.memset(inner[:], 0.0).then_inc(zeros_set, 1)
            pool.sem_inc(lo_ready, 1)
            with pool.Fori(0, B) as b:
                pool.wait_ge(rest_ready, b + 1)
                nc.gpsimd.tensor_tensor(xp[:, 2], xs[:], xp[:, 1], ALU.subtract).then_inc(lo_ready, 1)

        @block.tensor
        def _(pe):
            def turn_x(b):
                pe.wait_ge(xs_ready, b + 1)
                for ci in range(2):
                    for half in range(2):
                        for t in range(4):
                            mm = pe.transpose(banks[ci * 2 + half][:, t * P:(t + 1) * P],
                                              xs[:, half * 4 + t, ci * P:(ci + 1) * P], ident[:])
                mm.then_inc(turned, 1)

            def logits(b):
                pe.wait_ge(xT_ready, b + 1)
                for half in range(2):
                    for ci in range(2):
                        mm = pe.matmul(banks[4 + half][:], wc[:, ci, :], xT[:, ci, half * 512:(half + 1) * 512],
                                       start=(ci == 0), stop=(ci == 1))
                mm.then_inc(logits_done, 1)

            def turn_perm(b):
                pe.wait_ge(perm_ready, b + 1)
                for t in range(KT):
                    mm = pe.transpose(banks[0][:].bitcast(BF16)[:, t * ES:(t + 1) * ES],
                                      perm_all[:, bass.ds(b * N + t * P, P)], identb[:])
                mm.then_inc(perm_turned, 1)

            def hidden_layer(b, half):
                for q in range(half * 16, half * 16 + 16):
                    for ci in range(2):
                        for j in range(4):
                            mm = pe.matmul(banks[6 + half][j * F:(j + 1) * F, (q % 16) * GB:(q % 16 + 1) * GB],
                                           w1[:, ci, 4 * q + j, :], taken_x[:, ci, 4 * q + j, :],
                                           start=(ci == 0), stop=(ci == 1))
                mm.then_inc(hidden_done, 1)

            pe.wait_ge(loaded, 16 * 5)
            turn_x(0)
            logits(0)
            turn_perm(0)

            def body(b, more):
                pe.wait_ge(perm_out, b + 1)
                pe.wait_ge(lo_ready, b + 2)
                for k in range(KT // 2):
                    if k >= 2:
                        pe.wait_ge(got_act, b * (KT // 2) + k - 1)
                        pe.wait_ge(got_dve, b * (KT // 2) + k - 1)
                    elif k == 1:
                        pe.wait_ge(hidden_taken, b * 2 + 2)
                    for t in range(2):
                        for ci in range(2):
                            for part in range(SPLIT):
                                for g in range(4):
                                    mm = pe.matmul(banks[(k % 2) * 4 + g][:, (t * 2 + ci) * ES:(t * 2 + ci + 1) * ES],
                                                   xp[g * GT:(g + 1) * GT, part, 2 * k + t, ci * P:(ci + 1) * P],
                                                   perm[g * GT:(g + 1) * GT, 2 * k + t, :],
                                                   start=(part == 0), stop=(part == SPLIT - 1))
                    mm.then_inc(gathered, 1)
                if more:
                    pe.wait_ge(got_act, b * (KT // 2) + KT // 2 - 1)
                    pe.wait_ge(got_dve, b * (KT // 2) + KT // 2 - 1)
                    turn_x(b + 1)
                pe.wait_ge(got_act, (b + 1) * (KT // 2))
                pe.wait_ge(got_dve, (b + 1) * (KT // 2))
                hidden_layer(b, 0)
                if more:
                    logits(b + 1)
                hidden_layer(b, 1)
                if more:
                    turn_perm(b + 1)

            run_batches(pe, body)

        def gather_out(copy, k, g):
            src = banks[(k % 2) * 4 + g][:].rearrange("p (t c e) -> p t c e", t=2, c=2)
            for ci in range(2):
                ins = copy(taken_x[:, ci].rearrange("p e (t g) -> p t e g", g=4)[:, 2 * k:2 * k + 2, :, g],
                           src[:, :, ci, :])
            return ins

        @block.scalar
        def _(act):
            def route(b):
                act.wait_ge(turned, b + 1)
                for ci in range(2):
                    for half in range(2):
                        ins = nc.scalar.copy(xT[:, ci, half * 512:(half + 1) * 512], banks[ci * 2 + half][:])
                ins.then_inc(xT_ready, 1)
                nc.scalar.copy(xp[:, 0], xs[:]).then_inc(hi_ready, 1)
                act.wait_ge(mid_ready, b + 1)
                nc.scalar.copy(xp[:, 1], xs[:]).then_inc(rest_ready, 1)
                act.wait_ge(perm_turned, b + 1)
                nc.scalar.copy(perm[:].rearrange("p t e -> p (t e)"), banks[0][:].bitcast(BF16)).then_inc(perm_out, 1)

            route(0)

            def body(b, more):
                for k in range(KT // 2):
                    act.wait_ge(gathered, b * (KT // 2) + k + 1)
                    for g in range(2):
                        ins = gather_out(nc.scalar.copy, k, g)
                    ins.then_inc(got_act, 1)
                if more:
                    route(b + 1)

            run_batches(act, body)

        @block.vector
        def _(dve):
            def copy_x(b):
                dve.wait_ge(lo_ready, b + 1)
                nc.vector.tensor_copy(xs[:], x_all[:, bass.ds(b * KT, KT), :]).then_inc(xs_ready, 1)

            def rest(b):
                dve.wait_ge(hi_ready, b + 1)
                nc.vector.tensor_tensor(xs[:], xs[:], xp[:, 0], ALU.subtract).then_inc(mid_ready, 1)

            def choose(b):
                dve.wait_ge(logits_done, b + 1)
                for half in range(2):
                    ins = nc.vector.scalar_tensor_tensor(
                        out=lg[:, half * 512:(half + 1) * 512].rearrange("p (g t) -> p g t", t=GT),
                        in0=banks[4 + half][:].rearrange("p (g t) -> p g t", t=GT), scalar=bc[:, 0:1],
                        in1=tie[:, None, :].to_broadcast([P, GB // 2, GT]), op0=ALU.add, op1=ALU.add)
                ins.then_inc(lg_step, 1)
                dve.wait_ge(lg_step, b * 2 + 1)
                by_group = lg[:].rearrange("p (g t) -> p g t", t=GT)
                nc.vector.tensor_reduce(gmax[:], by_group, AX.X, ALU.max).then_inc(lg_step, 1)
                dve.wait_ge(lg_step, b * 2 + 2)
                nc.vector.tensor_tensor(perm_all[:, bass.ds(b * N, N)].rearrange("p (g t) -> p g t", t=GT), by_group,
                                        gmax[:, :, None].to_broadcast([P, GB, GT]), ALU.is_equal) \
                    .then_inc(perm_ready, 1)

            def bias_and_relu(b, half):
                dve.wait_ge(hidden_done, b * 2 + half + 1)
                nc.vector.tensor_tensor(
                    hidden[:].rearrange("p (q g) -> p q g", g=GB),
                    banks[6 + half][:].rearrange("p (q g) -> p q g", g=GB),
                    b1[:, half * 16:(half + 1) * 16, None].to_broadcast([P, 16, GB]), ALU.add) \
                    .then_inc(hidden_taken, 1)
                dve.wait_ge(hidden_taken, b * 2 + half + 3)
                for j in range(4):
                    ins = nc.vector.tensor_scalar(
                        inner[j * F:(j + 1) * F, half * 16:(half + 1) * 16, j, bass.ds(b * GB, GB)],
                        hidden[j * F:(j + 1) * F, :].rearrange("p (q g) -> p q g", g=GB), 0.0, None, ALU.max)
                ins.then_inc(hidden_out, 1)
                dve.wait_ge(hidden_out, b * 2 + half + 1)

            dve.sem_inc(hidden_taken, 2)
            dve.wait_ge(loaded, 16 * 5)
            copy_x(0)
            nc.vector.tensor_copy(identb[:], ident[:])
            rest(0)
            choose(0)
            dve.wait_ge(zeros_set, 1)

            def body(b, more):
                if more:
                    copy_x(b + 1)
                for k in range(KT // 2):
                    dve.wait_ge(gathered, b * (KT // 2) + k + 1)
                    for g in range(2, 4):
                        ins = gather_out(nc.vector.tensor_copy, k, g)
                    ins.then_inc(got_dve, 1)
                if more:
                    rest(b + 1)
                bias_and_relu(b, 0)
                if more:
                    choose(b + 1)
                bias_and_relu(b, 1)

            run_batches(dve, body)


def combine_phase(nc, io, x_all, w1, perm_all, inner, out):
    with ExitStack() as ctx:
        def sb(name, shape, dt=F32):
            return ctx.enter_context(nc.sbuf_tensor(name, shape, dt))

        def sem(name):
            return ctx.enter_context(nc.semaphore(name))

        ident = sb("ident4", [P, P])
        w2 = w1[:, 0:QUADS * HALF_C].rearrange("p (q d) -> p q d", d=HALF_C)
        permf = w1[:, QUADS * HALF_C:QUADS * HALF_C + B * N]
        b2 = sb("b2", [ES, HALF_C])
        res = sb("res", [P, GALL, ES])
        resT = sb("resT", [P, 2, 4, HALF_C])
        LAST = 4
        LT = B * KT // LAST
        stats = sb("stats4", [P, LAST, LT, 6])
        mv = sb("mv4", [P, LAST, LT, 2])
        var, ln_t, ln_h, ln_r, ln_m = (sb(n, [P, LAST, LT]) for n in ("var4", "ln_t4", "ln_h4", "ln_r4", "ln_m4"))
        factors = sem("factors4")
        outer_banks = [ctx.enter_context(nc.psum_tensor(f"E{n}", [P, 512], F32)) for n in range(4)]
        turn_banks = [ctx.enter_context(nc.psum_tensor(f"T{n}", [P, 512], F32)) for n in range(2)]
        sum_banks = [ctx.enter_context(nc.psum_tensor(f"Y{n}", [P, 512], F32)) for n in range(2)]
        loaded, w2_loaded = sem("loaded4"), sem("w2_loaded")
        outer_done, out_act, out_dve = sem("outer_done"), sem("out_act"), sem("out_dve")
        rows_turned, rows_act, rows_dve = sem("rows_turned4"), sem("rows_act"), sem("rows_dve")
        summed, added = sem("summed"), sem("added")
        permf_ready, ln_step, normed, stored = sem("permf_ready"), sem("ln_step"), sem("normed"), sem("stored")
        block = ctx.enter_context(nc.Block())
        TILES = B * KT

        @block.sync
        def _(sp):
            sp.dma_start(ident[:], io["ident"]).then_inc(loaded, 16)
            with sp.Fori(0, 2) as c:
                sp.wait_ge(summed, c * (TILES // 4) + 1)
                sp.dma_start(w2, io["W2T"][:, bass.ds(c, 1)].rearrange("p o q d -> p (o q) d")) \
                    .then_inc(w2_loaded, 16)
                sp.dma_start(b2[:], io["b2"][:, bass.ds(c, 1)].rearrange("e o d -> e (o d)")).then_inc(w2_loaded, 16)
            for k in range(CHUNKS):
                sp.wait_ge(normed, k + 1)
                sp.dma_start(out[:, k * CHUNK:(k + 1) * CHUNK], x_all[:, k * CHUNK:(k + 1) * CHUNK]) \
                    .then_inc(stored, 16)
            sp.wait_ge(stored, 16 * CHUNKS)

        @block.tensor
        def _(pe):
            pe.sem_inc(summed, 1)
            pe.wait_ge(loaded, 16)
            pe.wait_ge(permf_ready, 1)
            with pe.Fori(0, 2) as c:
                pe.wait_ge(w2_loaded, c * 32 + 32)
                for q in range(QUADS):
                    if q >= 4:
                        pe.wait_ge((out_act, out_dve)[q % 2], c * (QUADS // 2) + q // 2 - 1)
                    pe.matmul(outer_banks[q % 4][:], w2[:, q, :], inner[:, q].rearrange("p j g -> p (j g)"),
                              start=True, stop=True).then_inc(outer_done, 1)
                pe.wait_ge(out_act, (c + 1) * (QUADS // 2))
                pe.wait_ge(out_dve, (c + 1) * (QUADS // 2))

                def combine(k):
                    pe.wait_ge((rows_act, rows_dve)[k % 2], c * (TILES // 2) + k // 2 + 1)
                    y = sum_banks[(k // 4) % 2]
                    if k % 4 == 0 and k >= 8:
                        pe.wait_ge(added, c * (TILES // 4) + k // 4 - 1)
                    for first in (True, False):
                        for g in range(4):
                            mm = pe.matmul(y[g * GT:(g + 1) * GT, (k % 4) * HALF_C:(k % 4 + 1) * HALF_C],
                                           permf[:, k * P + g * GT:k * P + (g + 1) * GT],
                                           b2[:] if first else resT[:, k % 2, g, :],
                                           start=first, stop=not first)
                    if k % 4 == 3:
                        mm.then_inc(summed, 1)

                for k in range(TILES):
                    if k >= 2:
                        pe.wait_ge((rows_act, rows_dve)[k % 2], c * (TILES // 2) + k // 2)
                    for g in range(4):
                        mm = pe.transpose(turn_banks[k % 2][:, g * HALF_C:(g + 1) * HALF_C],
                                          res[:, 4 * k + g, :], ident[:])
                    mm.then_inc(rows_turned, 1)
                    if k >= 1:
                        combine(k - 1)
                combine(TILES - 1)
                pe.wait_ge(added, (c + 1) * (TILES // 4))

        def experts_out(copy, q):
            return copy(res[:, :, 4 * q:4 * q + 4].rearrange("p g j -> p j g"),
                        outer_banks[q % 4][:].rearrange("p (j g) -> p j g", j=4))

        def evacuate(eng, copy, c, which, out_sem, rows_sem, extra):
            for q in range(which, QUADS, 2):
                eng.wait_ge(outer_done, c * QUADS + q + 1)
                experts_out(copy, q).then_inc(out_sem, 1)
            for k in range(which, TILES, 2):
                eng.wait_ge(rows_turned, c * TILES + k + 1)
                copy(resT[:, k % 2].rearrange("p g d -> p (g d)"), turn_banks[k % 2][:]).then_inc(rows_sem, 1)
                extra(c, k)

        @block.scalar
        def _(act):
            with act.Fori(0, 2) as c:
                evacuate(act, nc.scalar.copy, c, 0, out_act, rows_act, lambda c, k: None)
            for k in range(LAST):
                act.wait_ge(factors, k + 1)
                for t in range(LT):
                    ins = nc.scalar.activation(x_all[:, k * LT + t, :], x_all[:, k * LT + t, :], ACT.Identity,
                                               scale=ln_r[:, k, t:t + 1], bias=ln_m[:, k, t:t + 1])
                    if t % 4 == 3:
                        ins.then_inc(normed, 1)

        @block.vector
        def _(dve):
            nc.vector.tensor_copy(permf, perm_all[:]).then_inc(permf_ready, 1)

            def add(c, k4):
                dve.wait_ge(summed, c * (TILES // 4) + k4 + 2)
                x = x_all[:, k4 * 4:k4 * 4 + 4, bass.ds(c * HALF_C, HALF_C)]
                nc.vector.tensor_tensor(x, sum_banks[k4 % 2][:].rearrange("p (t d) -> p t d", d=HALF_C), x,
                                        ALU.add).then_inc(added, 1)

            with dve.Fori(0, 2) as c:
                evacuate(dve, nc.vector.tensor_copy, c, 1, out_dve, rows_dve,
                         lambda c, k: add(c, k // 4 - 1) if k % 4 == 1 and k > 4 else None)
                add(c, TILES // 4 - 1)

            n = [0]

            def link(ins):
                n[0] += 1
                ins.then_inc(ln_step, 1)
                dve.wait_ge(ln_step, n[0])

            dve.wait_ge(added, 2 * (TILES // 4))
            for k in range(LAST):
                norm_factors(nc, link, LT, lambda t: x_all[:, k * LT + t, :], stats[:, k], mv[:, k], var[:, k],
                             (ln_r[:, k], ln_t[:, k], ln_h[:, k]), ln_m[:, k]).then_inc(factors, 1)


def program(nc, io, out):
    qk_parts = nc.dram_tensor("qk_parts", [SPLIT, 2, B, C, N], BF16, kind="Internal").ap()
    v_scratch = nc.dram_tensor("v_scratch", [PAIRS, 2, P, H, VW], F32, kind="Internal").ap()
    attn_scratch = nc.dram_tensor("attn_scratch", [GROUPS, KT, P, HG * D], F32, kind="Internal").ap()
    shift_scratch = nc.dram_tensor("shift_scratch", [SHIFT, HG * N], BF16, kind="Internal").ap()
    attention_phases(nc, io, qk_parts, v_scratch, attn_scratch, shift_scratch)
    with nc.sbuf_tensor("x_all", [P, B * KT, C], F32) as x_all:
        with nc.sbuf_tensor("w1", [P, 2 * ES * F], F32) as w1:
            cross_attention_phase(nc, io, attn_scratch, x_all, w1)
            with nc.sbuf_tensor("perm_all", [P, B * N], BF16) as perm_all, \
                    nc.sbuf_tensor("inner", [P, QUADS, 4, GALL], F32) as inner:
                route_phase(nc, io, x_all, w1, perm_all, inner)
                combine_phase(nc, io, x_all, w1, perm_all, inner, out)


def kernel(**inputs):
    import numpy as np
    import concourse.bacc as bacc
    from concourse.bass_utils import run_bass_kernel_spmd as run

    a = {k: np.asarray(v) for k, v in inputs.items()}
    half = D // 2
    freqs = (1.0 / 2500 ** (np.arange(half, dtype=np.float32) / half)).astype(np.float32)
    angle = np.outer(np.arange(N, dtype=np.float32), freqs).astype(np.float32)
    angle = np.concatenate([angle, angle], -1)

    def by_tile(t):
        return np.ascontiguousarray(np.tile(t.reshape(KT, P, D).transpose(1, 0, 2), (1, B, 1)))

    sign = np.where(np.arange(D) < half, -1.0, 1.0).astype(np.float32)
    x = a["x"].reshape(B * N, C)
    ctxT = a["ctx_1024"].reshape(B * KC, C).T

    def by_half(w):
        return w.reshape(2, P, -1).transpose(1, 0, 2)

    arrays = {
        "xT": x.T.reshape(2, P, B * N).transpose(1, 0, 2),
        "w_qkv": a["L0_attn_w_qkv"].reshape(2, P, 3 * C).transpose(1, 0, 2),
        "q_scale": a["L0_attn_q_scale"].reshape(1, D),
        "k_scale": a["L0_attn_k_scale"].reshape(1, D),
        "ident": np.eye(P, dtype=np.float32),
        "cos": by_tile(np.cos(angle).astype(np.float32)),
        "sin": by_tile(np.sin(angle).astype(np.float32) * sign),
        "x": x.reshape(B * KT, P, C).transpose(1, 0, 2),
        "w_proj": by_half(a["L0_attn_w_proj"]),
        "WqT": by_half(a["L0_xattn_Wq"].T), "WkT": by_half(a["L0_xattn_Wk"].T),
        "WvT": by_half(a["L0_xattn_Wv"].T), "WoT": by_half(a["L0_xattn_Wo"].T),
        "b_proj": a["L0_attn_b_proj"].reshape(1, C), "bv": a["L0_xattn_bv"].reshape(1, C),
        "bo": a["L0_xattn_bo"].reshape(1, C),
        "bias_cols": np.stack([a["L0_xattn_bq"].reshape(2, P).T, a["L0_xattn_bk"].reshape(2, P).T], 1),
        "head_mask": (np.arange(P)[:, None] // D == np.arange(P // D)[None]).astype(np.float32),
        "half_mask": (np.arange(P)[:, None] // KC == np.arange(2 * D)[None] // D).astype(np.float32),
        "Wc": by_half(a["L0_ffn_Wc"].reshape(C, ES)),
        "bc": a["L0_ffn_bc"].reshape(ES, 1),
        "tie": np.linspace(0.0, 1e-6, GT, dtype=np.float32).reshape(1, GT),
        "W1": a["L0_ffn_W1"].reshape(ES, 2, P, F).transpose(2, 1, 0, 3),
        "b1": a["L0_ffn_b1"].reshape(QUADS, P).T,
        "W2T": a["L0_ffn_W2"].reshape(QUADS, 4, 2, HALF_C, F).transpose(1, 4, 2, 0, 3).reshape(P, 2, QUADS, HALF_C),
        "b2": a["L0_ffn_b2"].reshape(ES, 2, HALF_C),
        "ctxT": by_half(ctxT).reshape(P, 2, B, KC),
        "ctxT2": np.repeat(by_half(ctxT).reshape(P, 2, B, 1, KC), 2, axis=3),
    }
    nc = bacc.Bacc("TRN2", target_bir_lowering=False, num_devices=1)
    feed, handles = {}, {}
    for name, array in arrays.items():
        feed["in_" + name] = np.ascontiguousarray(array)
        handles[name] = nc.dram_tensor("in_" + name, array.shape, F32, kind="ExternalInput").ap()
    out = nc.dram_tensor("out_0", [P, B * KT, C], F32, kind="ExternalOutput").ap()
    program(nc, handles, out)
    r = run(nc, [feed], core_ids=[0])
    return np.ascontiguousarray(r.results[0]["out_0"].transpose(1, 0, 2)).reshape(B, N, C)
```

```python
from contextlib import ExitStack

import concourse.bass as bass
from concourse import mybir

F32 = mybir.dt.float32
BF16 = mybir.dt.bfloat16
I32 = mybir.dt.int32
ACT = mybir.ActivationFunctionType
ALU = mybir.AluOpType
AX = mybir.AxisListType

P = 128
B, N, C = 4, 1024, 256
H, D = 16, 16
KT = N // P
HG = 4
GPB = H // HG
GROUPS = B * GPB
VW = 32
SPLIT = 3
Q_PART = [0, 0, 0, 1, 1, 2]
K_PART = [0, 1, 2, 0, 1, 0]
STACK = D * len(Q_PART)
SHIFT = 2
AHEAD = 6
PAIRS = B * KT // 2
LOOP_PAIRS = PAIRS - AHEAD
RMS_EPS = 1e-6
LN_EPS = 1e-5
SAFE_LOGIT = 60.0
MAGIC = float(0x5F3759DF)


PAIRED = (2, 3, 4)
PROBS = 4
QW = N // HG


def wait(eng, sem, value):
    if not (isinstance(value, int) and value <= 0):
        eng.wait_ge(sem, value)


def newton_rsqrt(nc, link, y, t, hv, v):
    bits = y.bitcast(I32)
    nc.vector.tensor_scalar(bits, v.bitcast(I32), 1, None, ALU.logical_shift_right)
    link(nc.vector.tensor_scalar(hv, v, -0.5, None, ALU.mult))
    link(nc.vector.tensor_scalar(bits, bits, -1.0, MAGIC, ALU.mult, ALU.add))
    for step in range(3):
        link(nc.vector.tensor_tensor(t, y, y, ALU.mult))
        link(nc.vector.tensor_tensor(t, t, hv, ALU.mult))
        link(nc.vector.scalar_tensor_tensor(out=y, in0=t, scalar=1.5, in1=y, op0=ALU.add, op1=ALU.mult))


def attention_phases(nc, io, qk_parts, v_scratch, attn_scratch, shift_scratch):
    with ExitStack() as ctx:
        def sb(name, shape, dt):
            return ctx.enter_context(nc.sbuf_tensor(name, shape, dt))

        def psum(name, shape):
            return ctx.enter_context(nc.psum_tensor(name, shape, F32))

        wqkv = sb("wqkv", [P, 2, 3 * C], F32)
        ident = sb("ident", [P, P], F32)
        zeros = sb("zeros", [P, 8 * P], F32)
        cos = sb("cos", [P, B * KT, D], F32)
        sin = sb("sin", [P, B * KT, D], F32)
        scales = sb("scales", [P, 2, D], F32)
        rope_c = sb("rope_c", [P, B * KT, 2, D], F32)
        rope_s = sb("rope_s", [P, B * KT, 2, D], F32)
        xT = sb("xT", [P, 2, 2 * P], F32)
        raw = sb("raw", [P, 2, 2 * C], F32)
        sq = sb("sq", [P, 2, 2 * C], F32)
        ra = sb("ra", [P, 2, 2 * C], F32)
        rb = sb("rb", [P, 2, 2 * C], F32)
        ms, rstd, nt, nh = (sb(n, [P, 2 * 2 * H], F32) for n in ("ms", "rstd", "nt", "nh"))
        qn = sb("qn", [P, 2, 2 * C], F32)
        rest = sb("rest", [P, 4, 2, P], F32)
        parts = sb("parts", [P, SPLIT, 4, 2, P], BF16)
        vbuf = sb("vbuf", [P, 2, H, VW], F32)
        qst = sb("qst", [P, 2, HG, N], BF16)
        kst = sb("kst", [P, 2, HG, N], BF16)
        vst = sb("vst", [P, 2, KT, HG, VW], F32)
        prob = sb("prob", [P, PROBS, HG, N], F32)
        oT = sb("oT", [P, N], F32)
        rden = sb("rden", [P, 2, 4 * HG], F32)
        attn = sb("attn", [P, KT, HG, D], F32)
        flag = sb("flag", [1, 1], I32)
        bound = sb("bound", [1, 4], F32)
        rmax = sb("rmax", [P, HG * KT], F32)
        shift = sb("shift", [HG * KT, SHIFT, P], BF16)

        S = [psum(f"S{n}", [P, N]) for n in range(2)]
        O = psum("O", [P, N])
        X = [psum(f"X{n}", [P, 512]) for n in range(2)]

        def pe_qk(pe, x, bank):
            for c in range(2):
                mm = pe.matmul(bank[:, 0:2 * C], x(c), wqkv[:, c, 0:2 * C], start=(c == 0), stop=(c == 1))
            return mm

        def pe_v(pe, x, bank):
            for c in range(2):
                mm = pe.matmul(bank[:, 0:C], x(c), wqkv[:, c, 2 * C:3 * C], start=(c == 0), stop=(c == 1))
            return mm

        def x_tile(u):
            return lambda c: xT[:, c, u * P:(u + 1) * P]

        def pe_turn(pe, u, bank):
            for c in range(4):
                mm = pe.transpose(bank[:, c * P:(c + 1) * P], qn[:, u, c * P:(c + 1) * P], ident[:])
            return mm

        def rope_view(t):
            return t.rearrange("p u (a h d) -> p (u a) h d", a=2, d=D)

        ROPE_LINKS = 1 + 2 + 11

        def dve_products(dve, s, link, n, pair):
            def table(t, lo, hi):
                return t[:, bass.ds(pair * 2, 2), :, lo:hi].rearrange("p u a d -> p (u a) d")[:, :, None, :] \
                    .to_broadcast([P, 4, H, hi - lo])
            dve.wait_ge(s["qn_ready"], n + 1)
            dve.wait_ge(s["raw_ready"], n * 2 + 4)
            half = D // 2
            nc.vector.tensor_tensor(rope_view(ra[:]), rope_view(raw[:]), table(rope_c, 0, D), ALU.mult)
            nc.vector.tensor_tensor(rope_view(rb[:])[:, :, :, 0:half], rope_view(raw[:])[:, :, :, half:D],
                                    table(rope_s, 0, half), ALU.mult)
            link(nc.vector.tensor_tensor(rope_view(rb[:])[:, :, :, half:D], rope_view(raw[:])[:, :, :, 0:half],
                                         table(rope_s, half, D), ALU.mult))

        def add_products(engine, s):
            engine.tensor_tensor(ra[:], ra[:], rb[:], ALU.add).then_inc(s["rotated"], 1)

        def dve_norm(dve, s, link, n):
            dve.wait_ge(s["sq_ready"], n + 1)
            link(nc.vector.tensor_reduce(ms[:], sq[:].rearrange("p u (h d) -> p (u h) d", d=D), AX.X, ALU.add))
            link(nc.vector.tensor_scalar(ms[:], ms[:], 1.0 / D, RMS_EPS, ALU.mult, ALU.add))
            newton_rsqrt(nc, link, rstd[:], nt[:], nh[:], ms[:])
            dve.wait_ge(s["rotated"], n + 2)
            nc.vector.tensor_tensor(qn[:].rearrange("p u (h d) -> p (u h) d", d=D),
                                    ra[:].rearrange("p u (h d) -> p (u h) d", d=D),
                                    rstd[:, :, None].to_broadcast([P, 4 * H, D]), ALU.mult).then_inc(s["qn_ready"], 1)

        def dve_rest(dve, s, n, u, bank, hi_sem, hi_count):
            dve.wait_ge(hi_sem, hi_count)
            if u == 0:
                dve.wait_ge(s["parts_ready"], n + 1)
            nc.vector.tensor_tensor(rest[:, :, u, :], bank[:].rearrange("p (c t) -> p c t", c=4),
                                    parts[:, 0, :, u, :], ALU.subtract).then_inc(s["t_taken"], 1)

        def pool_square(pool, s, n):
            pool.wait_ge(s["raw_ready"], n * 2 + 4)
            pool.wait_ge(s["qn_ready"], n + 1)
            nc.gpsimd.tensor_tensor(sq[:], raw[:], raw[:], ALU.mult).then_inc(s["sq_ready"], 1)

        def pool_parts(pool, s, n):
            def flat(t):
                return t.rearrange("p c u t -> p (c u t)")
            pool.wait_ge(s["t_taken"], n * 2 + 4)
            nc.gpsimd.tensor_tensor(flat(parts[:, 1]), flat(rest[:]), zeros[:], ALU.add).then_inc(s["mid_ready"], 1)
            pool.wait_ge(s["mid_ready"], n + 1)
            nc.gpsimd.tensor_tensor(flat(parts[:, 2]), flat(rest[:]), flat(parts[:, 1]),
                                    ALU.subtract).then_inc(s["parts_ready"], 1)

        def load_x(eng, s, pair):
            eng.dma_start(xT[:], io["xT"][:, :, bass.ds(pair * 2 * P, 2 * P)]).then_inc(s["x_loaded"], 16)

        def sp_store_v(sp, s, pair):
            sp.dma_start(v_scratch[bass.ds(pair, 1)].rearrange("o u p h w -> p (o u) (h w)"),
                         vbuf[:].rearrange("p u h w -> p u (h w)")).then_inc(s["v_written"], 16)

        def sp_store_parts(sp, s, b, quarter):
            for part in range(SPLIT):
                for a in range(2):
                    dst = qk_parts[part, a, bass.ds(b, 1), :, bass.ds(quarter * 2 * P, 2 * P)] \
                        .rearrange("o (c p) t -> p (o c) t", p=P)
                    src = parts[:, part, 2 * a:2 * a + 2].rearrange("p c u t -> p c (u t)")
                    sp.dma_start(dst, src).then_inc(s["parts_written"], 16)

        PARTS_WRITTEN = 16 * SPLIT * 2

        def projection_semaphores(stack, tag):
            names = ("x_loaded", "qk_ps", "v_ps", "t_ps", "raw_ready", "sq_ready", "v_ready", "hi_ready",
                     "rotated", "qn_ready", "t_taken", "mid_ready", "parts_ready", "v_written", "parts_written")
            return {n: stack.enter_context(nc.semaphore(f"{tag}_{n}")) for n in names}

        def sp_credits(sp, s):
            sp.sem_inc(s["v_written"], 16)
            sp.sem_inc(s["parts_written"], PARTS_WRITTEN)

        stacks_loaded = [ctx.enter_context(nc.semaphore(f"stacks_loaded{n}")) for n in range(2)]

        def load_stacks(sp, i, par):
            b, g = i // GPB, i % GPB
            for a, (dst, order) in enumerate(((qst, Q_PART), (kst, K_PART))):
                for r, part in enumerate(order):
                    src = qk_parts[part, a, bass.ds(b, 1), bass.ds(g * HG * D, HG * D), :] \
                        .rearrange("o (h d) t -> d (o h) t", d=D)
                    sp.dma_start(dst[r * D:(r + 1) * D, par], src).then_inc(stacks_loaded[par], 16)
            src = v_scratch[bass.ds(b * (KT // 2), KT // 2), :, :, bass.ds(g * HG, HG), :] \
                .rearrange("q u p h w -> p (q u) (h w)")
            sp.dma_start(vst[:, par].rearrange("p k h w -> p k (h w)"), src).then_inc(stacks_loaded[par], 16)

        first = projection_semaphores(ctx, "a")

        with ExitStack() as stage:
            s = first
            const_loaded = stage.enter_context(nc.semaphore("const_loaded"))
            tables_loaded = stage.enter_context(nc.semaphore("tables_loaded"))
            table_step = stage.enter_context(nc.semaphore("table_step"))
            rope_step = stage.enter_context(nc.semaphore("a_rope_step"))
            zeros_set = stage.enter_context(nc.semaphore("zeros_set"))
            pad_set = stage.enter_context(nc.semaphore("pad_set"))
            block = stage.enter_context(nc.Block())

            def run_pairs(eng, body):
                with eng.Fori(0, AHEAD - 2) as it:
                    body(it, 2)
                body(AHEAD - 2, 1)
                body(AHEAD - 1, 0)

            @block.sync
            def _(sp):
                sp_credits(sp, s)
                load_x(sp, s, 0)
                sp.dma_start(wqkv[:], io["w_qkv"]).then_inc(const_loaded, 16)
                sp.dma_start(scales[:, 0, :], io["q_scale"].to_broadcast([P, D])).then_inc(tables_loaded, 16)
                sp.dma_start(scales[:, 1, :], io["k_scale"].to_broadcast([P, D])).then_inc(tables_loaded, 16)
                sp.dma_start(cos[:], io["cos"]).then_inc(tables_loaded, 16)
                sp.dma_start(sin[:], io["sin"]).then_inc(tables_loaded, 16)
                sp.dma_start(ident[:], io["ident"]).then_inc(const_loaded, 16)
                sp.wait_ge(s["v_ps"], 2)
                load_x(sp, s, 1)
                sp.wait_ge(s["v_ready"], 4)
                sp_store_v(sp, s, 0)

                def body(it, more):
                    if not more:
                        sp.wait_ge(s["v_written"], 16 * (AHEAD + 1))
                        sp.wait_ge(s["parts_written"], PARTS_WRITTEN * AHEAD)
                        load_stacks(sp, 0, 0)
                    if more:
                        sp.wait_ge(s["v_ready"], it * 2 + 6)
                        sp_store_v(sp, s, it + 1)
                    if more == 2:
                        load_x(sp, s, it + 2)
                    sp.wait_ge(s["parts_ready"], it + 2)
                    sp_store_parts(sp, s, it // 4, it % 4)

                run_pairs(sp, body)

            @block.tensor
            def _(pe):
                def project(pair):
                    pe.wait_ge(s["x_loaded"], pair * 16 + 16)
                    for u in range(2):
                        pe.wait_ge(s["raw_ready"], pair * 2 + u + 1)
                        pe_qk(pe, x_tile(u), S[u][:, 0:512]).then_inc(s["qk_ps"], 1)
                        pe.wait_ge(s["v_ready"], pair * 2 + u + 1)
                        pe_v(pe, x_tile(u), S[u][:, 512:1024]).then_inc(s["v_ps"], 1)

                pe.wait_ge(const_loaded, 16 * 2)
                project(0)

                def body(it, more):
                    if more:
                        project(it + 1)
                    for u in range(2):
                        pe.wait_ge(s["qn_ready"], it + 2)
                        pe.wait_ge(s["t_taken"], it * 2 + u + 1)
                        pe_turn(pe, u, X[u]).then_inc(s["t_ps"], 1)

                run_pairs(pe, body)

            @block.scalar
            def _(act):
                act.sem_inc(s["raw_ready"], 2)
                act.sem_inc(s["v_ready"], 2)
                act.wait_ge(pad_set, 1)

                def evacuate(pair):
                    for u in range(2):
                        act.wait_ge(s["qk_ps"], pair * 2 + u + 1)
                        if u == 0:
                            act.wait_ge(s["rotated"], pair + 1)
                            wait(act, s["sq_ready"], pair)
                        nc.scalar.copy(raw[:, u, :], S[u][:, 0:512]).then_inc(s["raw_ready"], 1)
                        if u == 0:
                            act.wait_ge(s["v_written"], pair * 16 + 16)
                        act.wait_ge(s["v_ps"], pair * 2 + u + 1)
                        nc.scalar.copy(vbuf[:, u, :, 0:D],
                                       S[u][:, 512:512 + C].rearrange("p (h d) -> p h d", d=D)).then_inc(s["v_ready"], 1)

                def squares(pair):
                    act.wait_ge(s["raw_ready"], pair * 2 + 4)
                    act.wait_ge(s["qn_ready"], pair + 1)
                    nc.scalar.activation(sq[:], raw[:], ACT.Square).then_inc(s["sq_ready"], 1)

                evacuate(0)
                squares(0)

                def body(it, more):
                    if more:
                        evacuate(it + 1)
                        squares(it + 1)
                    for u in range(2):
                        act.wait_ge(s["t_ps"], it * 2 + u + 1)
                        if u == 0:
                            act.wait_ge(s["parts_written"], it * PARTS_WRITTEN + PARTS_WRITTEN)
                        nc.scalar.copy(parts[:, 0, :, u, :],
                                       X[u][:].rearrange("p (c t) -> p c t", c=4)).then_inc(s["hi_ready"], 1)

                run_pairs(act, body)

            @block.vector
            def _(dve):
                count = [0]

                def once(ins):
                    count[0] += 1
                    ins.then_inc(table_step, 1)
                    dve.wait_ge(table_step, count[0])

                nc.vector.memset(vbuf[:, :, :, D + 1:VW], 0.0)
                nc.vector.memset(vbuf[:, :, :, D:D + 1], 1.0).then_inc(pad_set, 1)
                dve.wait_ge(tables_loaded, 16 * 4)
                half = D // 2
                for a in range(2):
                    def scale(lo, hi):
                        return scales[:, a:a + 1, lo:hi].to_broadcast([P, B * KT, hi - lo])
                    nc.vector.tensor_tensor(rope_c[:, :, a, :], cos[:], scale(0, D), ALU.mult)
                    nc.vector.tensor_tensor(rope_s[:, :, a, 0:half], sin[:, :, 0:half], scale(half, D), ALU.mult)
                    once(nc.vector.tensor_tensor(rope_s[:, :, a, half:D], sin[:, :, half:D], scale(0, half), ALU.mult))
                once(nc.vector.tensor_reduce(bound[:, 0:2], scales[0:1], AX.X, ALU.max, apply_absolute_value=True))
                once(nc.vector.tensor_tensor(bound[:, 2:3], bound[:, 0:1], bound[:, 1:2], ALU.mult))
                once(nc.vector.tensor_scalar(flag[:], bound[:, 2:3], SAFE_LOGIT * D ** 0.5 / D, None, ALU.is_le))
                dve.sem_inc(s["qn_ready"], 1)
                dve.sem_inc(s["t_taken"], 2)

                def linker(start):
                    links = [0]

                    def link(ins):
                        links[0] += 1
                        ins.then_inc(rope_step, 1)
                        dve.wait_ge(rope_step, start + links[0])
                    return link

                dve_products(dve, s, linker(0), 0, 0)

                def body(it, more):
                    dve_norm(dve, s, linker(it * ROPE_LINKS + 1), it)
                    if more:
                        dve_products(dve, s, linker((it + 1) * ROPE_LINKS), it + 1, it + 1)
                    for u in range(2):
                        dve_rest(dve, s, it, u, X[u], s["hi_ready"], it * 2 + u + 1)

                run_pairs(dve, body)

            @block.gpsimd
            def _(pool):
                pool.sem_inc(s["parts_ready"], 1)
                nc.gpsimd.memset(zeros[:], 0.0).then_inc(zeros_set, 1)
                pool.wait_ge(zeros_set, 1)
                nc.gpsimd.memset(kst[STACK:P, :, :, :], 1.0).then_inc(zeros_set, 1)
                pool.wait_ge(zeros_set, 2)
                nc.gpsimd.memset(qst[STACK:P, :, :, :], 0.0).then_inc(zeros_set, 1)
                pool.wait_ge(zeros_set, 3)
                pool.sem_inc(s["rotated"], 1)

                def rotated(n):
                    pool.wait_ge(rope_step, n * ROPE_LINKS + 1)
                    add_products(nc.gpsimd, s)

                rotated(0)

                def body(it, more):
                    if more:
                        rotated(it + 1)
                    pool_parts(pool, s, it)

                run_pairs(pool, body)

        with ExitStack() as stage:
            s = projection_semaphores(stage, "m")

            def sem(name):
                return stage.enter_context(nc.semaphore(name))

            flag_read = sem("flag_read")
            rope_step = sem("m_rope_step")
            qk_done, exp_done, av_done = sem("qk_done"), sem("exp_done"), sem("av_done")
            o_copied, at_ps, at_taken = sem("o_copied"), sem("at_ps"), sem("at_taken")
            rden_ready, attn_written = sem("rden_ready"), sem("attn_written")
            row_scores, row_taken, rows_turned = sem("row_scores"), sem("row_taken"), sem("rows_turned")
            shift_ready, shift_loaded = sem("shift_ready"), sem("shift_loaded")
            shift_high, shift_stored = sem("shift_high"), sem("shift_stored")
            block = stage.enter_context(nc.Block())
            LOADS = 16 * (2 * len(Q_PART) + 1)
            TILES = HG * KT

            WITH, WITHOUT = LOOP_PAIRS // 2, GROUPS // 2 - 1 - LOOP_PAIRS // 2

            def run_groups(eng, body):
                with eng.Fori(0, WITH) as jj:
                    for par in range(2):
                        body(jj * 2 + par, par, True, False)
                with eng.Fori(WITH, WITH + WITHOUT) as jj:
                    for par in range(2):
                        body(jj * 2 + par, par, False, False)
                for par in range(2):
                    body(GROUPS - 2 + par, par, False, par == 1)

            @block.sync
            def _(sp):
                sp.wait_ge(first["parts_written"], PARTS_WRITTEN * (AHEAD + 1))
                sp_credits(sp, s)
                sp.sem_inc(attn_written, 16)
                general = sp.value_load(flag[:], min_val=0, max_val=1)

                def load_shift(i, par):
                    with sp.If(general < 1):
                        sp.wait_ge(shift_ready, i + 1)
                        sp.dma_start(shift_scratch.rearrange("r (n q) -> n r q", q=P), shift[:]).then_inc(shift_stored, 16)
                        sp.wait_ge(shift_stored, (i + 1) * 16)
                        sp.dma_start(qst[STACK:STACK + SHIFT, par].rearrange("r h t -> r (h t)"),
                                     shift_scratch).then_inc(shift_loaded, 16)

                load_shift(0, 0)

                def body(i, par, project, last):
                    if not last:
                        groups_before = i * (2 * KT) + 2 * KT
                        sp.wait_ge(av_done, groups_before)
                        if project:
                            sp.wait_ge(s["v_written"], groups_before)
                            sp.wait_ge(s["parts_written"], i * PARTS_WRITTEN + PARTS_WRITTEN)
                        elif not isinstance(i, int):
                            sp.wait_ge(s["v_written"], 16 * (LOOP_PAIRS + 1))
                            sp.wait_ge(s["parts_written"], PARTS_WRITTEN * (LOOP_PAIRS + 1))
                        load_stacks(sp, i + 1, 1 - par)
                    if project:
                        sp.wait_ge(s["v_ready"], i * 2 + 4)
                        sp_store_v(sp, s, i + AHEAD)
                        sp.wait_ge(s["parts_ready"], i + 2)
                        sp_store_parts(sp, s, (i + AHEAD) // 4, (i + AHEAD) % 4)
                    if not last:
                        load_shift(i + 1, 1 - par)
                    sp.wait_ge(at_taken, i * 2 + 4)
                    sp.dma_start(attn_scratch[bass.ds(i, 1)].rearrange("o t p c -> p (o t) c"),
                                 attn[:].rearrange("p t h d -> p t (h d)")).then_inc(attn_written, 16)

                run_groups(sp, body)
                sp.wait_ge(attn_written, 16 * (GROUPS + 1))

            @block.tensor
            def _(pe):
                pe.sem_inc(s["v_ps"], 1)
                pe.sem_inc(av_done, 2 * KT)
                general = pe.value_load(flag[:], min_val=0, max_val=1)

                def scores(i, par, kt, h):
                    n = kt * HG + h
                    pe.wait_ge(exp_done, i * TILES + n + 1)
                    for half in range(2):
                        mm = pe.matmul(S[h % 2][:, half * 512:(half + 1) * 512],
                                       kst[0:STACK + SHIFT, par, h, kt * P:(kt + 1) * P],
                                       qst[0:STACK + SHIFT, par, h, half * 512:(half + 1) * 512],
                                       start=True, stop=True)
                    mm.then_inc(qk_done, 1)

                def values(i, par, kt, quarter, width=1):
                    pe.wait_ge(exp_done, i * TILES + kt * HG + HG + 2)
                    if kt == 0 and quarter % 2 == 0:
                        pe.wait_ge(o_copied, i * 2 + quarter // 2 + 1)
                    q = slice(quarter * QW, (quarter + width) * QW)
                    ends_bank = (quarter + width) % 2 == 0
                    for h in range(HG):
                        mm = pe.matmul(O[h * VW:(h + 1) * VW, q], vst[:, par, kt, h, :], prob[:, kt % PROBS, h, q],
                                       start=(kt == 0 and quarter % 2 == 0), stop=(kt == KT - 1 and ends_bank))
                    if ends_bank:
                        mm.then_inc(av_done, 1)

                def turn_output(i, half):
                    pe.wait_ge(o_copied, i * 2 + half + 3)
                    pe.wait_ge(at_taken, i * 2 + half + 1)
                    for t in range(4):
                        mm = pe.transpose(X[half][:, t * P:(t + 1) * P],
                                          oT[:, half * 512 + t * P:half * 512 + (t + 1) * P], ident[:])
                    mm.then_inc(at_ps, 1)

                def projection(i, kt, h):
                    if (kt, h) == (2, 2):
                        pe.wait_ge(s["x_loaded"], i * 16 + 16)
                        pe.wait_ge(at_taken, i * 2 + 1)
                        pe_qk(pe, x_tile(0), X[0]).then_inc(s["qk_ps"], 1)
                    elif (kt, h) == (3, 0):
                        pe.wait_ge(at_taken, i * 2 + 2)
                        pe_v(pe, x_tile(0), X[1]).then_inc(s["v_ps"], 1)
                    elif (kt, h) == (3, 2):
                        pe.wait_ge(s["raw_ready"], i * 2 + 3)
                        pe_qk(pe, x_tile(1), X[0]).then_inc(s["qk_ps"], 1)
                    elif (kt, h) == (4, 1):
                        pe.wait_ge(s["v_ready"], i * 2 + 3)
                        pe_v(pe, x_tile(1), X[1]).then_inc(s["v_ps"], 1)
                    elif (kt, h) in ((7, 0), (7, 2)):
                        u = h // 2
                        pe.wait_ge(s["qn_ready"], i + 2)
                        pe.wait_ge(s["v_ready"] if u else s["raw_ready"], i * 2 + 4)
                        pe_turn(pe, u, X[u]).then_inc(s["t_ps"], 1)

                def row_maxima(i, par):
                    with pe.If(general < 1):
                        pe.wait_ge(stacks_loaded[par], (i // 2) * LOADS + LOADS)
                        pe.wait_ge(exp_done, i * TILES + 2)
                        for n in range(TILES):
                            h, t = n // KT, n % KT
                            pe.wait_ge(row_taken, i * TILES + n + 1)
                            for half in range(2):
                                mm = pe.matmul(S[n % 2][:, half * 512:(half + 1) * 512],
                                               qst[0:STACK, par, h, t * P:(t + 1) * P],
                                               kst[0:STACK, par, h, half * 512:(half + 1) * 512],
                                               start=True, stop=True)
                            mm.then_inc(row_scores, 1)
                        pe.wait_ge(row_taken, (i + 1) * TILES + 2)
                        pe.transpose(S[0][0:TILES, 0:P], rmax[:], ident[:]).then_inc(rows_turned, 1)
                        pe.wait_ge(shift_loaded, (i + 1) * 16)

                def first_tiles(i, par, previous, projected=False):
                    row_maxima(i, par)
                    pe.wait_ge(stacks_loaded[par], (i // 2) * LOADS + LOADS)
                    if previous is None:
                        for h in range(HG):
                            scores(i, par, 0, h)
                        for h in range(HG):
                            scores(i, par, 1, h)
                            if h > 0:
                                values(i, par, 0, h - 1)
                        return
                    last = (previous, 1 - par, KT - 1)
                    for h in range(HG):
                        scores(i, par, 0, h)
                        if h > 0:
                            values(*last, h - 1)
                        elif not in_pairs(projected, KT - 1):
                            values(previous, 1 - par, KT - 2, HG - 1)
                    scores(i, par, 1, 0)
                    values(*last, HG - 1)
                    turn_output(previous, 0)
                    scores(i, par, 1, 1)
                    values(i, par, 0, 0)
                    scores(i, par, 1, 2)
                    values(i, par, 0, 1)
                    turn_output(previous, 1)
                    scores(i, par, 1, 3)
                    values(i, par, 0, 2)

                first_tiles(0, 0, None)

                def in_pairs(project, kt):
                    return project and kt in PAIRED

                def body(i, par, project, last):
                    for kt in range(2, KT):
                        for h in range(HG):
                            scores(i, par, kt, h)
                            if h == 0:
                                if not in_pairs(project, kt - 1):
                                    values(i, par, kt - 2, HG - 1)
                            elif not in_pairs(project, kt):
                                values(i, par, kt - 1, h - 1)
                            elif h % 2 == 1:
                                values(i, par, kt - 1, h - 1, 2)
                            if project:
                                projection(i, kt, h)
                    if last:
                        values(i, par, KT - 2, HG - 1)
                        for quarter in range(HG):
                            values(i, par, KT - 1, quarter)
                        for half in range(2):
                            turn_output(i, half)
                    else:
                        first_tiles(i + 1, 1 - par, i, project)

                run_groups(pe, body)

            @block.scalar
            def _(act):
                act.sem_inc(exp_done, 2)

                def exps(i, par, kt):
                    for h in range(HG):
                        n = kt * HG + h
                        act.wait_ge(qk_done, i * TILES + n + 1)
                        if h == 0:
                            act.wait_ge(av_done, (i * KT + kt - PROBS) * 2 + 2 * KT + 2)
                        nc.scalar.activation(prob[:, kt % PROBS, h, :], S[h % 2][:], ACT.Exp,
                                             scale=float(D) ** -0.5).then_inc(exp_done, 1)

                for kt in range(2):
                    exps(0, 0, kt)

                def body(i, par, project, last):
                    for kt in range(2, KT):
                        exps(i, par, kt)
                    if not last:
                        for kt in range(2):
                            exps(i + 1, 1 - par, kt)

                run_groups(act, body)

            @block.vector
            def _(dve):
                dve.sem_inc(s["raw_ready"], 2)
                dve.sem_inc(s["v_ready"], 2)
                dve.sem_inc(s["qn_ready"], 1)
                dve.sem_inc(s["rotated"], 1)
                dve.sem_inc(s["t_taken"], 2)
                dve.sem_inc(o_copied, 2)
                dve.sem_inc(at_taken, 2)
                dve.sem_inc(row_taken, 2)
                general = dve.value_load(flag[:], min_val=0, max_val=1)

                def raw_copy(i, u):
                    dve.wait_ge(s["qk_ps"], i * 2 + u + 1)
                    nc.vector.tensor_copy(raw[:, u, :], X[0][:]).then_inc(s["raw_ready"], 1)

                def v_copy(i, u):
                    if u == 0:
                        dve.wait_ge(s["v_written"], i * 16 + 16)
                    dve.wait_ge(s["v_ps"], i * 2 + u + 2)
                    nc.vector.tensor_copy(vbuf[:, u, :, 0:D],
                                          X[1][:, 0:C].rearrange("p (h d) -> p h d", d=D)).then_inc(s["v_ready"], 1)

                def first_part(i, u):
                    dve.wait_ge(s["t_ps"], i * 2 + u + 1)
                    if u == 0:
                        dve.wait_ge(s["parts_written"], i * PARTS_WRITTEN + PARTS_WRITTEN)
                    nc.vector.tensor_copy(parts[:, 0, :, u, :],
                                          X[u][:].rearrange("p (c t) -> p c t", c=4)).then_inc(s["hi_ready"], 1)

                def row_maxima(i):
                    with dve.If(general < 1):
                        for n in range(TILES):
                            dve.wait_ge(row_scores, i * TILES + n + 1)
                            nc.vector.tensor_reduce(rmax[:, n:n + 1], S[n % 2][:], AX.X, ALU.max)\
                                .then_inc(row_taken, 1)
                        dve.wait_ge(rows_turned, i + 1)
                        nc.vector.tensor_scalar(shift[:, 0, :], S[0][0:TILES, 0:P], -1.0, None, ALU.mult)\
                            .then_inc(shift_high, 1)
                        dve.wait_ge(shift_high, i + 1)
                        nc.vector.scalar_tensor_tensor(out=shift[:, 1, :], in0=S[0][0:TILES, 0:P], scalar=-1.0,
                                                       in1=shift[:, 0, :], op0=ALU.mult,
                                                       op1=ALU.subtract).then_inc(shift_ready, 1)

                row_maxima(0)

                def body(i, par, project, last):
                    if project:
                        links = [0]

                        def link(ins):
                            links[0] += 1
                            ins.then_inc(rope_step, 1)
                            dve.wait_ge(rope_step, i * ROPE_LINKS + links[0])

                        for u in range(2):
                            raw_copy(i, u)
                            v_copy(i, u)
                        dve_products(dve, s, link, i, i + AHEAD)
                        add_products(nc.vector, s)
                        dve_norm(dve, s, link, i)
                        for u in range(2):
                            first_part(i, u)
                            dve_rest(dve, s, i, u, X[u], s["hi_ready"], i * 2 + u + 1)
                        assert links[0] == ROPE_LINKS
                    if not last:
                        row_maxima(i + 1)
                    for half in range(2):
                        dve.wait_ge(av_done, (i * KT + KT - 1) * 2 + 2 * KT + half + 1)
                        nc.vector.tensor_copy(oT[:, half * 512:(half + 1) * 512],
                                              O[:, half * 512:(half + 1) * 512]).then_inc(o_copied, 1)
                    for half in range(2):
                        dve.wait_ge(at_ps, i * 2 + half + 1)
                        x = X[half][:].rearrange("p (c w) -> p c w", w=VW)
                        nc.vector.reciprocal(rden[:, half, :], x[:, :, D]).then_inc(rden_ready, 1)
                        dve.wait_ge(rden_ready, i * 2 + half + 1)
                        if half == 0:
                            dve.wait_ge(attn_written, i * 16 + 16)
                        nc.vector.tensor_tensor(attn[:, half * 4:(half + 1) * 4].rearrange("p t h d -> p (t h) d"),
                                                x[:, :, 0:D],
                                                rden[:, half, :, None].to_broadcast([P, 4 * HG, D]),
                                                ALU.mult).then_inc(at_taken, 1)

                run_groups(dve, body)

            @block.gpsimd
            def _(pool):
                pool.sem_inc(s["parts_ready"], 1)
                with pool.Fori(0, LOOP_PAIRS) as it:
                    pool.wait_ge(s["v_ps"], it * 2 + 1)
                    load_x(pool, s, it + AHEAD)
                    pool_square(pool, s, it)
                    pool_parts(pool, s, it)


CHUNK = 4
CW = CHUNK * P
CHUNKS = B * N // CW
KC = 64
PAIRH = H // 2


NORM_LINKS = 4 + 11


def norm_statistics(nc, tiles, y, stats):
    for t in range(tiles):
        ins = nc.vector.bn_stats(stats[:, t, :], y(t))
    return ins


def norm_factors(nc, link, stats, mv, var, rsqrt, minus):
    mean, apart = mv[:, :, 0], mv[:, :, 1]
    nc.vector.tensor_tensor(mean, stats[:, :, 1], stats[:, :, 4], ALU.add)
    nc.vector.tensor_tensor(apart, stats[:, :, 1], stats[:, :, 4], ALU.subtract)
    link(nc.vector.tensor_tensor(var, stats[:, :, 2], stats[:, :, 5], ALU.add))
    nc.vector.tensor_tensor(apart, apart, apart, ALU.mult)
    link(nc.vector.tensor_scalar(var, var, 1.0 / C, LN_EPS, ALU.mult, ALU.add))
    link(nc.vector.scalar_tensor_tensor(out=var, in0=apart, scalar=0.25, in1=var, op0=ALU.mult, op1=ALU.add))
    newton_rsqrt(nc, link, *rsqrt, var)
    return nc.vector.scalar_tensor_tensor(out=minus, in0=mean, scalar=-0.5, in1=rsqrt[0], op0=ALU.mult, op1=ALU.mult)


def cross_attention_phase(nc, io, attn_scratch, x_all, w1, ident, router):
    with ExitStack() as ctx:
        def sb(name, shape, dt=F32):
            return ctx.enter_context(nc.sbuf_tensor(name, shape, dt))

        def psum(name, shape):
            return ctx.enter_context(nc.psum_tensor(name, shape, F32))

        def sem(name):
            return ctx.enter_context(nc.semaphore(name))

        wproj, wq, wk = sb("wproj", [P, 2, C]), sb("wq", [P, 2, C]), sb("wk", [P, 2, C])
        wv, wo = sb("wv", [P, 2, C]), sb("wo", [P, 2, C])
        rows = {n: sb("row_" + n, [P, C]) for n in ("b_proj", "bv", "bo")}
        cols = sb("bias_cols", [P, 2, 2])
        head_mask = sb("head_mask", [P, P // D])
        half_mask = sb("half_mask", [P, 2 * D])
        ctxT = sb("ctxT", [P, 2, B, KC])
        ctxT2 = sb("ctxT2", [P, 2, B, 2, KC])
        kT = sb("kT", [P, 2, B, KC])
        kbd = sb("kbd", [P, B, 2, P // D, KC])
        vrow = sb("vrow", [P, B, C])
        vbd_all = sb("vbd_all", [P, B, PAIRH, 2 * D])
        vbd = sb("vbd", [P, PAIRH, 2 * D])

        at = sb("at", [P, CHUNK, C])
        aT = sb("aT", [P, 2, CW])
        y1 = sb("y1", [P, CHUNK, C])
        x1 = sb("x1", [P, CHUNK, C])
        x1T = sb("x1T", [P, 2, CW])
        qT = sb("qT", [P, 2, CW])
        mx = sb("mx", [P, 2, H])
        z = sb("z", [P, 2, H * KC])
        pr = sb("pr", [P, 2, H * KC])
        pT = sb("pT", [P, PAIRH, CW])
        total = sb("total", [P, 2, H])
        rden = sb("rden2", [P, 2, H])
        pn = sb("pn", [P, 2, H * KC])
        oT = sb("oT2", [P, 2, CW])
        y2 = sb("y2", [P, CHUNK, C])
        stats = sb("stats", [P, 2, CHUNK, 6])
        mv = sb("mv", [P, 2, CHUNK, 2])
        var, ln_t, ln_h, ln_r, ln_m = (sb(n, [P, 2, CHUNK]) for n in ("var", "ln_t", "ln_h", "ln_r", "ln_m"))

        W = [psum(f"W{n}", [P, 2 * 512]) for n in range(2)]
        SS = [psum(f"SS{n}", [P, 2 * 512]) for n in range(2)]

        context_loaded, first_loaded = sem("context_loaded"), sem("first_loaded")
        x_in, at_loaded = sem("x_in"), sem("at_loaded")
        full = {j: sem("full_" + j) for j in ("prep", "x1T", "V", "aT", "q", "proj", "O", "pT", "S")}
        taken = {j: sem("taken_" + j) for j in ("prep", "x1T", "V", "aT", "q", "proj", "O", "pT")}
        z_ready, exp_done, x1_ready = sem("z_ready"), sem("exp_done2"), sem("x1_ready")
        proj_bias_added, out_bias_added, dve_step = sem("proj_bias_added"), sem("out_bias_added"), sem("dve_step2")
        factors, x2_ready, k_ready = sem("factors"), sem("x2_ready"), sem("k_ready")
        total_ready, rden_ready, normalised = sem("total_ready"), sem("rden_ready2"), sem("normalised")
        vbd_loaded = sem("vbd_loaded")
        max_ready, w1_loaded = sem("max_ready"), sem("w1_loaded")

        def run_chunks(eng, body, prepare):
            body(-2, True, False, False, False)
            prepare()
            body(-1, True, True, False, False)
            body(0, True, True, True, False)
            with eng.Fori(1, CHUNKS - 2) as c:
                body(c, True, True, True, True)
            body(CHUNKS - 2, False, True, True, True)
            body(CHUNKS - 1, False, False, True, True)
            body(CHUNKS, False, False, False, True)

        PROB_BANK = (0, 1, 0, 0)
        PREP_DVE = 2 + B

        block = ctx.enter_context(nc.Block())

        @block.sync
        def _(sp):
            def load_at(c):
                for t in range(CHUNK):
                    b, half = c // 2, c % 2
                    src = attn_scratch[bass.ds(b * GPB, GPB), bass.ds(half * CHUNK + t, 1)] \
                        .rearrange("g o p c -> p (g o) c")
                    sp.dma_start(at[:, t, :].rearrange("p (g c) -> p g c", g=GPB), src).then_inc(at_loaded, 16)

            def load_x(k):
                wait(sp, proj_bias_added, k)
                sp.dma_start(x_all[:, bass.ds(k * CHUNK, CHUNK), :], io["x"][:, bass.ds(k * CHUNK, CHUNK), :]) \
                    .then_inc(x_in, 16)

            load_at(0)
            for dst, src in ((ident[:], io["ident"]), (wproj[:], io["w_proj"]),
                             (rows["b_proj"][:], io["b_proj"].to_broadcast([P, C]))):
                sp.dma_start(dst, src).then_inc(first_loaded, 16)
            load_x(0)
            for dst, src in ((ctxT[:], io["ctxT"]), (wk[:], io["WkT"]), (ctxT2[:], io["ctxT2"]), (wv[:], io["WvT"]),
                             (cols[:], io["bias_cols"]), (rows["bv"][:], io["bv"].to_broadcast([P, C])),
                             (head_mask[:], io["head_mask"]), (half_mask[:], io["half_mask"]),
                             (wq[:], io["WqT"]), (rows["bo"][:], io["bo"].to_broadcast([P, C])),
                             (wo[:], io["WoT"])):
                sp.dma_start(dst, src).then_inc(context_loaded, 16)
            load_x(1)

            def load_vbd(k):
                wait(sp, full["V"], k)
                sp.dma_start(vbd[:], vbd_all[:, bass.ds(k // 2, 1)].rearrange("p o h d -> p (o h) d")) \
                    .then_inc(vbd_loaded, 16)

            for k in range(1, 4):
                sp.wait_ge(full["aT"], k)
                load_at(k)
                load_x(k + 1)
                if k == 1:
                    sp.wait_ge(taken["prep"], PREP_DVE)
                    load_vbd(0)
            with sp.Fori(1, CHUNKS - 4) as k:
                load_vbd(k)
                sp.wait_ge(full["aT"], k + 3)
                load_at(k + 3)
                load_x(k + 4)
            load_vbd(CHUNKS - 4)
            sp.wait_ge(full["aT"], CHUNKS - 1)
            load_at(CHUNKS - 1)
            sp.dma_start(w1[:].rearrange("p (c n) -> p c n", c=2), io["W1"].rearrange("p c e f -> p c (e f)")) \
                .then_inc(w1_loaded, 16)
            for dst, src in ((router["wc"], io["Wc"]), (router["b1"], io["b1"]), (router["bc"], io["bc"]),
                             (router["tie"], io["tie"].to_broadcast([P, GT]))):
                sp.dma_start(dst, src).then_inc(w1_loaded, 16)
            for k in range(CHUNKS - 3, CHUNKS):
                load_vbd(k)
            sp.wait_ge(w1_loaded, 16 * 5)

        @block.tensor
        def _(pe):
            def turn(dst, src):
                for ci in range(2):
                    for t in range(CHUNK):
                        mm = pe.transpose(dst[:, ci * CW + t * P:ci * CW + (t + 1) * P],
                                          src[:, t, ci * P:(ci + 1) * P], ident[:])
                return mm

            def scores(c, t):
                wait(pe, z_ready, c * CHUNK + t - 1)
                for g in range(2):
                    mm = pe.matmul(SS[t % 2][:, g * 512:(g + 1) * 512], qT[:, g, t * P:(t + 1) * P],
                                   kbd[:, bass.ds(c // 2, 1), g].rearrange("p o h k -> p (o h k)"),
                                   start=True, stop=True)
                mm.then_inc(full["S"], 1)

            def turn_probs(c, t):
                pe.wait_ge(normalised, c * CHUNK + t + 1)
                for h in range(PAIRH):
                    mm = pe.transpose(W[PROB_BANK[t]][:, h * P:(h + 1) * P], pn[:, t % 2, h * P:(h + 1) * P], ident[:])
                mm.then_inc(full["pT"], 1)

            def by_tokens(bank, lhs, weights):
                for t in range(CHUNK):
                    for ci in range(2):
                        mm = pe.matmul(bank[:, t * C:(t + 1) * C], lhs[:, ci, t * P:(t + 1) * P], weights[:, ci, :],
                                       start=(ci == 0), stop=(ci == 1))
                return mm

            def body(c, a, b, m, l):
                if m:
                    if isinstance(c, int) and c == 0:
                        pe.wait_ge(k_ready, 1)
                    pe.wait_ge(taken["q"], c + 1)
                    scores(c, 0)
                    scores(c, 1)
                if l:
                    pe.wait_ge(taken["pT"], c * CHUNK)
                    pe.wait_ge(vbd_loaded, c * 16)
                    for g in range(2):
                        for j in range(4):
                            mm = pe.matmul(W[1][32 * j:32 * j + 32, g * CW:(g + 1) * CW],
                                           vbd[:, 4 * g + j, :], pT[:, 4 * g + j, :], start=True, stop=True)
                    mm.then_inc(full["V"], 1)
                if b:
                    pe.wait_ge(x1_ready, c + 2)
                    pe.wait_ge(taken["proj"], c + 2)
                    turn(W[0], x1).then_inc(full["x1T"], 1)
                if m:
                    scores(c, 2)
                if a:
                    pe.wait_ge(at_loaded, (c + 3) * 16 * CHUNK)
                    if isinstance(c, int) and c == -2:
                        pe.wait_ge(first_loaded, 16 * 3)
                    wait(pe, taken["aT"], c + 2)
                    if l:
                        pe.wait_ge(taken["V"], c)
                    turn(W[1], at).then_inc(full["aT"], 1)
                if m:
                    scores(c, 3)
                    if b:
                        pe.wait_ge(taken["x1T"], c + 2)
                    turn_probs(c, 0)
                if l:
                    pe.wait_ge(taken["V"], c)
                    if a:
                        pe.wait_ge(taken["aT"], c + 3)
                    by_tokens(W[1], oT, wo).then_inc(full["O"], 1)
                if a:
                    pe.wait_ge(taken["aT"], c + 3)
                    if m:
                        pe.wait_ge(taken["pT"], c * CHUNK + 1)
                    elif b:
                        pe.wait_ge(taken["x1T"], c + 2)
                    by_tokens(W[0], aT, wproj).then_inc(full["proj"], 1)
                if m:
                    if l:
                        pe.wait_ge(taken["O"], c)
                    turn_probs(c, 1)
                    if a:
                        pe.wait_ge(taken["proj"], c + 3)
                    else:
                        pe.wait_ge(taken["pT"], c * CHUNK + 1)
                    turn_probs(c, 2)
                if b:
                    pe.wait_ge(taken["x1T"], c + 2)
                    if m:
                        pe.wait_ge(taken["pT"], c * CHUNK + 2)
                    else:
                        pe.wait_ge(taken["aT"], c + 3)
                    for half in range(2):
                        for ci in range(2):
                            mm = pe.matmul(W[1][:, half * CW:(half + 1) * CW], wq[:, ci, half * P:(half + 1) * P],
                                           x1T[:, ci, :], start=(ci == 0), stop=(ci == 1))
                    mm.then_inc(full["q"], 1)
                if m:
                    pe.wait_ge(taken["pT"], c * CHUNK + 3)
                    turn_probs(c, 3)

            def prepare():
                pe.wait_ge(context_loaded, 16 * 11)
                pe.wait_ge(taken["proj"], 1)
                pe.wait_ge(taken["aT"], 1)
                for m in range(2):
                    for ci in range(2):
                        mm = pe.matmul(W[m][:, 0:B * KC], wk[:, ci, m * P:(m + 1) * P],
                                       ctxT[:, ci].rearrange("p b k -> p (b k)"), start=(ci == 0), stop=(ci == 1))
                    mm.then_inc(full["prep"], 1)
                for b in range(B):
                    pe.wait_ge(taken["prep"], b + 1)
                    for ci in range(2):
                        mm = pe.matmul(W[b % 2][:, 0:C], ctxT2[:, ci, b].rearrange("p j k -> p (j k)"), wv[:, ci, :],
                                       start=(ci == 0), stop=(ci == 1))
                    mm.then_inc(full["prep"], 1)
                pe.wait_ge(taken["prep"], PREP_DVE)

            run_chunks(pe, body, prepare)

        @block.scalar
        def _(act):

            def expo(c, t):
                act.wait_ge(z_ready, c * CHUNK + t + 1)
                wait(act, normalised, c * CHUNK + t - 1)
                nc.scalar.activation(pr[:, t % 2, :], z[:, t % 2, :], ACT.Exp, scale=float(D) ** -0.5) \
                    .then_inc(exp_done, 1)

            def probs_out(c, t):
                act.wait_ge(full["pT"], c * CHUNK + t + 1)
                if t == 0:
                    wait(act, full["V"], c)
                nc.scalar.copy(pT[:, :, t * P:(t + 1) * P], W[PROB_BANK[t]][:].rearrange("p (h q) -> p h q", q=P)) \
                    .then_inc(taken["pT"], 1)

            def scaled(which, t, dst, src):
                return nc.scalar.activation(dst, src[:, t, :], ACT.Identity, scale=ln_r[:, which, t:t + 1],
                                            bias=ln_m[:, which, t:t + 1])

            def body(c, a, b, m, l):
                if m:
                    expo(c, 0)
                if l:
                    act.wait_ge(full["V"], c)
                    wait(act, full["O"], c - 1)
                    nc.scalar.copy(oT[:].rearrange("p c t -> p (c t)"), W[1][:]).then_inc(taken["V"], 1)
                if b:
                    act.wait_ge(full["x1T"], c + 2)
                    wait(act, full["q"], c + 1)
                    nc.scalar.copy(x1T[:].rearrange("p c t -> p (c t)"), W[0][:]).then_inc(taken["x1T"], 1)
                if m:
                    expo(c, 1)
                if a:
                    act.wait_ge(full["aT"], c + 3)
                    wait(act, full["proj"], c + 2)
                    nc.scalar.copy(aT[:].rearrange("p c t -> p (c t)"), W[1][:]).then_inc(taken["aT"], 1)
                if m:
                    expo(c, 2)
                    probs_out(c, 0)
                    expo(c, 3)
                    probs_out(c, 1)
                    probs_out(c, 2)
                if b:
                    act.wait_ge(full["q"], c + 2)
                    if m:
                        act.wait_ge(full["S"], (c + 1) * CHUNK)
                    for half in range(2):
                        ins = nc.scalar.activation(qT[:, half, :], W[1][:, half * CW:(half + 1) * CW], ACT.Identity,
                                                   bias=cols[:, 0, half:half + 1])
                    ins.then_inc(taken["q"], 1)
                if m:
                    probs_out(c, 3)
                act.wait_ge(factors, c + 3)
                if a:
                    wait(act, out_bias_added, c + 2)
                    for t in range(CHUNK):
                        ins = scaled(0, t, x1[:, t, :], y1)
                    ins.then_inc(x1_ready, 1)
                if l:
                    for t in range(CHUNK):
                        ins = scaled(1, t, x_all[:, bass.ds((c - 1) * CHUNK + t, 1), :].rearrange("p o c -> p (o c)"), y2)
                    ins.then_inc(x2_ready, 1)

            run_chunks(act, body, lambda: act.wait_ge(context_loaded, 16 * 11))

        @block.vector
        def _(dve):
            def norm(first, last, start):
                n = [0]

                def link(ins):
                    n[0] += 1
                    ins.then_inc(dve_step, 1)
                    dve.wait_ge(dve_step, start + n[0])

                def both(t):
                    return t[:, first:last + 1].rearrange("p w t -> p (w t)")

                spread = stats[:, first:last + 1].rearrange("p w t s -> p (w t) s")
                link(norm_statistics(nc, (last - first + 1) * CHUNK,
                                     lambda t: (y1, y2)[first + t // CHUNK][:, t % CHUNK, :], spread))
                norm_factors(nc, link, spread,
                             mv[:, first:last + 1].rearrange("p w t s -> p (w t) s"), both(var),
                             (both(ln_r), both(ln_t), both(ln_h)), both(ln_m)).then_inc(factors, 1)
                assert n[0] == NORM_LINKS

            def sums(c, t):
                dve.wait_ge(exp_done, c * CHUNK + t + 1)
                nc.vector.tensor_reduce(total[:, t % 2, :], pr[:, t % 2, :].rearrange("p (h k) -> p h k", k=KC),
                                        AX.X, ALU.add).then_inc(total_ready, 1)
                dve.wait_ge(total_ready, c * CHUNK + t + 1)
                wait(dve, normalised, c * CHUNK + t - 1)
                nc.vector.reciprocal(rden[:, t % 2, :], total[:, t % 2, :]).then_inc(rden_ready, 1)

            def add_x(y, bank, k):
                return nc.vector.tensor_tensor(y[:], bank[:].rearrange("p (t c) -> p t c", c=C),
                                               x_all[:, bass.ds(k * CHUNK, CHUNK), :], ALU.add)

            def body(c, a, b, m, l):
                if m:
                    attend(c, 0)
                    attend(c, 1)
                    sums(c, 0)
                    attend(c, 2)
                    attend(c, 3)
                    sums(c, 1)
                    sums(c, 2)
                if l:
                    dve.wait_ge(full["O"], c)
                    dve.wait_ge(out_bias_added, c)
                    wait(dve, x2_ready, c - 1)
                    add_x(y2, W[1], c - 1).then_inc(taken["O"], 1)
                if a:
                    dve.wait_ge(full["proj"], c + 3)
                    dve.wait_ge(proj_bias_added, c + 3)
                    wait(dve, x1_ready, c + 2)
                    add_x(y1, W[0], c + 2).then_inc(taken["proj"], 1)
                if m:
                    sums(c, 3)
                if l:
                    dve.wait_ge(taken["O"], c)
                if a:
                    dve.wait_ge(taken["proj"], c + 3)
                norm(0 if a else 1, 1 if l else 0,
                     0 if isinstance(c, int) and c == -2 else B + (c + 2) * NORM_LINKS)

            def attend(c, t):
                dve.wait_ge(full["S"], c * CHUNK + t + 1)
                s = SS[t % 2][:].rearrange("p (h k) -> p h k", k=KC)
                nc.vector.tensor_reduce(mx[:, t % 2, :], s, AX.X, ALU.max).then_inc(max_ready, 1)
                dve.wait_ge(max_ready, c * CHUNK + t + 1)
                wait(dve, exp_done, c * CHUNK + t - 1)
                nc.vector.tensor_tensor(z[:, t % 2, :].rearrange("p (h k) -> p h k", k=KC), s,
                                        mx[:, t % 2, :, None].to_broadcast([P, H, KC]), ALU.subtract) \
                    .then_inc(z_ready, 1)

            def prepare():
                dve.wait_ge(context_loaded, 16 * 11)
                for m in range(2):
                    dve.wait_ge(full["prep"], m + 1)
                    nc.vector.tensor_scalar(kT[:, m].rearrange("p b k -> p (b k)"), W[m][:, 0:B * KC],
                                            cols[:, 1, m:m + 1], None, ALU.add).then_inc(taken["prep"], 1)
                for b in range(B):
                    dve.wait_ge(full["prep"], 3 + b)
                    nc.vector.tensor_tensor(vrow[:, b], W[b % 2][:, 0:C], rows["bv"][:], ALU.add) \
                        .then_inc(dve_step, 1)
                    dve.wait_ge(dve_step, NORM_LINKS + b + 1)
                    nc.vector.tensor_tensor(vbd_all[:, b], vrow[:, b].rearrange("p (h d) -> p h d", d=2 * D),
                                            half_mask[:, None, :].to_broadcast([P, PAIRH, 2 * D]), ALU.mult) \
                        .then_inc(taken["prep"], 1)
                for b in range(B):
                    for m in range(2):
                        ins = nc.vector.tensor_tensor(kbd[:, b, m],
                                                      kT[:, m, b, None, :].to_broadcast([P, P // D, KC]),
                                                      head_mask[:, :, None].to_broadcast([P, P // D, KC]), ALU.mult)
                ins.then_inc(k_ready, 1)

            run_chunks(dve, body, prepare)

        @block.gpsimd
        def _(pool):
            def body(c, a, b, m, l):
                if a:
                    pool.wait_ge(x_in, (c + 3) * 16)
                    x = x_all[:, bass.ds((c + 2) * CHUNK, CHUNK), :]
                    nc.gpsimd.tensor_tensor(x, x, rows["b_proj"][:, None, :].to_broadcast([P, CHUNK, C]), ALU.add) \
                        .then_inc(proj_bias_added, 1)
                if b:
                    pool.wait_ge(x1_ready, c + 2)
                    nc.gpsimd.tensor_tensor(x_all[:, bass.ds((c + 1) * CHUNK, CHUNK), :], x1[:],
                                            rows["bo"][:, None, :].to_broadcast([P, CHUNK, C]), ALU.add) \
                        .then_inc(out_bias_added, 1)
                if m:
                    for t in range(CHUNK):
                        pool.wait_ge(rden_ready, c * CHUNK + t + 1)
                        wait(pool, full["pT"], c * CHUNK + t - 1)
                        nc.gpsimd.tensor_tensor(pn[:, t % 2, :].rearrange("p (h k) -> p h k", k=KC),
                                                pr[:, t % 2, :].rearrange("p (h k) -> p h k", k=KC),
                                                rden[:, t % 2, :, None].to_broadcast([P, H, KC]), ALU.mult) \
                            .then_inc(normalised, 1)

            pool.wait_ge(first_loaded, 16 * 3)
            run_chunks(pool, body, lambda: pool.wait_ge(context_loaded, 16 * 11))


GT = 32
ES = 128
F = 32
QUADS = ES // 4
GB = N // GT
GALL = B * GB
HALF_C = C // 2


def route_phase(nc, io, x_all, w1, ident, router, perm_all, inner):
    with ExitStack() as ctx:
        def sb(name, shape, dt=F32):
            return ctx.enter_context(nc.sbuf_tensor(name, shape, dt))

        def sem(name):
            return ctx.enter_context(nc.semaphore(name))

        identb = sb("ident3b", [P, P], BF16)
        w1 = w1[:].rearrange("p (c e f) -> p c e f", c=2, f=F)
        wc, b1, bc, tie = router["wc"], router["b1"], router["bc"], router["tie"]
        xs = sb("xs", [P, KT, C])
        xT = sb("xT3", [P, 2, N])
        lg = sb("lg", [P, N])
        hidden = sb("hidden", [P, N // 2])
        gmax = sb("gmax", [P, GB])
        perm = sb("perm", [P, KT, ES], BF16)
        xp = sb("xp", [P, SPLIT, KT, C], BF16)
        taken_x = sb("taken_x", [P, 2, ES, GB])

        banks = [ctx.enter_context(nc.psum_tensor(f"R{n}", [P, 512], F32)) for n in range(8)]
        xs_ready, turned, xT_ready, logits_done = sem("xs_ready"), sem("turned"), sem("xT_ready"), sem("logits_done")
        lg_step, perm_ready, perm_turned, perm_out = sem("lg_step"), sem("perm_ready"), sem("perm_turned"), sem("perm_out")
        hi_ready, rest_ready, mid_ready, lo_ready = sem("hi3"), sem("rest3"), sem("mid3"), sem("lo3")
        gathered, got_act, got_dve = sem("gathered"), sem("got_act"), sem("got_dve")
        hidden_done, hidden_taken, hidden_out = sem("hidden_done"), sem("hidden_taken"), sem("hidden_out")
        zeros_set = sem("zeros_set3")

        def run_batches(eng, body):
            with eng.Fori(0, B - 1) as b:
                body(b, True)
            body(B - 1, False)

        block = ctx.enter_context(nc.Block())

        @block.gpsimd
        def _(pool):
            nc.gpsimd.memset(inner[:], 0.0).then_inc(zeros_set, 1)
            pool.sem_inc(lo_ready, 1)
            with pool.Fori(0, B) as b:
                pool.wait_ge(rest_ready, b + 1)
                nc.gpsimd.tensor_tensor(xp[:, 2], xs[:], xp[:, 1], ALU.subtract).then_inc(lo_ready, 1)

        @block.tensor
        def _(pe):
            def turn_x(b):
                pe.wait_ge(xs_ready, b + 1)
                for ci in range(2):
                    for half in range(2):
                        for t in range(4):
                            mm = pe.transpose(banks[ci * 2 + half][:, t * P:(t + 1) * P],
                                              xs[:, half * 4 + t, ci * P:(ci + 1) * P], ident[:])
                mm.then_inc(turned, 1)

            def logits(b):
                pe.wait_ge(xT_ready, b + 1)
                for half in range(2):
                    for ci in range(2):
                        mm = pe.matmul(banks[4 + half][:], wc[:, ci, :], xT[:, ci, half * 512:(half + 1) * 512],
                                       start=(ci == 0), stop=(ci == 1))
                mm.then_inc(logits_done, 1)

            def turn_perm(b):
                pe.wait_ge(perm_ready, b + 1)
                for t in range(KT):
                    mm = pe.transpose(banks[0][:].bitcast(BF16)[:, t * ES:(t + 1) * ES],
                                      perm_all[:, bass.ds(b * N + t * P, P)], identb[:])
                mm.then_inc(perm_turned, 1)

            def hidden_layer(b, half):
                for q in range(half * 16, half * 16 + 16):
                    for ci in range(2):
                        for j in range(4):
                            mm = pe.matmul(banks[6 + half][j * F:(j + 1) * F, (q % 16) * GB:(q % 16 + 1) * GB],
                                           w1[:, ci, 4 * q + j, :], taken_x[:, ci, 4 * q + j, :],
                                           start=(ci == 0), stop=(ci == 1))
                mm.then_inc(hidden_done, 1)

            turn_x(0)
            logits(0)
            turn_perm(0)

            def body(b, more):
                pe.wait_ge(perm_out, b + 1)
                pe.wait_ge(lo_ready, b + 2)
                for k in range(KT // 2):
                    if k >= 2:
                        pe.wait_ge(got_act, b * (KT // 2) + k - 1)
                        pe.wait_ge(got_dve, b * (KT // 2) + k - 1)
                    elif k == 1:
                        pe.wait_ge(hidden_taken, b * 2 + 2)
                    for t in range(2):
                        for ci in range(2):
                            for part in range(SPLIT):
                                for g in range(4):
                                    mm = pe.matmul(banks[(k % 2) * 4 + g][:, (t * 2 + ci) * ES:(t * 2 + ci + 1) * ES],
                                                   xp[g * GT:(g + 1) * GT, part, 2 * k + t, ci * P:(ci + 1) * P],
                                                   perm[g * GT:(g + 1) * GT, 2 * k + t, :],
                                                   start=(part == 0), stop=(part == SPLIT - 1))
                    mm.then_inc(gathered, 1)
                if more:
                    pe.wait_ge(got_act, b * (KT // 2) + KT // 2 - 1)
                    pe.wait_ge(got_dve, b * (KT // 2) + KT // 2 - 1)
                    turn_x(b + 1)
                pe.wait_ge(got_act, (b + 1) * (KT // 2))
                pe.wait_ge(got_dve, (b + 1) * (KT // 2))
                hidden_layer(b, 0)
                if more:
                    logits(b + 1)
                hidden_layer(b, 1)
                if more:
                    turn_perm(b + 1)

            run_batches(pe, body)

        def gather_out(copy, k, g):
            src = banks[(k % 2) * 4 + g][:].rearrange("p (t c e) -> p t c e", t=2, c=2)
            for ci in range(2):
                ins = copy(taken_x[:, ci].rearrange("p e (t g) -> p t e g", g=4)[:, 2 * k:2 * k + 2, :, g],
                           src[:, :, ci, :])
            return ins

        @block.scalar
        def _(act):
            def route(b):
                act.wait_ge(turned, b + 1)
                for ci in range(2):
                    for half in range(2):
                        ins = nc.scalar.copy(xT[:, ci, half * 512:(half + 1) * 512], banks[ci * 2 + half][:])
                ins.then_inc(xT_ready, 1)
                nc.scalar.copy(xp[:, 0], xs[:]).then_inc(hi_ready, 1)
                act.wait_ge(mid_ready, b + 1)
                nc.scalar.copy(xp[:, 1], xs[:]).then_inc(rest_ready, 1)
                act.wait_ge(perm_turned, b + 1)
                nc.scalar.copy(perm[:].rearrange("p t e -> p (t e)"), banks[0][:].bitcast(BF16)).then_inc(perm_out, 1)

            route(0)

            def body(b, more):
                for k in range(KT // 2):
                    act.wait_ge(gathered, b * (KT // 2) + k + 1)
                    for g in range(2):
                        ins = gather_out(nc.scalar.copy, k, g)
                    ins.then_inc(got_act, 1)
                if more:
                    route(b + 1)

            run_batches(act, body)

        @block.vector
        def _(dve):
            def copy_x(b):
                dve.wait_ge(lo_ready, b + 1)
                nc.vector.tensor_copy(xs[:], x_all[:, bass.ds(b * KT, KT), :]).then_inc(xs_ready, 1)

            def rest(b):
                dve.wait_ge(hi_ready, b + 1)
                nc.vector.tensor_tensor(xs[:], xs[:], xp[:, 0], ALU.subtract).then_inc(mid_ready, 1)

            def choose(b):
                dve.wait_ge(logits_done, b + 1)
                for half in range(2):
                    ins = nc.vector.scalar_tensor_tensor(
                        out=lg[:, half * 512:(half + 1) * 512].rearrange("p (g t) -> p g t", t=GT),
                        in0=banks[4 + half][:].rearrange("p (g t) -> p g t", t=GT), scalar=bc[:, 0:1],
                        in1=tie[:, None, :].to_broadcast([P, GB // 2, GT]), op0=ALU.add, op1=ALU.add)
                ins.then_inc(lg_step, 1)
                dve.wait_ge(lg_step, b * 2 + 1)
                by_group = lg[:].rearrange("p (g t) -> p g t", t=GT)
                nc.vector.tensor_reduce(gmax[:], by_group, AX.X, ALU.max).then_inc(lg_step, 1)
                dve.wait_ge(lg_step, b * 2 + 2)
                nc.vector.tensor_tensor(perm_all[:, bass.ds(b * N, N)].rearrange("p (g t) -> p g t", t=GT), by_group,
                                        gmax[:, :, None].to_broadcast([P, GB, GT]), ALU.is_equal) \
                    .then_inc(perm_ready, 1)

            def bias_and_relu(b, half):
                dve.wait_ge(hidden_done, b * 2 + half + 1)
                nc.vector.tensor_tensor(
                    hidden[:].rearrange("p (q g) -> p q g", g=GB),
                    banks[6 + half][:].rearrange("p (q g) -> p q g", g=GB),
                    b1[:, half * 16:(half + 1) * 16, None].to_broadcast([P, 16, GB]), ALU.add) \
                    .then_inc(hidden_taken, 1)
                dve.wait_ge(hidden_taken, b * 2 + half + 3)
                for j in range(4):
                    ins = nc.vector.tensor_scalar(
                        inner[j * F:(j + 1) * F, half * 16:(half + 1) * 16, j, bass.ds(b * GB, GB)],
                        hidden[j * F:(j + 1) * F, :].rearrange("p (q g) -> p q g", g=GB), 0.0, None, ALU.max)
                ins.then_inc(hidden_out, 1)
                dve.wait_ge(hidden_out, b * 2 + half + 1)

            dve.sem_inc(hidden_taken, 2)
            copy_x(0)
            nc.vector.tensor_copy(identb[:], ident[:])
            rest(0)
            choose(0)
            dve.wait_ge(zeros_set, 1)

            def body(b, more):
                if more:
                    copy_x(b + 1)
                for k in range(KT // 2):
                    dve.wait_ge(gathered, b * (KT // 2) + k + 1)
                    for g in range(2, 4):
                        ins = gather_out(nc.vector.tensor_copy, k, g)
                    ins.then_inc(got_dve, 1)
                if more:
                    rest(b + 1)
                bias_and_relu(b, 0)
                if more:
                    choose(b + 1)
                bias_and_relu(b, 1)

            run_batches(dve, body)


def combine_phase(nc, io, x_all, w1, ident, perm_all, inner, out):
    with ExitStack() as ctx:
        def sb(name, shape, dt=F32):
            return ctx.enter_context(nc.sbuf_tensor(name, shape, dt))

        def sem(name):
            return ctx.enter_context(nc.semaphore(name))

        w2 = w1[:, 0:QUADS * HALF_C].rearrange("p (q d) -> p q d", d=HALF_C)
        permf = w1[:, QUADS * HALF_C:QUADS * HALF_C + B * N]
        FIRST = 4
        b2 = sb("b2", [P, ES])
        res = sb("res", [P, GALL, ES])
        resT = sb("resT", [P, 2, 4, HALF_C])
        LAST = 2
        LT = B * KT // LAST
        stats = sb("stats4", [P, LAST, LT, 6])
        mv = sb("mv4", [P, LAST, LT, 2])
        ln_r, ln_m = sb("ln_r4", [P, LAST, LT]), sb("ln_m4", [P, LAST, LT])
        var, ln_t, ln_h = (sb(n, [P, LT]) for n in ("var4", "ln_t4", "ln_h4"))
        factors, normed_dve = sem("factors4"), sem("normed_dve")
        outer_banks = [ctx.enter_context(nc.psum_tensor(f"E{n}", [P, 512], F32)) for n in range(4)]
        turn_banks = [ctx.enter_context(nc.psum_tensor(f"T{n}", [P, 512], F32)) for n in range(2)]
        sum_banks = [ctx.enter_context(nc.psum_tensor(f"Y{n}", [P, 512], F32)) for n in range(2)]
        w2_first, w2_rest = sem("w2_first"), sem("w2_rest")
        outer_done, out_act, out_dve = sem("outer_done"), sem("out_act"), sem("out_dve")
        rows_turned, rows_act, rows_dve = sem("rows_turned4"), sem("rows_act"), sem("rows_dve")
        summed, added = sem("summed"), sem("added")
        permf_ready, ln_step, normed, stored = sem("permf_ready"), sem("ln_step"), sem("normed"), sem("stored")
        block = ctx.enter_context(nc.Block())
        TILES = B * KT

        @block.sync
        def _(sp):
            with sp.Fori(0, 2) as c:
                sp.wait_ge(out_act, c * (QUADS // 2) + 1)
                sp.wait_ge(out_dve, c * (QUADS // 2) + 1)
                sp.dma_start(w2[:, 0:FIRST], io["W2T"][:, bass.ds(c, 1), 0:FIRST].rearrange("p o q d -> p (o q) d")) \
                    .then_inc(w2_first, 16)
                sp.dma_start(b2[:], io["b2"][:, bass.ds(c, 1)].rearrange("d o e -> d (o e)")).then_inc(w2_first, 16)
                sp.dma_start(w2[:, FIRST:], io["W2T"][:, bass.ds(c, 1), FIRST:].rearrange("p o q d -> p (o q) d")) \
                    .then_inc(w2_rest, 16)
            for k in list(range(CHUNKS - 4)) + [CHUNKS - 2, CHUNKS - 4, CHUNKS - 1, CHUNKS - 3]:
                if k < CHUNKS - 2:
                    sp.wait_ge(normed, k + 1)
                else:
                    sp.wait_ge(normed_dve, k - (CHUNKS - 2) + 1)
                sp.dma_start(out[:, k * CHUNK:(k + 1) * CHUNK], x_all[:, k * CHUNK:(k + 1) * CHUNK]) \
                    .then_inc(stored, 16)
            sp.wait_ge(stored, 16 * CHUNKS)

        @block.tensor
        def _(pe):
            with pe.Fori(0, 2) as c:
                pe.wait_ge(w2_first, c * 32 + 32)
                for q in range(QUADS):
                    if q == FIRST:
                        pe.wait_ge(w2_rest, c * 16 + 16)
                    if q >= 4:
                        pe.wait_ge((out_act, out_dve)[q % 2], c * (QUADS // 2) + q // 2)
                    pe.matmul(outer_banks[q % 4][:], w2[:, q, :], inner[:, q].rearrange("p j g -> p (j g)"),
                              start=True, stop=True).then_inc(outer_done, 1)
                pe.wait_ge(out_act, (c + 1) * (QUADS // 2) + 1)
                pe.wait_ge(out_dve, (c + 1) * (QUADS // 2) + 1)
                pe.wait_ge(permf_ready, 1)

                def combine(k):
                    pe.wait_ge((rows_act, rows_dve)[k % 2], c * (TILES // 2) + k // 2 + 1)
                    y = sum_banks[(k // 4) % 2]
                    if k % 4 == 0 and k >= 8:
                        pe.wait_ge(added, c * (TILES // 4) + k // 4 - 1)
                    for g in range(4):
                        mm = pe.matmul(y[g * GT:(g + 1) * GT, (k % 4) * HALF_C:(k % 4 + 1) * HALF_C],
                                       permf[:, k * P + g * GT:k * P + (g + 1) * GT], resT[:, k % 2, g, :],
                                       start=True, stop=True)
                    if k % 4 == 3:
                        mm.then_inc(summed, 1)

                for k in range(TILES):
                    if k >= 2:
                        pe.wait_ge((rows_act, rows_dve)[k % 2], c * (TILES // 2) + k // 2)
                    for g in range(4):
                        mm = pe.transpose(turn_banks[k % 2][:, g * HALF_C:(g + 1) * HALF_C],
                                          res[:, 4 * k + g, :], ident[:])
                    mm.then_inc(rows_turned, 1)
                    if k >= 1:
                        combine(k - 1)
                combine(TILES - 1)
                pe.wait_ge(added, (c + 1) * (TILES // 4))

        def evacuate_rows(eng, copy, c, k, rows_sem):
            eng.wait_ge(rows_turned, c * TILES + k + 1)
            copy(resT[:, k % 2].rearrange("p g d -> p (g d)"), turn_banks[k % 2][:]).then_inc(rows_sem, 1)

        @block.scalar
        def _(act):
            act.sem_inc(out_act, 1)

            def scaled(t):
                return nc.scalar.activation(x_all[:, t, :], x_all[:, t, :], ACT.Identity,
                                            scale=ln_r[:, t // LT, t % LT:t % LT + 1],
                                            bias=ln_m[:, t // LT, t % LT:t % LT + 1])

            def body(c):
                act.wait_ge(w2_first, c * 32 + 32)
                for q in range(0, QUADS, 2):
                    act.wait_ge(outer_done, c * QUADS + q + 1)
                    for j in range(4):
                        ins = nc.scalar.activation(res[:, :, 4 * q + j], outer_banks[q % 4][:, j * GALL:(j + 1) * GALL],
                                                   ACT.Identity, bias=b2[:, 4 * q + j:4 * q + j + 1])
                    ins.then_inc(out_act, 1)
                done = 0
                for k in range(0, TILES, 2):
                    evacuate_rows(act, nc.scalar.copy, c, k, rows_act)
                    if c == 1 and k >= 22:
                        if done == 0:
                            act.wait_ge(factors, 1)
                        for _ in range(2):
                            ins = scaled(done)
                            done += 1
                        if done % CHUNK == 0:
                            ins.then_inc(normed, 1)
                return done

            body(0)
            done = body(1)
            for t in range(done, TILES - 2 * CHUNK):
                if t == LT:
                    act.wait_ge(factors, 2)
                ins = scaled(t)
                if t % CHUNK == CHUNK - 1:
                    ins.then_inc(normed, 1)

        @block.vector
        def _(dve):
            dve.sem_inc(out_dve, 1)
            nc.vector.tensor_copy(permf, perm_all[:]).then_inc(permf_ready, 1)
            n = [0]

            def link(ins):
                n[0] += 1
                ins.then_inc(ln_step, 1)
                dve.wait_ge(ln_step, n[0])

            def add(c, k4):
                dve.wait_ge(summed, c * (TILES // 4) + k4 + 1)
                x = x_all[:, k4 * 4:k4 * 4 + 4, c * HALF_C:(c + 1) * HALF_C]
                nc.vector.tensor_tensor(x, sum_banks[k4 % 2][:].rearrange("p (t d) -> p t d", d=HALF_C), x,
                                        ALU.add).then_inc(added, 1)

            def statistics(k4):
                dve.wait_ge(added, TILES // 4 + k4 + 1)
                k, t = k4 * 4 // LT, k4 * 4 % LT
                link(norm_statistics(nc, 4, lambda j: x_all[:, k4 * 4 + j, :], stats[:, k, t:t + 4]))

            def all_factors(k):
                norm_factors(nc, link, stats[:, k], mv[:, k], var[:], (ln_r[:, k], ln_t[:], ln_h[:]),
                             ln_m[:, k]).then_inc(factors, 1)

            def body(c):
                dve.wait_ge(w2_first, c * 32 + 32)
                for q in range(1, QUADS, 2):
                    dve.wait_ge(outer_done, c * QUADS + q + 1)
                    nc.vector.tensor_tensor(res[:, :, 4 * q:4 * q + 4].rearrange("p g j -> p j g"),
                                            outer_banks[q % 4][:].rearrange("p (j g) -> p j g", j=4),
                                            b2[:, 4 * q:4 * q + 4, None].to_broadcast([P, 4, GALL]),
                                            ALU.add).then_inc(out_dve, 1)
                for k in range(1, TILES, 2):
                    evacuate_rows(dve, nc.vector.tensor_copy, c, k, rows_dve)
                    if k > 4 and k % 4 == 1:
                        add(c, k // 4 - 1)
                    if k > 4 and k % 4 == 3 and c == 1:
                        statistics(k // 4 - 1)
                        if (k // 4) * 4 == LT:
                            all_factors(0)
                add(c, TILES // 4 - 1)

            body(0)
            body(1)
            statistics(TILES // 4 - 1)
            all_factors(1)
            dve.wait_ge(factors, 2)
            for t in range(TILES - 2 * CHUNK, TILES):
                ins = nc.vector.tensor_scalar(x_all[:, t, :], x_all[:, t, :], ln_r[:, 1, t - LT:t - LT + 1],
                                              ln_m[:, 1, t - LT:t - LT + 1], ALU.mult, ALU.add)
                if t % CHUNK == CHUNK - 1:
                    ins.then_inc(normed_dve, 1)


def program(nc, io, out):
    qk_parts = nc.dram_tensor("qk_parts", [SPLIT, 2, B, C, N], BF16, kind="Internal").ap()
    v_scratch = nc.dram_tensor("v_scratch", [PAIRS, 2, P, H, VW], F32, kind="Internal").ap()
    attn_scratch = nc.dram_tensor("attn_scratch", [GROUPS, KT, P, HG * D], F32, kind="Internal").ap()
    shift_scratch = nc.dram_tensor("shift_scratch", [SHIFT, HG * N], BF16, kind="Internal").ap()
    attention_phases(nc, io, qk_parts, v_scratch, attn_scratch, shift_scratch)
    with nc.sbuf_tensor("x_all", [P, B * KT, C], F32) as x_all:
        with nc.sbuf_tensor("w1", [P, 2 * ES * F], F32) as w1, \
                nc.sbuf_tensor("ident2", [P, P], F32) as ident, \
                nc.sbuf_tensor("wc", [P, 2, ES], F32) as wc, \
                nc.sbuf_tensor("router_rows", [P, QUADS + 1 + GT], F32) as small:
            router = {"wc": wc[:], "b1": small[:, 0:QUADS], "bc": small[:, QUADS:QUADS + 1],
                      "tie": small[:, QUADS + 1:]}
            cross_attention_phase(nc, io, attn_scratch, x_all, w1, ident, router)
            with nc.sbuf_tensor("perm_all", [P, B * N], BF16) as perm_all, \
                    nc.sbuf_tensor("inner", [P, QUADS, 4, GALL], F32) as inner:
                route_phase(nc, io, x_all, w1, ident, router, perm_all, inner)
                combine_phase(nc, io, x_all, w1, ident, perm_all, inner, out)


def kernel(**inputs):
    import numpy as np
    import concourse.bacc as bacc
    from concourse.bass_utils import run_bass_kernel_spmd as run

    a = {k: np.asarray(v) for k, v in inputs.items()}
    half = D // 2
    freqs = (1.0 / 2500 ** (np.arange(half, dtype=np.float32) / half)).astype(np.float32)
    angle = np.outer(np.arange(N, dtype=np.float32), freqs).astype(np.float32)
    angle = np.concatenate([angle, angle], -1)

    def by_tile(t):
        return np.ascontiguousarray(np.tile(t.reshape(KT, P, D).transpose(1, 0, 2), (1, B, 1)))

    sign = np.where(np.arange(D) < half, -1.0, 1.0).astype(np.float32)
    x = a["x"].reshape(B * N, C)
    ctxT = a["ctx_1024"].reshape(B * KC, C).T

    def by_half(w):
        return w.reshape(2, P, -1).transpose(1, 0, 2)

    arrays = {
        "xT": x.T.reshape(2, P, B * N).transpose(1, 0, 2),
        "w_qkv": a["L0_attn_w_qkv"].reshape(2, P, 3 * C).transpose(1, 0, 2),
        "q_scale": a["L0_attn_q_scale"].reshape(1, D),
        "k_scale": a["L0_attn_k_scale"].reshape(1, D),
        "ident": np.eye(P, dtype=np.float32),
        "cos": by_tile(np.cos(angle).astype(np.float32)),
        "sin": by_tile(np.sin(angle).astype(np.float32) * sign),
        "x": x.reshape(B * KT, P, C).transpose(1, 0, 2),
        "w_proj": by_half(a["L0_attn_w_proj"]),
        "WqT": by_half(a["L0_xattn_Wq"].T), "WkT": by_half(a["L0_xattn_Wk"].T),
        "WvT": by_half(a["L0_xattn_Wv"].T), "WoT": by_half(a["L0_xattn_Wo"].T),
        "b_proj": a["L0_attn_b_proj"].reshape(1, C), "bv": a["L0_xattn_bv"].reshape(1, C),
        "bo": a["L0_xattn_bo"].reshape(1, C),
        "bias_cols": np.stack([a["L0_xattn_bq"].reshape(2, P).T, a["L0_xattn_bk"].reshape(2, P).T], 1),
        "head_mask": (np.arange(P)[:, None] // D == np.arange(P // D)[None]).astype(np.float32),
        "half_mask": (np.arange(P)[:, None] // KC == np.arange(2 * D)[None] // D).astype(np.float32),
        "Wc": by_half(a["L0_ffn_Wc"].reshape(C, ES)),
        "bc": a["L0_ffn_bc"].reshape(ES, 1),
        "tie": np.linspace(0.0, 1e-6, GT, dtype=np.float32).reshape(1, GT),
        "W1": a["L0_ffn_W1"].reshape(ES, 2, P, F).transpose(2, 1, 0, 3),
        "b1": a["L0_ffn_b1"].reshape(QUADS, P).T,
        "W2T": a["L0_ffn_W2"].reshape(QUADS, 4, 2, HALF_C, F).transpose(1, 4, 2, 0, 3).reshape(P, 2, QUADS, HALF_C),
        "b2": a["L0_ffn_b2"].reshape(ES, 2, HALF_C).transpose(2, 1, 0),
        "ctxT": by_half(ctxT).reshape(P, 2, B, KC),
        "ctxT2": np.repeat(by_half(ctxT).reshape(P, 2, B, 1, KC), 2, axis=3),
    }
    nc = bacc.Bacc("TRN2", target_bir_lowering=False, num_devices=1)
    feed, handles = {}, {}
    for name, array in arrays.items():
        feed["in_" + name] = np.ascontiguousarray(array)
        handles[name] = nc.dram_tensor("in_" + name, array.shape, F32, kind="ExternalInput").ap()
    out = nc.dram_tensor("out_0", [P, B * KT, C], F32, kind="ExternalOutput").ap()
    program(nc, handles, out)
    r = run(nc, [feed], core_ids=[0])
    return np.ascontiguousarray(r.results[0]["out_0"].transpose(1, 0, 2)).reshape(B, N, C)
```
